# Optimizing a Trainium2 kernel written in Bass

```python
import numpy as np
import jax
import jax.numpy as jnp

def _softmax(x, axis=-1):
    return jax.nn.softmax(x, axis=axis)

def _gelu(x):
    return jax.nn.gelu(x, approximate=True)

def _silu(x):
    return jax.nn.silu(x)

def _sigmoid(x):
    return jax.nn.sigmoid(x)

def _layernorm(x, axis=-1, eps=1e-05):
    m = jnp.mean(x, axis=axis, keepdims=True)
    v = jnp.var(x, axis=axis, keepdims=True)
    return (x - m) / jnp.sqrt(v + eps)

def _scatter_add(tgt, idx, src, axis=0):
    return tgt.at[idx].add(src)

def _segment_sum(src, seg, n):
    return jax.ops.segment_sum(src, seg, n)
kernel_name = 'mk_gnn_resnorm_d4_gnn_r8_b8c20f'

def setup_inputs(seed: int=0):
    np.random.seed(seed)
    _w = jnp.asarray

    def _rec_inputs():
        import jax
        import jax.numpy as jnp
        _gk = jax.random.key(seed)
        x = -0.000202 + 1 * jax.random.normal(jax.random.fold_in(_gk, 1), (6250, 128), jnp.float32)
        _s = jax.random.randint(jax.random.fold_in(_gk, 2), (100000,), 0, 6250, jnp.int32)
        _d = jax.random.randint(jax.random.fold_in(_gk, 3), (100000,), 0, 6250, jnp.int32)
        _loop = jnp.arange(6250, dtype=jnp.int32)
        src = jnp.concatenate([_s, _d, _loop])
        dst = jnp.concatenate([_d, _s, _loop])
        _o = jnp.argsort(dst, stable=True)
        src = src[_o]
        dst = dst[_o]
        edge_attr_64 = 0.000102155 + 1.00015 * jax.random.normal(jax.random.fold_in(_gk, 11), (206250, 64), jnp.float32)
        return (x, src, dst, edge_attr_64)
    x, src, dst, edge_attr_64 = _rec_inputs()

    def _L0_gnn_setup():
        import jax, jax.numpy as jnp
        import numpy as np
        N = 6250
        E = 100000
        IN = 128
        OUT = 128
        H = 4
        C = OUT // H
        NEG_SLOPE = 0.2

        def _segment_softmax(scores, seg, n):
            seg_max = jax.ops.segment_max(scores, seg, num_segments=n)
            ex = jnp.exp(scores - seg_max[seg])
            seg_sum = jax.ops.segment_sum(ex, seg, num_segments=n)
            return ex / (seg_sum[seg] + 1e-16)
        key = jax.random.key(seed)
        ks = jax.random.split(key, 7)
        x = jax.random.normal(ks[0], (N, IN), dtype=jnp.float32)
        edge_index = jax.random.randint(ks[1], (2, E), 0, N, dtype=jnp.int32)
        s_in = 1.0 / np.sqrt(IN)
        W_gat = jax.random.normal(ks[2], (OUT, IN), dtype=jnp.float32) * s_in
        att_src = jax.random.normal(ks[3], (H, C), dtype=jnp.float32) * 0.1
        att_dst = jax.random.normal(ks[4], (H, C), dtype=jnp.float32) * 0.1
        bias = jnp.zeros((OUT,), dtype=jnp.float32)
        W_skip = jax.random.normal(ks[5], (OUT, IN), dtype=jnp.float32) * s_in
        return {'x': x, 'edge_index': edge_index, 'W_gat': W_gat, 'att_src': att_src, 'att_dst': att_dst, 'bias': bias, 'W_skip': W_skip}
    _L0_gnn_all = _L0_gnn_setup()
    _L0_gnn_in = {k: v for k, v in _L0_gnn_all.items() if k in ('W_gat', 'att_src', 'att_dst', 'bias', 'W_skip')}
    del _L0_gnn_all

    def _L1_gnn_setup():
        import jax, jax.numpy as jnp
        import numpy as np
        N_NODES = 12500
        key = jax.random.key(seed)
        ks = jax.random.split(key, 5)
        x = jax.random.normal(ks[0], (N_NODES, 128), dtype=jnp.float32)
        edge_index = jax.random.randint(ks[1], (2, 62500), 0, N_NODES, dtype=jnp.int64)
        W_l = jax.random.normal(ks[2], (128, 128), dtype=jnp.float32) * 0.05
        b_l = jnp.zeros((128,), dtype=jnp.float32)
        W_r = jax.random.normal(ks[3], (128, 128), dtype=jnp.float32) * 0.05
        return {'x': x, 'edge_index': edge_index, 'W_l': W_l, 'b_l': b_l, 'W_r': W_r}
    _L1_gnn_all = _L1_gnn_setup()
    _L1_gnn_in = {k: v for k, v in _L1_gnn_all.items() if k in ('W_l', 'b_l', 'W_r')}
    del _L1_gnn_all

    def _L2_gnn_setup():
        import jax, jax.numpy as jnp
        import numpy as np
        N_NODES = 12500
        N_EDGES = 200000
        D_IN = 128
        D_HID = 32
        key = jax.random.key(seed)
        k1, k2, k3, k4, k5 = jax.random.split(key, 5)
        x = jax.random.normal(k1, (N_NODES, D_IN), dtype=jnp.float32)
        edge_index = jax.random.randint(k2, (2, N_EDGES), 0, N_NODES, dtype=jnp.int64)
        W1 = jax.random.normal(k3, (D_IN, D_HID), dtype=jnp.float32) / np.sqrt(D_IN)
        b1 = jnp.zeros((D_HID,), dtype=jnp.float32)
        W2 = jax.random.normal(k4, (D_HID, D_IN), dtype=jnp.float32) / np.sqrt(D_HID)
        b2 = jnp.zeros((D_IN,), dtype=jnp.float32)
        return {'x': x, 'edge_index': edge_index, 'W1': W1, 'b1': b1, 'W2': W2, 'b2': b2}
    _L2_gnn_all = _L2_gnn_setup()
    _L2_gnn_in = {k: v for k, v in _L2_gnn_all.items() if k in ('W1', 'b1', 'W2', 'b2')}
    del _L2_gnn_all

    def _L3_gnn_setup():
        import jax, jax.numpy as jnp
        import numpy as np
        D_NODE = 128
        D_EDGE = 64
        N_NODES = 12500
        N_EDGES = 62500
        key = jax.random.key(seed)
        ks = jax.random.split(key, 12)

        def lin(k, fan_in, fan_out):
            bound = 1.0 / np.sqrt(fan_in)
            kw, kb = jax.random.split(k)
            W = jax.random.uniform(kw, (fan_in, fan_out), jnp.float32, -bound, bound)
            b = jax.random.uniform(kb, (fan_out,), jnp.float32, -bound, bound)
            return (W, b)
        node_features = jax.random.normal(ks[0], (N_NODES, D_NODE), jnp.float32)
        edge_index = jax.random.randint(ks[1], (2, N_EDGES), 0, N_NODES, jnp.int64 if jax.config.jax_enable_x64 else jnp.int32)
        edge_features = jax.random.normal(ks[2], (N_EDGES, D_EDGE), jnp.float32)
        W1, b1 = lin(ks[3], 2 * D_NODE + D_EDGE, D_NODE)
        W2, b2 = lin(ks[4], D_NODE, D_NODE)
        Wg, bg = lin(ks[5], 2 * D_NODE, D_NODE)
        Wt, bt = lin(ks[6], 2 * D_NODE, D_NODE)
        gamma = jnp.ones((D_NODE,), jnp.float32)
        beta = jnp.zeros((D_NODE,), jnp.float32)
        return {'node_features': node_features, 'edge_features': edge_features, 'W1': W1, 'b1': b1, 'W2': W2, 'b2': b2, 'Wg': Wg, 'bg': bg, 'Wt': Wt, 'bt': bt, 'gamma': gamma, 'beta': beta, 'edge_index': edge_index}
    _L3_gnn_all = _L3_gnn_setup()
    _L3_gnn_in = {k: v for k, v in _L3_gnn_all.items() if k in ('W1', 'b1', 'W2', 'b2', 'Wg', 'bg', 'Wt', 'bt', 'gamma', 'beta')}
    del _L3_gnn_all
    return {'x': x, 'src': src, 'dst': dst, 'edge_attr_64': edge_attr_64, 'L0_gnn_W_gat': _L0_gnn_in['W_gat'], 'L0_gnn_att_src': _L0_gnn_in['att_src'], 'L0_gnn_att_dst': _L0_gnn_in['att_dst'], 'L0_gnn_bias': _L0_gnn_in['bias'], 'L0_gnn_W_skip': _L0_gnn_in['W_skip'], 'L1_gnn_W_l': _L1_gnn_in['W_l'], 'L1_gnn_b_l': _L1_gnn_in['b_l'], 'L1_gnn_W_r': _L1_gnn_in['W_r'], 'L2_gnn_W1': _L2_gnn_in['W1'], 'L2_gnn_b1': _L2_gnn_in['b1'], 'L2_gnn_W2': _L2_gnn_in['W2'], 'L2_gnn_b2': _L2_gnn_in['b2'], 'L3_gnn_W1': _L3_gnn_in['W1'], 'L3_gnn_b1': _L3_gnn_in['b1'], 'L3_gnn_W2': _L3_gnn_in['W2'], 'L3_gnn_b2': _L3_gnn_in['b2'], 'L3_gnn_Wg': _L3_gnn_in['Wg'], 'L3_gnn_bg': _L3_gnn_in['bg'], 'L3_gnn_Wt': _L3_gnn_in['Wt'], 'L3_gnn_bt': _L3_gnn_in['bt'], 'L3_gnn_gamma': _L3_gnn_in['gamma'], 'L3_gnn_beta': _L3_gnn_in['beta']}

def reference(x, src, dst, edge_attr_64, L0_gnn_W_gat, L0_gnn_att_src, L0_gnn_att_dst, L0_gnn_bias, L0_gnn_W_skip, L1_gnn_W_l, L1_gnn_b_l, L1_gnn_W_r, L2_gnn_W1, L2_gnn_b1, L2_gnn_W2, L2_gnn_b2, L3_gnn_W1, L3_gnn_b1, L3_gnn_W2, L3_gnn_b2, L3_gnn_Wg, L3_gnn_bg, L3_gnn_Wt, L3_gnn_bt, L3_gnn_gamma, L3_gnn_beta):
    import jax
    import jax.numpy as jnp

    def _L0_gnn_ref(x, edge_index, W_gat, att_src, att_dst, bias, W_skip):
        import jax, jax.numpy as jnp
        import numpy as np
        N = 6250
        E = 100000
        IN = 128
        OUT = 128
        H = 4
        C = OUT // H
        NEG_SLOPE = 0.2

        def _segment_softmax(scores, seg, n):
            seg_max = jax.ops.segment_max(scores, seg, num_segments=n)
            ex = jnp.exp(scores - seg_max[seg])
            seg_sum = jax.ops.segment_sum(ex, seg, num_segments=n)
            return ex / (seg_sum[seg] + 1e-16)
        loops = jnp.arange(N, dtype=edge_index.dtype)
        src = jnp.concatenate([edge_index[0], loops])
        dst = jnp.concatenate([edge_index[1], loops])
        x_proj = (x @ W_gat.T).reshape(N, H, C)
        a_src = jnp.einsum('nhc,hc->nh', x_proj, att_src)
        a_dst = jnp.einsum('nhc,hc->nh', x_proj, att_dst)
        e = a_src[src] + a_dst[dst]
        e = jnp.where(e > 0, e, NEG_SLOPE * e)
        alpha = _segment_softmax(e, dst, N)
        msgs = alpha[:, :, None] * x_proj[src]
        agg = jax.ops.segment_sum(msgs, dst, num_segments=N)
        out = agg.reshape(N, OUT) + bias
        out = out + x @ W_skip.T
        return jax.nn.elu(out)

    def _L1_gnn_ref(x, edge_index, W_l, b_l, W_r):
        import jax, jax.numpy as jnp
        import numpy as np
        N_NODES = 12500
        src, dst = (edge_index[0], edge_index[1])
        n = x.shape[0]
        msg = x[src]
        summed = jax.ops.segment_sum(msg, dst, num_segments=n)
        deg = jax.ops.segment_sum(jnp.ones_like(dst, dtype=x.dtype), dst, num_segments=n)
        agg = summed / jnp.maximum(deg, 1.0)[:, None]
        h = agg @ W_l.T + b_l + x @ W_r.T
        return jnp.tanh(h)

    def _L2_gnn_ref(x, edge_index, W1, b1, W2, b2):
        import jax, jax.numpy as jnp
        import numpy as np
        N_NODES = 12500
        N_EDGES = 200000
        D_IN = 128
        D_HID = 32
        N = x.shape[0]
        loop = jnp.arange(N, dtype=edge_index.dtype)
        src = jnp.concatenate([edge_index[0], loop])
        dst = jnp.concatenate([edge_index[1], loop])
        deg = jax.ops.segment_sum(jnp.ones_like(dst, dtype=jnp.float32), dst, num_segments=N)
        dinv = jax.lax.rsqrt(deg)
        norm = dinv[src] * dinv[dst]

        def gcn_conv(h, W, b):
            h = h @ W
            msg = h[src] * norm[:, None]
            out = jax.ops.segment_sum(msg, dst, num_segments=N)
            return out + b
        h = gcn_conv(x.astype(jnp.float32), W1, b1)
        h = gcn_conv(h, W2, b2)
        return jax.nn.relu(h)

    def _L3_gnn_ref(node_features, edge_features, W1, b1, W2, b2, Wg, bg, Wt, bt, gamma, beta, edge_index):
        import jax, jax.numpy as jnp
        import numpy as np
        D_NODE = 128
        D_EDGE = 64
        N_NODES = 12500
        N_EDGES = 62500
        num_nodes = node_features.shape[0]
        src, dst = (edge_index[0], edge_index[1])
        h_src = node_features[src]
        h_dst = node_features[dst]
        msg_in = jnp.concatenate([h_src, h_dst, edge_features], axis=-1)
        messages = jax.nn.silu(msg_in @ W1 + b1) @ W2 + b2
        aggregated = jax.ops.segment_sum(messages, dst, num_segments=num_nodes)
        count = jax.ops.segment_sum(jnp.ones((dst.shape[0],), messages.dtype), dst, num_segments=num_nodes)
        aggregated = aggregated / jnp.clip(count, 1.0)[:, None]
        gate_in = jnp.concatenate([node_features, aggregated], axis=-1)
        gate = jax.nn.sigmoid(gate_in @ Wg + bg)
        transform = jnp.tanh(gate_in @ Wt + bt)
        updated = gate * node_features + (1.0 - gate) * transform
        mu = jnp.mean(updated, axis=-1, keepdims=True)
        var = jnp.var(updated, axis=-1, keepdims=True)
        normed = (updated - mu) * jax.lax.rsqrt(var + 1e-05)
        return normed * gamma + beta
    edge_index = jnp.stack([src, dst])
    x = _layernorm(x + _L0_gnn_ref(x, edge_index, L0_gnn_W_gat, L0_gnn_att_src, L0_gnn_att_dst, L0_gnn_bias, L0_gnn_W_skip), axis=-1)
    x = _layernorm(x + _L1_gnn_ref(x, edge_index, L1_gnn_W_l, L1_gnn_b_l, L1_gnn_W_r), axis=-1)
    x = _layernorm(x + _L2_gnn_ref(x, edge_index, L2_gnn_W1, L2_gnn_b1, L2_gnn_W2, L2_gnn_b2), axis=-1)
    x = _layernorm(x + _L3_gnn_ref(x, edge_attr_64, L3_gnn_W1, L3_gnn_b1, L3_gnn_W2, L3_gnn_b2, L3_gnn_Wg, L3_gnn_bg, L3_gnn_Wt, L3_gnn_bt, L3_gnn_gamma, L3_gnn_beta, edge_index), axis=-1)
    return x

_drawn_inputs = setup_inputs


def setup_inputs(seed=0):
    import zlib

    import numpy as np

    out = dict(_drawn_inputs(seed))
    spreads = {'L0_gnn_bias': (0.0, 0.1),
     'L1_gnn_b_l': (0.0, 0.1),
     'L2_gnn_b1': (0.0, 0.1),
     'L2_gnn_b2': (0.0, 0.1),
     'L3_gnn_gamma': (1.0, 0.2),
     'L3_gnn_beta': (0.0, 0.1)}
    factors = {'edge_attr_64': 8.0,
     'L3_gnn_b1': 27.427,
     'L3_gnn_b2': 5.12,
     'L3_gnn_bg': 6.243,
     'L3_gnn_bt': 4.142}
    for name, (base, spread) in spreads.items():
        noise = np.random.default_rng([zlib.crc32(name.encode()), seed]).standard_normal(out[name].shape)
        drawn = base * np.exp(spread * noise) if base else spread * noise
        out[name] = jnp.asarray(drawn.astype(out[name].dtype))
    for name, factor in factors.items():
        out[name] = (out[name] * factor).astype(out[name].dtype)
    return out
```

```python
from contextlib import ExitStack

import concourse.bass as bass
from concourse import mybir

ALU = mybir.AluOpType
ACT = mybir.ActivationFunctionType
AX = mybir.AxisListType
F32 = mybir.dt.float32
BF16 = mybir.dt.bfloat16
I32 = mybir.dt.int32

P = 128
EPS = 1e-5
BIG = float(2.0 ** 100)
SLOPE = 0.2
NO_NODE = 20000
UNROLL = 32
RING = 16
QUARTER = 8
LIN = 7
XW = 132
AW = 133


def gnn(nc, A, out):
    N, DF = A["x"].shape
    E = A["src"].shape[0]
    DE = A["edge_attr_64"].shape[1]
    H, C = A["att_src"].shape
    HID = A["L2_W1"].shape[1]
    G = -(-N // P)
    T = -(-E // P)
    FULL = N // P
    TAIL = N - FULL * P
    STEPS = -(-(T + G - 1) // UNROLL) * UNROLL
    BODIES = STEPS // UNROLL
    CH = STEPS // P
    TP = STEPS - (G - 1)
    LAST = E - P
    OVER = T * P - E
    NB = G - 1
    assert DF == P and G % LIN == 0 and STEPS % P == 0 and TP >= T and OVER > 0

    def dram(name, shape, dt):
        return nc.dram_tensor(name, shape, dt).ap()

    dst_pad = dram("dst_pad", [TP, P], I32)
    src_pad = dram("src_pad", [TP, P], I32)
    src_steps = dram("src_steps", [P, STEPS], I32)
    group_steps = dram("group_steps", [1, STEPS], I32)
    base_steps = dram("base_steps", [1, STEPS], I32)
    tab_proj = dram("tab_proj", [G * P, XW], F32)
    tab_x = dram("tab_x", [G * P, P], F32)
    tab_y1 = dram("tab_y1", [G * P, HID], F32)
    tab_y2 = dram("tab_y2", [G * P, HID], F32)
    tab_ps = dram("tab_ps", [G * P, P], F32)

    with ExitStack() as ctx:
        def sb(name, shape, dt=F32):
            return ctx.enter_context(nc.sbuf_tensor(name, shape, dt))

        def sem(name):
            return ctx.enter_context(nc.semaphore(name))

        X = sb("X", [P, G, P])
        ACC = sb("ACC", [P, G, AW])
        TA = sb("TA", [P, G, XW])
        TB = sb("TB", [P, G, P])
        TC = sb("TC", [P, G, P])
        node_ad = sb("node_ad", [P, G, 2 * H])
        node_as = sb("node_as", [P, G, H])
        node_max = sb("node_max", [P, G, H])
        stat = sb("stat", [P, 4, G])
        count = sb("count", [P, G])
        rcount = sb("rcount", [P, G])
        dinv = sb("dinv", [P, G])
        dloc = sb("dloc", [P, STEPS])
        srcs = sb("srcs", [P, STEPS], I32)
        gtab = sb("gtab", [1, QUARTER + STEPS + UNROLL], I32)
        btab = sb("btab", [1, STEPS], I32)
        iota_i = sb("iota_i", [P, P], I32)
        iota = sb("iota", [P, P])
        ident = sb("ident", [P, P])
        nident = sb("nident", [P, H, P], BF16)
        ones = sb("ones", [P, P])
        wts = sb("wts", [P, 14, P])
        rows = sb("rows", [P, 12, P])
        fill = sb("fill", [8, 2, P], I32)
        bound = sb("bound", [P, 3, NB])
        bound_i = sb("bound_i", [P, 2, NB], I32)
        sidx_i = sb("sidx_i", [P, CH], I32)
        sidx = sb("sidx", [P, 5, CH])
        tile_i = sb("tile_i", [P, 3, CH], I32)
        tile_rows = sb("tile_rows", [P, 2, 2, P], I32)
        tile_f = sb("tile_f", [P, 2, 2, P])
        idx = sb("idx", [P, UNROLL], I32)
        got = sb("got", [P, RING, XW])
        D = sb("D", [P, 8, P])
        ND = sb("ND", [P, 4, P], BF16)
        DT = sb("DT", [P, 2, P])
        diag = sb("diag", [P, 2, H, P])
        m4 = sb("m4", [P, 2, H])
        z4 = sb("z4", [P, 4, 3, H])
        p4 = sb("p4", [P, 4, H])
        msg = sb("msg", [P, 3, AW])
        ef = sb("ef", [P, 8, DE])
        efT = sb("efT", [DE, 2, P])
        pre = sb("pre", [P, 2, P])
        silu_out = sb("silu_out", [P, 2, P])
        tc = TC[:].rearrange("p g c -> p (g c)")
        Y = tc[:, 0:G * HID].rearrange("p (g c) -> p g c", g=G)
        s0 = tc[:, 0:G * H].rearrange("p (g h) -> p g h", g=G)
        p_self = tc[:, G * H:2 * G * H].rearrange("p (g h) -> p g h", g=G)
        flat = got[:].rearrange("p r w -> p (r w)")
        stage = flat[:, 0:LIN * P].rearrange("p (j c) -> p j c", j=LIN)
        xT = flat[:, LIN * P:2 * LIN * P].rearrange("p (j c) -> p j c", j=LIN)

        PS = ctx.enter_context(nc.psum_tensor("PS", [P, 8, 512], F32))
        ps_flat = PS[:].rearrange("p b c -> p (b c)")
        lin_in = ps_flat[:, 0:LIN * P].rearrange("p (j c) -> p j c", j=LIN)
        lin_o = ps_flat[:, 1024:1024 + LIN * 2 * P].rearrange("p (j c) -> p j c", j=LIN)

        s_in = sem("inputs_landed")
        s_x = sem("x_landed")
        s_xpad = sem("x_pad_zeroed")
        s_fill = sem("fill_ready")
        s_pad1 = sem("pad_rows_written")
        s_pad = sem("pad_lists_written")
        s_dst = sem("dst_landed")
        s_iota = sem("iotas_ready")
        s_cnt = sem("bound_counts_ready")
        s_bnd = sem("bounds_summed")
        s_tix = sem("tile_indices_ready")
        s_trow = [sem(f"tile_rows_landed{i}") for i in range(4)]
        s_tf = sem("tile_rows_converted")
        s_tt = sem("tile_rows_transposed")
        s_tc = sem("step_columns_stored")
        s_steps = sem("step_tables_written")
        s_gtab = sem("step_registers_landed")
        s_chain = sem("dve_chain")
        s_pool = sem("pool_chain")
        s_slot = sem("gather_slot_free")
        s_linr = sem("linear_input_ready")
        s_linw = sem("linear_staged")
        s_linT = sem("linear_transposed")
        s_linX = sem("linear_xT_ready")
        s_linY = sem("linear_product_ready")
        s_linO = sem("linear_stored")
        s_areq = sem("act_request")
        s_arep = sem("act_reply")
        s_tabr = sem("table_ready")
        s_tabw = sem("table_written")
        s_idx = [sem(f"indices_landed{i}") for i in range(UNROLL // QUARTER)]
        s_got = [sem(f"gathered{i}") for i in range(RING)]
        s_d = sem("onehot_ready")
        s_d2 = sem("not_onehot_ready")
        s_diag = sem("diag_ready")
        s_max = sem("masked_scores_ready")
        s_red = sem("tile_max_ready")
        s_dT = sem("onehot_transposed")
        s_dTc = sem("onehotT_stored")
        s_ex = sem("expanded")
        s_z = sem("logit_step")
        s_p = sem("weights_ready")
        s_msg = sem("messages_ready")
        s_seg = sem("segment_sums_ready")
        s_done = sem("step_done")
        s_ef = [sem(f"edge_features_landed{i}") for i in range(8)]
        s_fT = sem("edge_features_transposed")
        s_fTc = sem("edge_featuresT_stored")
        s_pre = sem("preactivation_ready")
        s_silu = sem("silu_ready")
        s_out = sem("output_written")
        block = ctx.enter_context(nc.Block())

        NW = 14 + 12
        x_in = A["x"]

        def free(ap, w):
            return ap.unsqueeze(2).to_broadcast([P, ap.shape[1], w])

        def across(ap, n):
            return ap.unsqueeze(1).to_broadcast([P, n, ap.shape[1]])

        @block.sync
        def _(sp):
            sp.wait_ge(s_xpad, 1)
            sp.dma_start(X[:, 0:FULL, :], x_in[0:FULL * P].rearrange("(g p) f -> p g f", p=P)).then_inc(s_x, 16)
            sp.dma_start(X[0:TAIL, FULL:G, :], x_in[FULL * P:N].unsqueeze(1)).then_inc(s_x, 16)
            for n, w in enumerate(("gatT", "skipT", "WlT", "WrT")):
                sp.dma_start(wts[:, n, :], A[w]).then_inc(s_in, 16)
            sp.dma_start(wts[:, 4, 0:HID], A["L2_W1"]).then_inc(s_in, 16)
            sp.dma_start(wts[0:HID, 5, :], A["L2_W2"]).then_inc(s_in, 16)
            sp.dma_start(wts[:, 6, :], A["L3_W1"][0:P]).then_inc(s_in, 16)
            sp.dma_start(wts[:, 7, :], A["L3_W1"][P:2 * P]).then_inc(s_in, 16)
            sp.dma_start(wts[:, 8, :], A["L3_W2"]).then_inc(s_in, 16)
            sp.dma_start(wts[:, 9, :], A["L3_Wg"][0:P]).then_inc(s_in, 16)
            sp.dma_start(wts[:, 10, :], A["L3_Wt"][0:P]).then_inc(s_in, 16)
            sp.dma_start(wts[:, 11, :], A["L3_Wg"][P:2 * P]).then_inc(s_in, 16)
            sp.dma_start(wts[:, 12, :], A["L3_Wt"][P:2 * P]).then_inc(s_in, 16)
            sp.dma_start(wts[0:DE, 13, :], A["L3_W1"][2 * P:2 * P + DE]).then_inc(s_in, 16)
            for n, b in enumerate(("L0_bias", "att_src", "att_dst", "L1_b", "L2_b1", "L2_b2", "L3_b1", "L3_b2",
                                   "L3_bg", "L3_bt", "gamma", "beta")):
                row = A[b].rearrange("h c -> (h c)") if len(A[b].shape) == 2 else A[b]
                sp.dma_start(rows[:, n, 0:row.shape[0]], row.partition_broadcast(P)).then_inc(s_in, 16)

            sp.wait_ge(s_fill, 2)
            for pad, lst, f in ((dst_pad, A["dst"], 0), (src_pad, A["src"], 1)):
                flat = pad.rearrange("t p -> (t p)")
                body = (T - 1) * P
                sp.dma_start(flat[0:body].rearrange("(a b) -> a b", b=P), lst[0:body].rearrange("(a b) -> a b", b=P)).then_inc(s_pad, 16)
                sp.dma_start(pad[T - 1:TP, :], fill[0:TP - T + 1, f, :]).then_inc(s_pad1, 16)
            sp.wait_ge(s_pad1, 32)
            for pad, lst in ((dst_pad, A["dst"]), (src_pad, A["src"])):
                sp.dma_start(pad[T - 1:T, OVER:P], lst[(T - 1) * P:E].unsqueeze(0)).then_inc(s_pad, 16)
            sp.wait_ge(s_pad, 64)
            sp.dma_start(srcs[:, 0:T], dst_pad[0:T].rearrange("t p -> (t p)").rearrange("(q c) -> q c", q=P)).then_inc(s_dst, 16)

            sp.wait_ge(s_tix, 3)
            with nc.allow_non_contiguous_dma(reason="one small table"):
                sp.dma_start(group_steps.rearrange("a (c p) -> p (a c)", p=P), tile_i[:, 0, :]).then_inc(s_steps, 16)
                sp.dma_start(base_steps.rearrange("a (c p) -> p (a c)", p=P), tile_i[:, 2, :]).then_inc(s_steps, 16)
            sp.wait_ge(s_steps, 32)
            sp.dma_start(gtab[:, QUARTER:QUARTER + STEPS], group_steps).then_inc(s_gtab, 16)
            sp.dma_start(btab[:, :], base_steps).then_inc(s_gtab, 16)
            sp.wait_ge(s_tc, 2 * CH)
            sp.dma_start(src_steps, srcs[:, :]).then_inc(s_steps, 16)
            sp.wait_ge(s_steps, 48)
            sp.wait_ge(s_gtab, 32)

            tables = ((tab_proj, TA[:, :, :]), None, (tab_x, X[:, :, :]), (tab_y1, Y), (tab_y2, Y),
                      (tab_ps, TA[:, :, 0:P]))
            written = 0
            base_regs = [sp.alloc_register(f"base{k}") for k in range(16)]
            for q in range(6):
                if tables[q] is not None:
                    written += 1
                    sp.wait_ge(s_tabr, written)
                    sp.dma_start(tables[q][0].rearrange("(g p) f -> p g f", p=P), tables[q][1]).then_inc(s_tabw, 16)
                for r in range(UNROLL // QUARTER):
                    if q:
                        sp.wait_ge(s_done, q * STEPS)
                    sp.dma_start(idx[:, r * QUARTER:(r + 1) * QUARTER], src_steps[:, r * QUARTER:(r + 1) * QUARTER]).then_inc(s_idx[r], 16)

                def refresh(i, r):
                    sp.wait_ge(s_done, i * UNROLL + (r + 1) * QUARTER)
                    at = (i - q * BODIES + 1) * UNROLL + r * QUARTER
                    sp.dma_start(idx[:, r * QUARTER:(r + 1) * QUARTER], src_steps[:, bass.ds(at, QUARTER)]).then_inc(s_idx[r], 16)

                def features(i, half, first):
                    sp.load(base_regs, btab[0:1, bass.ds((i - q * BODIES) * UNROLL + 16 * half, 16)])
                    for k in range(16 * half, 16 * half + 16):
                        base = sp.snap(base_regs[k % 16], min_val=0, max_val=LAST)
                        if not (first and k < 8):
                            sp.wait_ge(s_done, i * UNROLL + k - 7)
                        sp.dma_start(ef[:, k % 8, :], A["edge_attr_64"][bass.ds(base, P), :]).then_inc(s_ef[k % 8], 16)
                        if k % 8 == 7 and not (first and k == 7) :
                            yield k // 8 - 1

                if q < 5:
                    with sp.Fori(q * BODIES, (q + 1) * BODIES - 1) as i:
                        for r in range(UNROLL // QUARTER):
                            refresh(i, r)
                else:
                    def body(i, first):
                        for half in range(2):
                            for r in features(i, half, first):
                                if r >= 0:
                                    refresh(i, r)
                                else:
                                    refresh(i - 1, UNROLL // QUARTER - 1)
                    body(q * BODIES, True)
                    with sp.Fori(q * BODIES + 1, (q + 1) * BODIES - 1) as i:
                        body(i, False)
                    last = (q + 1) * BODIES - 1
                    for half in range(2):
                        for r in features(last, half, False):
                            if r < 0:
                                refresh(last - 1, UNROLL // QUARTER - 1)
            sp.wait_ge(s_tabr, written + 1)
            sp.dma_start(out[0:FULL * P].rearrange("(g p) f -> p g f", p=P), X[:, 0:FULL, :]).then_inc(s_out, 16)
            sp.dma_start(out[FULL * P:N].unsqueeze(1), X[0:TAIL, FULL:G, :]).then_inc(s_out, 16)
            sp.wait_ge(s_out, 32)

        @block.gpsimd
        def _(pool):
            nc.gpsimd.memset(fill[:, 0, :], NO_NODE).then_inc(s_fill, 1)
            nc.gpsimd.memset(fill[:, 1, :], 0).then_inc(s_fill, 1)
            nc.gpsimd.memset(ident[:], 0.0).then_inc(s_pool, 1)
            nc.gpsimd.iota(iota_i[:], [[1, P]], base=0, channel_multiplier=0).then_inc(s_iota, 1)
            nc.gpsimd.iota(sidx_i[:], [[P, CH]], base=0, channel_multiplier=1).then_inc(s_iota, 1)
            nc.gpsimd.iota(bound_i[:, 1, :], [[1, NB]], base=1, channel_multiplier=0).then_inc(s_iota, 1)
            pool.wait_ge(s_pool, 1)
            nc.gpsimd.affine_select(out=ident[:], in_=ident[:], compare_op=ALU.not_equal, fill=1.0, base=0,
                                    pattern=[[-1, P]], channel_multiplier=1).then_inc(s_iota, 1)
            pool.wait_ge(s_pad, 64)
            pool.wait_ge(s_tix, 3)
            for c in range(CH):
                for f, pad in enumerate((dst_pad, src_pad)):
                    if c >= 2:
                        pool.wait_ge(s_tf, 2 * (c - 2) + f + 1)
                    nc.gpsimd.indirect_dma_start(
                        out=tile_rows[:, c % 2, f, :], out_offset=None, in_=pad,
                        in_offset=bass.IndirectOffsetOnAxis(ap=tile_i[:, 1, c:c + 1], axis=0)).then_inc(s_trow[2 * (c % 2) + f], 16)
            written = 0
            for q, (tab, w) in enumerate(((tab_proj, XW), (tab_proj, XW), (tab_x, P), (tab_y1, HID), (tab_y2, HID), (tab_ps, P))):
                written += q != 1
                pool.wait_ge(s_tabw, 16 * written)

                def body(i, first):
                    for k in range(UNROLL):
                        r = k // QUARTER
                        if k % QUARTER == 0:
                            pool.wait_ge(s_idx[r], i * 16 + 16)
                        if not (first and q == 0 and k < RING):
                            pool.wait_ge(s_done, i * UNROLL + k - RING + 1)
                        pool.sem_inc(s_slot, 1)
                        dest = got[:, k % RING, 0:w]
                        nc.gpsimd.indirect_dma_start(
                            out=dest, out_offset=None, in_=tab,
                            in_offset=bass.IndirectOffsetOnAxis(ap=idx[:, k:k + 1], axis=0)).then_inc(s_got[k % RING], 16)

                body(q * BODIES, True)
                with pool.Fori(q * BODIES + 1, (q + 1) * BODIES) as i:
                    body(i, False)

        def landed(eng, i, k):
            eng.wait_ge(s_got[k % RING], i * (16 * UNROLL // RING) + 16 * (k // RING + 1))

        def run_pass(eng, q, stages, loads=None):
            first = q * BODIES

            def body(i, peeled):
                for k in range(UNROLL):
                    if k % 16 == 0 and loads:
                        loads(i, k // 16)
                    for lag, fn in stages:
                        if k >= lag:
                            fn(i, k - lag)
                        elif not peeled:
                            fn(i - 1, k - lag + UNROLL)

            body(first, True)
            with eng.Fori(first + 1, first + BODIES) as i:
                body(i, False)
            last = first + BODIES - 1
            if loads:
                loads(last + 1, 0)
            for k in range(max(lag for lag, _ in stages)):
                for lag, fn in stages:
                    if k < lag:
                        fn(last, k - lag + UNROLL)

        def group_loader(eng, q, lag, name):
            regs = [eng.alloc_register(f"{name}{k}") for k in range(16)]

            def loads(i, half):
                eng.load(regs, gtab[0:1, bass.ds((i - q * BODIES) * UNROLL + 16 * half + QUARTER - lag, 16)])

            def group(k):
                return eng.snap(regs[(k + lag) % 16], min_val=0, max_val=G - 1)

            return loads, group, regs

        LINEARS = (
            (X, 0, 2 * P, ((TA, "copy"), (TB, "copy"))),
            (TC, 2, P, ((TA, "copy"),)),
            (X, 3, P, ((TA, "add"),)),
            (X, 4, HID, ((TA, "copy"),)),
            (TC, 5, P, ((TA, "copy"),)),
            (X, 6, 2 * P, ((TA, "copy"), (TB, "copy"))),
            (TC, 8, P, ((TA, "copy"),)),
            (X, 9, 2 * P, ((TB, "copy"), (TC, "copy"))),
            (TA, 11, 2 * P, ((TB, "add"), (TC, "add"))),
        )
        NL = G // LIN

        @block.tensor
        def _(pe):
            pe.sem_inc(s_linT, 1)
            pe.sem_inc(s_linY, 1)
            pe.wait_ge(s_cnt, 1)
            nc.tensor.matmul(PS[:, 0, 0:NB], ones[:], bound[:, 0, :], start=True, stop=True).then_inc(s_bnd, 1)
            pe.wait_ge(s_iota, 4)
            for n in range(2 * CH):
                pe.wait_ge(s_tf, n + 1)
                if n >= 2:
                    pe.wait_ge(s_tc, n - 1)
                nc.tensor.transpose(PS[:, 2 + n % 2, 0:P], tile_f[:, (n // 2) % 2, n % 2, :], ident[:]).then_inc(s_tt, 1)
            pe.wait_ge(s_in, 16 * NW)

            def linear(L):
                _, w, cols, _ = LINEARS[L]
                with pe.Fori(L * NL, (L + 1) * NL) as i:
                    pe.wait_ge(s_linw, i + 1)
                    pe.wait_ge(s_linX, i + 1)
                    for j in range(LIN):
                        mm = nc.tensor.transpose(lin_in[:, j, :], stage[:, j, :], ident[:])
                    mm.then_inc(s_linT, 1)
                    pe.wait_ge(s_linX, i + 2)
                    pe.wait_ge(s_linO, 2 * i + 2)
                    rhs = wts[:, w:w + 2, :].rearrange("p a b -> p (a b)")[:, 0:cols]
                    for j in range(LIN):
                        mm = nc.tensor.matmul(lin_o[:, j, 0:cols], xT[:, j, :], rhs, start=True, stop=True)
                    mm.then_inc(s_linY, 1)

            def segment_sum(q, rhs, ready):
                w = {1: AW, 2: P, 3: HID, 4: HID, 5: P}[q]

                def fn(i, k):
                    g = i * UNROLL + k
                    ready(i, k)
                    if not (q == 1 and isinstance(i, int) and i == BODIES and k < 2):
                        pe.wait_ge(s_done, g - 1)
                    nc.tensor.matmul(PS[:, 6 + k % 2, 0:w], D[:, k % 8, :], rhs(k), start=True, stop=True).then_inc(s_seg, 1)
                return fn

            def transpose_onehot(q, n):
                def fn(i, k):
                    pe.wait_ge(s_d, i * UNROLL + k + 1)
                    if not (n == 0 and isinstance(i, int) and k < 2):
                        pe.wait_ge(s_dTc, (i - q * BODIES + n * BODIES) * UNROLL + k - 1)
                    nc.tensor.transpose(PS[:, k % 2, 0:P], D[:, k % 8, :], ident[:]).then_inc(s_dT, 1)
                return fn

            linear(0)

            def masked_scores(i, k):
                g = i * UNROLL + k
                pe.wait_ge(s_d, g + 1)
                pe.wait_ge(s_d2, g + 1)
                pe.wait_ge(s_diag, g + 1)
                if not (isinstance(i, int) and k < 2):
                    pe.wait_ge(s_red, g - 1)
                o = PS[:, 4 + k % 2, :]
                nc.tensor.matmul(o, D[:, k % 8, :], diag[:, k % 2].rearrange("p h e -> p (h e)"), start=True, stop=False)
                nc.tensor.matmul(o, ND[:, k % 4, :], nident[:].rearrange("p h e -> p (h e)"), start=False, stop=True).then_inc(s_max, 1)
            run_pass(pe, 0, ((0, masked_scores),))

            pe.wait_ge(s_gtab, 32)
            loads, group, regs = group_loader(pe, 1, 1, "peg")

            def expand_scores(i, k):
                g = (i - BODIES) * UNROLL + k
                pe.wait_ge(s_dTc, g + 1)
                if not (isinstance(i, int) and i == BODIES and k < 2):
                    pe.wait_ge(s_z, 3 * (g - 1))
                nc.tensor.matmul(PS[:, 4 + k % 2, 0:2 * H], DT[:, k % 2, :], node_ad[:, bass.ds(group(k), 1), :].rearrange("p a c -> p (a c)"),
                                 start=True, stop=True).then_inc(s_ex, 1)

            def attention_ready(i, k):
                pe.wait_ge(s_msg, 2 * ((i - BODIES) * UNROLL + k) + 2)
            run_pass(pe, 1, ((0, transpose_onehot(1, 0)), (1, expand_scores),
                             (5, segment_sum(1, lambda k: msg[:, k % 2, :], attention_ready))), loads)

            def gathered_ready(i, k):
                pe.wait_ge(s_d, i * UNROLL + k + 1)
                landed(pe, i, k)

            linear_after = {2: (1, 2, 3), 3: (), 4: (4, 5)}
            for q, w in ((2, P), (3, HID), (4, HID)):
                run_pass(pe, q, ((0, segment_sum(q, lambda k, w=w: got[:, k % RING, 0:w], gathered_ready)),))
                for L in linear_after[q]:
                    linear(L)

            for r in regs:
                pe.free_register(r)
            loads5, group5, _ = group_loader(pe, 5, 1, "pem")

            def transpose_both(i, k):
                g = (i - 5 * BODIES) * UNROLL + k
                pe.wait_ge(s_ef[k % 8], (i - 5 * BODIES) * (16 * UNROLL // 8) + 16 * (k // 8 + 1))
                if not (isinstance(i, int) and k < 2):
                    pe.wait_ge(s_fTc, g - 1)
                transpose_onehot(5, 1)(i, k)
                nc.tensor.transpose(PS[0:DE, 2 + k % 2, 0:P], ef[:, k % 8, :], ident[:]).then_inc(s_fT, 1)

            def edge_linear(i, k):
                g = (i - 5 * BODIES) * UNROLL + k
                pe.wait_ge(s_dTc, g + STEPS + 1)
                pe.wait_ge(s_fTc, g + 1)
                if not (isinstance(i, int) and k < 2):
                    pe.wait_ge(s_pre, g - 1)
                o = PS[:, 4 + k % 2, 0:P]
                nc.tensor.matmul(o, DT[:, k % 2, :], TB[:, bass.ds(group5(k), 1), :].rearrange("p a c -> p (a c)"), start=True, stop=False)
                nc.tensor.matmul(o, efT[:, k % 2, :], wts[0:DE, 13, :], start=False, stop=True).then_inc(s_ex, 1)

            def silu_ready(i, k):
                pe.wait_ge(s_silu, (i - 5 * BODIES) * UNROLL + k + 1)
            run_pass(pe, 5, ((0, transpose_both), (1, edge_linear),
                             (3, segment_sum(5, lambda k: silu_out[:, k % 2, :], silu_ready))), loads5)
            for L in (6, 7, 8):
                linear(L)

        @block.scalar
        def _(act):
            act.sem_inc(s_linX, 1)
            requests = [0]

            def serve(out_, in_, func, scale=1.0):
                requests[0] += 1
                act.wait_ge(s_areq, requests[0])
                nc.scalar.activation(out_, in_, func, scale=scale).then_inc(s_arep, 1)

            def linear(L):
                tab = LINEARS[L][0]
                act.wait_ge(s_linr, L + 1)
                with act.Fori(L * NL, (L + 1) * NL) as i:
                    act.wait_ge(s_linT, i + 1)
                    nc.scalar.copy(stage, tab[:, bass.ds((i - L * NL) * LIN, LIN), 0:P]).then_inc(s_linw, 1)
                    act.wait_ge(s_linT, i + 2)
                    act.wait_ge(s_linY, i + 1)
                    nc.scalar.copy(xT, lin_in).then_inc(s_linX, 1)

            def norm():
                serve(stat[:, 2, :], stat[:, 1, :], ACT.Sqrt)

            def store_onehotT(q, n):
                def fn(i, k):
                    g = (i - q * BODIES + n * BODIES) * UNROLL + k
                    act.wait_ge(s_dT, g + 1)
                    if not (n == 0 and isinstance(i, int) and k < 2):
                        act.wait_ge(s_ex, g - 1)
                    nc.scalar.copy(DT[:, k % 2, :], PS[:, k % 2, 0:P]).then_inc(s_dTc, 1)
                return fn

            linear(0)

            def diagonals(i, k):
                g = i * UNROLL + k
                landed(act, i, k)
                if not (isinstance(i, int) and k < 2):
                    act.wait_ge(s_max, g - 1)
                for h in range(H):
                    ins = nc.scalar.activation(diag[:, k % 2, h, :], ident[:], ACT.Copy, scale=got[:, k % RING, P + h:P + h + 1])
                ins.then_inc(s_diag, 1)
            act.wait_ge(s_iota, 4)
            run_pass(act, 0, ((0, diagonals),))
            serve(p_self, p_self, ACT.Exp)

            def weights(i, k):
                g = (i - BODIES) * UNROLL + k
                act.wait_ge(s_z, 3 * g + 3)
                if not (isinstance(i, int) and i == BODIES and k < 4):
                    act.wait_ge(s_msg, 2 * (g - 3))
                nc.scalar.activation(p4[:, k % 4, :], z4[:, k % 4, 2, :], ACT.Exp).then_inc(s_p, 1)
            run_pass(act, 1, ((0, store_onehotT(1, 0)), (3, weights)))
            serve(TC[:], TC[:], ACT.Exp)
            norm()
            serve(dinv[:], dinv[:], ACT.Sqrt)
            linear(1)
            linear(2)
            serve(TA[:, :, 0:P], TA[:, :, 0:P], ACT.Tanh)
            norm()
            linear(3)
            linear(4)
            norm()
            linear(5)

            def store_featuresT(i, k):
                g = (i - 5 * BODIES) * UNROLL + k
                act.wait_ge(s_fT, g + 1)
                act.wait_ge(s_ex, STEPS + g - 1)
                nc.scalar.copy(efT[:, k % 2, :], PS[0:DE, 2 + k % 2, 0:P]).then_inc(s_fTc, 1)

            def silu(i, k):
                g = (i - 5 * BODIES) * UNROLL + k
                act.wait_ge(s_pre, g + 1)
                act.wait_ge(s_seg, 4 * STEPS + g - 1)
                nc.scalar.activation(silu_out[:, k % 2, :], pre[:, k % 2, :], ACT.Silu).then_inc(s_silu, 1)
            run_pass(act, 5, ((0, store_onehotT(5, 1)), (0, store_featuresT), (2, silu)))
            for L in (6, 7, 8):
                linear(L)
            serve(TB[:], TB[:], ACT.Sigmoid)
            serve(TC[:], TC[:], ACT.Tanh)
            norm()
            norm()

        @block.vector
        def _(dve):
            v = nc.vector
            chain = [0]
            asked = [0]
            dve.sem_inc(s_linO, 2)
            linears = [0]

            def link(ins):
                chain[0] += 1
                ins.then_inc(s_chain, 1)
                dve.wait_ge(s_chain, chain[0])

            def ask():
                asked[0] += 1
                dve.sem_inc(s_areq, 1)
                dve.wait_ge(s_arep, asked[0])

            def linear():
                L = linears[0]
                linears[0] += 1
                outs = LINEARS[L][3]
                cols = min(LINEARS[L][2], P)
                dve.sem_inc(s_linr, 1)
                with dve.Fori(L * NL, (L + 1) * NL) as i:
                    dve.wait_ge(s_linY, i + 2)
                    for n, (tab, mode) in enumerate(outs):
                        o = tab[:, bass.ds((i - L * NL) * LIN, LIN), 0:cols]
                        y = lin_o[:, :, n * P:n * P + cols]
                        ins = v.tensor_tensor(o, o, y, ALU.add) if mode == "add" else v.tensor_copy(o, y)
                        ins.then_inc(s_linO, 2 // len(outs))
                dve.wait_ge(s_linO, 2 * (L + 1) * NL + 2)

            def layernorm(Z, scratch):
                link(v.tensor_reduce(stat[:, 0, :], Z, AX.X, ALU.add))
                link(v.tensor_scalar(stat[:, 0, :], stat[:, 0, :], 1.0 / P, None, ALU.mult))
                link(v.tensor_tensor(Z, Z, free(stat[:, 0, :], P), ALU.subtract))
                link(v.tensor_tensor(scratch, Z, Z, ALU.mult))
                link(v.tensor_reduce(stat[:, 1, :], scratch, AX.X, ALU.add))
                link(v.tensor_scalar(stat[:, 1, :], stat[:, 1, :], 1.0 / P, EPS, ALU.mult, ALU.add))
                ask()
                link(v.reciprocal(stat[:, 3, :], stat[:, 2, :]))
                link(v.tensor_tensor(Z, Z, free(stat[:, 3, :], P), ALU.mult))

            def row(n, w=P):
                return across(rows[:, n, 0:w], G)

            def heads(tab):
                return tab.rearrange("p g (h c) -> p g h c", h=H)

            v.memset(X[96:P, FULL:G, :], 0.0).then_inc(s_xpad, 1)
            link(v.memset(ones[:], 1.0))
            link(v.memset(gtab[:], 0))
            dve.wait_ge(s_iota, 4)
            link(v.tensor_copy(iota[:], iota_i[:]))
            link(v.tensor_copy(sidx[:, 0, :], sidx_i[:]))
            link(v.tensor_copy(bound[:, 2, :], bound_i[:, 1, :]))
            for h in range(H):
                link(v.tensor_scalar(nident[:, h, :], ident[:], -BIG, None, ALU.mult))

            dve.wait_ge(s_dst, 16)
            link(v.tensor_copy(dloc[:, 0:T], srcs[:, 0:T]))
            less = TA[:].rearrange("p g c -> p (g c)")[:, 0:T]
            for g in range(1, G):
                link(v.tensor_scalar(less, dloc[:, 0:T], float(P * g), None, ALU.is_lt, ALU.add, accum_out=bound[:, 0, g - 1:g]))
            dve.sem_inc(s_cnt, 1)
            dve.wait_ge(s_bnd, 1)
            link(v.tensor_copy(bound_i[:, 0, :], PS[:, 0, 0:NB]))
            link(v.tensor_scalar(bound_i[:, 0, :], bound_i[:, 0, :], 7, None, ALU.arith_shift_right))
            link(v.tensor_copy(bound[:, 1, :], bound_i[:, 0, :]))
            link(v.tensor_tensor(bound[:, 1, :], bound[:, 1, :], bound[:, 2, :], ALU.add))
            cmp = TA[:].rearrange("p g c -> p (g c)")[:, 0:CH * NB].rearrange("p (c b) -> p c b", c=CH)
            link(v.tensor_tensor(cmp, free(sidx[:, 0, :], NB), across(bound[:, 1, :], CH), ALU.is_ge))
            link(v.tensor_reduce(sidx[:, 1, :], cmp, AX.X, ALU.add))
            link(v.tensor_tensor(sidx[:, 2, :], sidx[:, 0, :], sidx[:, 1, :], ALU.subtract))
            link(v.tensor_scalar(sidx[:, 3, :], sidx[:, 2, :], float(P), float(LAST), ALU.mult, ALU.min))
            link(v.tensor_scalar(sidx[:, 4, :], sidx[:, 1, :], float(P), None, ALU.mult))
            v.tensor_copy(tile_i[:, 0, :], sidx[:, 1, :]).then_inc(s_tix, 1)
            v.tensor_copy(tile_i[:, 1, :], sidx[:, 2, :]).then_inc(s_tix, 1)
            v.tensor_copy(tile_i[:, 2, :], sidx[:, 3, :]).then_inc(s_tix, 1)
            for n in range(2 * CH + 2):
                if n < 2 * CH:
                    c, f = n // 2, n % 2
                    dve.wait_ge(s_trow[2 * (c % 2) + f], 16 * (c // 2 + 1))
                    if n >= 4:
                        dve.wait_ge(s_tt, n - 3)
                    if f == 0:
                        v.tensor_scalar(tile_f[:, c % 2, 0, :], tile_rows[:, c % 2, 0, :], sidx[:, 4, c:c + 1], None, ALU.subtract).then_inc(s_tf, 1)
                    else:
                        v.tensor_copy(tile_f[:, c % 2, 1, :], tile_rows[:, c % 2, 1, :]).then_inc(s_tf, 1)
                if n >= 2:
                    m = n - 2
                    dve.wait_ge(s_tt, m + 1)
                    o = (dloc, srcs)[m % 2][:, (m // 2) * P:(m // 2 + 1) * P]
                    v.tensor_copy(o, PS[:, 2 + m % 2, 0:P]).then_inc(s_tc, 1)
            dve.wait_ge(s_tc, 2 * CH)

            def onehot(q):
                def fn(i, k):
                    g = i * UNROLL + k
                    if not (q == 0 and isinstance(i, int) and k < 8):
                        if q == 0:
                            dve.wait_ge(s_max, g - 7)
                        elif not (q == 1 and isinstance(i, int) and i == BODIES and k < 8):
                            dve.wait_ge(s_seg, g - STEPS - 7)
                    v.tensor_scalar(D[:, k % 8, :], iota[:], dloc[:, bass.ds((i - q * BODIES) * UNROLL + k, 1)], None, ALU.is_equal).then_inc(s_d, 1)
                return fn

            dve.wait_ge(s_x, 32)
            dve.wait_ge(s_in, 16 * NW)
            linear()
            for n, o in ((1, node_as[:]), (2, node_ad[:, :, 0:H])):
                link(v.tensor_tensor(TC[:], TA[:, :, 0:P], row(n), ALU.mult))
                link(v.tensor_reduce(o, heads(TC[:]), AX.X, ALU.add))
            link(v.tensor_copy(TA[:, :, P:XW], node_as[:]))
            link(v.tensor_copy(node_max[:], node_as[:]))
            dve.sem_inc(s_tabr, 1)

            dve.wait_ge(s_gtab, 32)
            loads, group, regs = group_loader(dve, 0, 2, "dvg")

            def not_onehot(i, k):
                if not (isinstance(i, int) and k < 4):
                    dve.wait_ge(s_max, i * UNROLL + k - 3)
                v.tensor_scalar(ND[:, k % 4, :], iota[:], dloc[:, bass.ds(i * UNROLL + k, 1)], None, ALU.not_equal).then_inc(s_d2, 1)

            def tile_max(i, k):
                g = i * UNROLL + k
                dve.wait_ge(s_max, g + 1)
                if not (isinstance(i, int) and k < 2):
                    dve.wait_ge(s_done, g - 1)
                v.tensor_reduce(m4[:, k % 2, :], PS[:, 4 + k % 2, :].rearrange("p (h e) -> p h e", h=H), AX.X, ALU.max).then_inc(s_red, 1)
                dve.wait_ge(s_red, g + 1)
                if not (isinstance(i, int) and k < 1):
                    dve.wait_ge(s_done, g)
                m = node_max[:, bass.ds(group(k), 1), :].rearrange("p a c -> p (a c)")
                v.tensor_tensor(m, m, m4[:, k % 2, :], ALU.max).then_inc(s_done, 1)
            run_pass(dve, 0, ((0, not_onehot), (0, onehot(0)), (2, tile_max)), loads)
            dve.wait_ge(s_done, STEPS)

            link(v.tensor_tensor(s0, node_ad[:, :, 0:H], node_max[:], ALU.add))
            link(v.scalar_tensor_tensor(out=node_ad[:, :, H:2 * H], in0=s0, scalar=SLOPE, in1=s0, op0=ALU.mult, op1=ALU.max))
            link(v.tensor_tensor(s0, node_as[:], node_ad[:, :, 0:H], ALU.add))
            link(v.scalar_tensor_tensor(out=p_self, in0=s0, scalar=SLOPE, in1=s0, op0=ALU.mult, op1=ALU.max))
            link(v.tensor_tensor(p_self, p_self, node_ad[:, :, H:2 * H], ALU.subtract))
            ask()
            link(v.memset(ACC[:], 0.0))
            link(v.tensor_copy(ACC[:, :, P:P + H], p_self))
            for h in range(H):
                link(v.tensor_tensor(ACC[:, :, h * C:(h + 1) * C], TA[:, :, h * C:(h + 1) * C], p_self[:, :, h:h + 1].to_broadcast([P, G, C]), ALU.mult))
            link(v.memset(msg[:], 1.0))

            def add_sums(q, w):
                def fn(i, k):
                    g = i * UNROLL + k
                    dve.wait_ge(s_seg, g - STEPS + 1)
                    dve.wait_ge(s_done, g)
                    a = ACC[:, bass.ds(groups[0](k), 1), 0:w].rearrange("p a c -> p (a c)")
                    v.tensor_tensor(a, a, PS[:, 6 + k % 2, 0:w], ALU.add).then_inc(s_done, 1)
                return fn
            groups = [None]
            for r in regs:
                dve.free_register(r)
            loads, groups[0], regs = group_loader(dve, 1, 6, "dva")

            def logits(i, k):
                g = (i - BODIES) * UNROLL + k
                dve.wait_ge(s_ex, g + 1)
                landed(dve, i, k)
                if not (isinstance(i, int) and i == BODIES and k < 4):
                    dve.wait_ge(s_p, g - 3)
                z, a = z4[:, k % 4], PS[:, 4 + k % 2, :]
                v.tensor_tensor(z[:, 0, :], got[:, k % RING, P:P + H], a[:, 0:H], ALU.add).then_inc(s_z, 1)
                dve.wait_ge(s_z, 3 * g + 1)
                v.scalar_tensor_tensor(out=z[:, 1, :], in0=z[:, 0, :], scalar=SLOPE, in1=z[:, 0, :], op0=ALU.mult, op1=ALU.max).then_inc(s_z, 1)
                dve.wait_ge(s_z, 3 * g + 2)
                v.tensor_tensor(z[:, 2, :], z[:, 1, :], a[:, H:2 * H], ALU.subtract).then_inc(s_z, 1)

            def messages(i, k):
                g = (i - BODIES) * UNROLL + k
                dve.wait_ge(s_p, g + 1)
                if not (isinstance(i, int) and i == BODIES and k < 2):
                    dve.wait_ge(s_seg, g - 1)
                o = msg[:, k % 2, :]
                p = p4[:, k % 4, :]
                v.scalar_tensor_tensor(out=o[:, 0:P].rearrange("p (h c) -> p h c", h=H), in0=free(p, C), scalar=1.0,
                                       in1=got[:, k % RING, 0:P].rearrange("p (h c) -> p h c", h=H), op0=ALU.min, op1=ALU.mult).then_inc(s_msg, 1)
                v.tensor_scalar(o[:, P:P + H], p, 1.0, None, ALU.min).then_inc(s_msg, 1)
            run_pass(dve, 1, ((0, onehot(1)), (2, logits), (4, messages), (6, add_sums(1, AW))), loads)
            dve.wait_ge(s_done, 2 * STEPS)

            sums = ACC[:, :, 0:P]
            link(v.tensor_scalar(ACC[:, :, P:P + H], ACC[:, :, P:P + H], 1e-16, None, ALU.add))
            link(v.reciprocal(ACC[:, :, P:P + H], ACC[:, :, P:P + H]))
            for h in range(H):
                link(v.tensor_tensor(TC[:, :, h * C:(h + 1) * C], ACC[:, :, h * C:(h + 1) * C], ACC[:, :, P + h:P + h + 1].to_broadcast([P, G, C]), ALU.mult))
            link(v.tensor_tensor(TC[:], TC[:], row(0), ALU.add))
            link(v.tensor_tensor(TB[:], TB[:], TC[:], ALU.add))
            link(v.tensor_scalar(TC[:], TB[:], 0.0, None, ALU.min))
            ask()
            link(v.tensor_scalar(TC[:], TC[:], -1.0, None, ALU.add))
            link(v.scalar_tensor_tensor(out=TC[:], in0=TB[:], scalar=0.0, in1=TC[:], op0=ALU.max, op1=ALU.add))
            link(v.tensor_tensor(X[:], X[:], TC[:], ALU.add))
            layernorm(X[:], TC[:])
            dve.sem_inc(s_tabr, 1)
            link(v.tensor_copy(count[:], ACC[:, :, P + H:AW].rearrange("p g a -> p (g a)")))
            link(v.tensor_scalar(rcount[:], count[:], 1.0, None, ALU.max))
            link(v.reciprocal(rcount[:], rcount[:]))
            link(v.tensor_scalar(dinv[:], count[:], 1.0, None, ALU.add))
            ask()
            link(v.reciprocal(dinv[:], dinv[:]))
            link(v.memset(ACC[:], 0.0))

            def sum_pass(q, w):
                for r in regs:
                    dve.free_register(r)
                loads, groups[0], new = group_loader(dve, q, 2, f"dv{q}_")
                regs[:] = new
                run_pass(dve, q, ((0, onehot(q)), (2, add_sums(q, w))), loads)
                dve.wait_ge(s_done, (q + 1) * STEPS)

            sum_pass(2, P)
            link(v.tensor_tensor(TC[:], sums, free(rcount[:], P), ALU.mult))
            linear()
            linear()
            ta = TA[:, :, 0:P]
            link(v.tensor_tensor(ta, ta, row(3), ALU.add))
            ask()
            link(v.tensor_tensor(X[:], X[:], ta, ALU.add))
            layernorm(X[:], TC[:])

            linear()
            hid = ACC[:, :, 0:HID]
            link(v.tensor_tensor(Y, TA[:, :, 0:HID], free(dinv[:], HID), ALU.mult))
            dve.sem_inc(s_tabr, 1)
            link(v.tensor_copy(hid, Y))
            sum_pass(3, HID)
            dve.wait_ge(s_tabw, 16 * 3)
            link(v.tensor_tensor(Y, hid, free(dinv[:], HID), ALU.mult))
            link(v.tensor_tensor(Y, Y, row(4, HID), ALU.add))
            link(v.tensor_tensor(Y, Y, free(dinv[:], HID), ALU.mult))
            dve.sem_inc(s_tabr, 1)
            link(v.tensor_copy(hid, Y))
            sum_pass(4, HID)
            dve.wait_ge(s_tabw, 16 * 4)
            link(v.memset(TC[:], 0.0))
            link(v.memset(wts[HID:2 * HID, 5, :], 0.0))
            link(v.memset(wts[2 * HID:P, 5, :], 0.0))
            link(v.tensor_tensor(TC[:, :, 0:HID], hid, free(dinv[:], HID), ALU.mult))
            linear()
            link(v.tensor_tensor(ta, ta, row(5), ALU.add))
            link(v.scalar_tensor_tensor(out=X[:], in0=ta, scalar=0.0, in1=X[:], op0=ALU.max, op1=ALU.add))
            layernorm(X[:], TC[:])

            linear()
            dve.sem_inc(s_tabr, 1)
            link(v.tensor_tensor(TB[:], TB[:], row(6), ALU.add))
            link(v.memset(ACC[:], 0.0))
            for r in regs:
                dve.free_register(r)
            loads, groups[0], regs = group_loader(dve, 5, 4, "dvm")

            def preactivation(i, k):
                g = (i - 5 * BODIES) * UNROLL + k
                dve.wait_ge(s_ex, STEPS + g + 1)
                landed(dve, i, k)
                if not (isinstance(i, int) and k < 2):
                    dve.wait_ge(s_silu, g - 1)
                v.tensor_tensor(pre[:, k % 2, :], got[:, k % RING, 0:P], PS[:, 4 + k % 2, 0:P], ALU.add).then_inc(s_pre, 1)
            run_pass(dve, 5, ((0, onehot(5)), (2, preactivation), (4, add_sums(5, P))), loads)
            dve.wait_ge(s_done, 6 * STEPS)
            link(v.tensor_copy(TC[:], sums))
            dve.wait_ge(s_tabw, 16 * 5)
            linear()
            link(v.tensor_tensor(TC[:], free(count[:], P), row(7), ALU.mult))
            link(v.tensor_tensor(ta, ta, TC[:], ALU.add))
            link(v.tensor_tensor(ta, ta, free(rcount[:], P), ALU.mult))
            linear()
            linear()
            link(v.tensor_tensor(TB[:], TB[:], row(8), ALU.add))
            ask()
            link(v.tensor_tensor(TC[:], TC[:], row(9), ALU.add))
            ask()
            link(v.tensor_tensor(ta, X[:], TC[:], ALU.subtract))
            link(v.tensor_tensor(ta, ta, TB[:], ALU.mult))
            link(v.tensor_tensor(TC[:], TC[:], ta, ALU.add))
            layernorm(TC[:], TB[:])
            link(v.tensor_tensor(TC[:], TC[:], row(10), ALU.mult))
            link(v.tensor_tensor(TC[:], TC[:], row(11), ALU.add))
            link(v.tensor_tensor(X[:], X[:], TC[:], ALU.add))
            layernorm(X[:], TC[:])
            dve.sem_inc(s_tabr, 1)


_NAMES = {"x": "x", "src": "src", "dst": "dst", "edge_attr_64": "edge_attr_64",
          "att_src": "L0_gnn_att_src", "att_dst": "L0_gnn_att_dst", "L0_bias": "L0_gnn_bias",
          "L1_b": "L1_gnn_b_l", "L2_W1": "L2_gnn_W1", "L2_b1": "L2_gnn_b1", "L2_W2": "L2_gnn_W2", "L2_b2": "L2_gnn_b2",
          "L3_W1": "L3_gnn_W1", "L3_b1": "L3_gnn_b1", "L3_W2": "L3_gnn_W2", "L3_b2": "L3_gnn_b2",
          "L3_Wg": "L3_gnn_Wg", "L3_bg": "L3_gnn_bg", "L3_Wt": "L3_gnn_Wt", "L3_bt": "L3_gnn_bt",
          "gamma": "L3_gnn_gamma", "beta": "L3_gnn_beta"}
_TRANSPOSED = {"gatT": "L0_gnn_W_gat", "skipT": "L0_gnn_W_skip", "WlT": "L1_gnn_W_l", "WrT": "L1_gnn_W_r"}


def kernel(**inputs):
    import numpy as np
    import concourse.bacc as bacc
    from concourse.bass_utils import run_bass_kernel_spmd

    nc = bacc.Bacc("TRN2", target_bir_lowering=False, num_devices=1)
    arrays, A = {}, {}
    for short, name in _NAMES.items():
        arrays[f"in_{short}"] = np.ascontiguousarray(inputs[name])
    for short, name in _TRANSPOSED.items():
        arrays[f"in_{short}"] = np.ascontiguousarray(np.asarray(inputs[name]).T)
    for key, a in arrays.items():
        A[key[3:]] = nc.dram_tensor(key, a.shape, mybir.dt.from_np(a.dtype), kind="ExternalInput").ap()
    out = nc.dram_tensor("out_x", A["x"].shape, F32, kind="ExternalOutput").ap()
    gnn(nc, A, out)
    r = run_bass_kernel_spmd(nc, [arrays], core_ids=[0])
    return r.results[0]["out_x"]
```

```python
from contextlib import ExitStack

import concourse.bass as bass
from concourse import mybir

ALU = mybir.AluOpType
ACT = mybir.ActivationFunctionType
AX = mybir.AxisListType
F32 = mybir.dt.float32
BF16 = mybir.dt.bfloat16
I32 = mybir.dt.int32

P = 128
EPS = 1e-5
BIG = float(2.0 ** 100)
SLOPE = 0.2
NO_NODE = 20000
UNROLL = 32
RING = 16
QUARTER = 8
SUB = 8
AUNROLL = 48
FINE = 256
LIN = 7
XW = 132
AW = 133


def gnn(nc, A, out):
    N, DF = A["x"].shape
    E = A["src"].shape[0]
    DE = A["edge_attr_64"].shape[1]
    H, C = A["att_src"].shape
    HID = A["L2_W1"].shape[1]
    G = -(-N // P)
    T = -(-E // P)
    FULL = N // P
    TAIL = N - FULL * P
    STEPS = -(-(T + G - 1) // UNROLL) * UNROLL
    BODIES = STEPS // UNROLL
    CH = STEPS // P
    HI = G
    AC = SUB * HI
    SG = G * P // SUB
    ASTEPS = BODIES * AUNROLL
    ACH = -(-ASTEPS // P)
    VCH = -(-SG // P)
    TP = STEPS - (G - 1)
    LAST = E - P
    OVER = T * P - E
    NB = G - 1
    assert DF == P and G % LIN == 0 and STEPS % P == 0 and TP >= T and OVER > 0
    assert AC <= 512 and ASTEPS >= T + SG + 1 and (G - 1) % 3 == 0 and T <= 2048

    def dram(name, shape, dt):
        return nc.dram_tensor(name, shape, dt).ap()

    dst_pad = dram("dst_pad", [TP, P], I32)
    src_pad = dram("src_pad", [TP, P], I32)
    src_steps = dram("src_steps", [P, STEPS], I32)
    group_steps = dram("group_steps", [1, STEPS], I32)
    asteps = dram("asteps", [1, ACH * P], mybir.dt.int16)
    base_steps = dram("base_steps", [1, STEPS], I32)
    adj = dram("adj", [P, SG + 1, AC], BF16)
    tab_proj = dram("tab_proj", [G * P, XW], F32)
    tab_x = dram("tab_x", [G * P, P], F32)
    tab_y1 = dram("tab_y1", [G * P, HID], F32)
    tab_y2 = dram("tab_y2", [G * P, HID], F32)
    tab_ps = dram("tab_ps", [G * P, P], F32)

    with ExitStack() as ctx:
        def sb(name, shape, dt=F32):
            return ctx.enter_context(nc.sbuf_tensor(name, shape, dt))

        def sem(name):
            return ctx.enter_context(nc.semaphore(name))

        X = sb("X", [P, G, P])
        ACC = sb("ACC", [P, G, AW])
        region = sb("region", [P, G * (XW + 2 * P)])
        TA = region[:, 0:G * XW].rearrange("p (g c) -> p g c", g=G)
        TB = region[:, G * XW:G * (XW + P)].rearrange("p (g c) -> p g c", g=G)
        TC = region[:, G * (XW + P):].rearrange("p (g c) -> p g c", g=G)
        region16 = region[:].bitcast(BF16)
        parts = region16[:, 0:G * 3 * P]
        acols = region16[:, G * 3 * P:G * 3 * P + 3 * P // SUB * AC].rearrange("p (b c) -> p b c", b=3)
        node_ad = sb("node_ad", [P, G, 2 * H])
        node_as = sb("node_as", [P, G, H])
        node_max = sb("node_max", [P, G, H])
        stat = sb("stat", [P, 4, G])
        count = sb("count", [P, G])
        rcount = sb("rcount", [P, G])
        dinv = sb("dinv", [P, G])
        dloc = sb("dloc", [P, STEPS])
        srcs = sb("srcs", [P, STEPS], I32)
        gtab = sb("gtab", [1, QUARTER + STEPS + UNROLL], I32)
        atab = sb("atab", [1, 16 + ACH * P + 32], mybir.dt.int16)
        iota = sb("iota", [P, P])
        ident = sb("ident", [P, P])
        nident = sb("nident", [P, H, P], BF16)
        iota16 = sb("iota16", [P, AC], mybir.dt.float16)
        flag = sb("flag", [P, 2])
        flag_i = sb("flag_i", [1, 1], I32)
        ones = sb("ones", [P, P])
        wts = sb("wts", [P, 14, P])
        rows = sb("rows", [P, 12, P])
        fill = sb("fill", [8, 2, P], I32)
        astage = sb("astage", [P, 8, AC], BF16)
        setup = ACC[:].rearrange("p g a -> p (g a)")
        trow = setup[:, 0:VCH * P]
        pos = setup[:, VCH * P:2 * VCH * P]
        cmp = setup[:, 2 * VCH * P:3 * VCH * P]
        dg = setup[:, 3 * VCH * P:4 * VCH * P].rearrange("p (c v) -> p c v", c=VCH)
        first_i = setup[0:1, 4 * VCH * P:4 * VCH * P + T].bitcast(I32)
        first = setup[0:1, 0:T]
        vcol = sb("vcol", [P, 2, VCH])
        sidx = sb("sidx", [P, 5, CH])
        tile_i = sb("tile_i", [P, 3, CH], I32)
        atile = sb("atile", [P, 4, ACH])
        atile_i = sb("atile_i", [P, ACH], I32)
        tile_rows = sb("tile_rows", [P, 2, 2, P], I32)
        tile_f = sb("tile_f", [P, 2, 2, P])
        alo = TC.rearrange("p g c -> p (g c)")[:, 0:ACH * P]
        akey = TC.rearrange("p g c -> p (g c)")[:, ACH * P:2 * ACH * P]
        LO = region16[:, 0:4 * P].rearrange("p (k c) -> p k c", k=4)
        KEY = region16[:, 4 * P:4 * P + 4 * AC].rearrange("p (k c) -> p k c", k=4)
        zero16 = region16[:, 4 * P + 4 * AC:4 * P + 4 * AC + P]
        idx = sb("idx", [P, UNROLL], I32)
        got = sb("got", [P, RING, XW])
        D = sb("D", [P, 8, P])
        ND = sb("ND", [P, 4, P], BF16)
        DT = sb("DT", [P, 2, P])
        diag = sb("diag", [P, 2, H, P])
        m4 = sb("m4", [P, 2, H])
        z4 = sb("z4", [P, 4, 3, H])
        p4 = sb("p4", [P, 4, H])
        msg = sb("msg", [P, 3, AW])
        ef = sb("ef", [P, 8, DE])
        efT = sb("efT", [DE, 2, P])
        pre = sb("pre", [P, 2, P])
        silu_out = sb("silu_out", [P, 2, P])
        tc = TC.rearrange("p g c -> p (g c)")
        Y = TB.rearrange("p g c -> p (g c)")[:, 0:G * HID].rearrange("p (g c) -> p g c", g=G)
        s0 = tc[:, 0:G * H].rearrange("p (g h) -> p g h", g=G)
        p_self = tc[:, G * H:2 * G * H].rearrange("p (g h) -> p g h", g=G)
        flat = got[:].rearrange("p r w -> p (r w)")
        stage = flat[:, 0:LIN * P].rearrange("p (j c) -> p j c", j=LIN)
        xT = flat[:, LIN * P:2 * LIN * P].rearrange("p (j c) -> p j c", j=LIN)

        PS = ctx.enter_context(nc.psum_tensor("PS", [P, 8, 512], F32))
        ps_flat = PS[:].rearrange("p b c -> p (b c)")
        lin_in = ps_flat[:, 0:LIN * P].rearrange("p (j c) -> p j c", j=LIN)
        lin_o = ps_flat[:, 1024:1024 + LIN * 2 * P].rearrange("p (j c) -> p j c", j=LIN)

        s_in = sem("inputs_landed")
        s_x = sem("x_landed")
        s_xpad = sem("x_pad_zeroed")
        s_fill = sem("fill_ready")
        s_pad1 = sem("pad_rows_written")
        s_pad = sem("pad_lists_written")
        s_dst = sem("dst_landed")
        s_iota = sem("iotas_ready")
        s_bnd = sem("bounds_summed")
        s_tix = sem("tile_indices_ready")
        s_trow = [sem(f"tile_rows_landed{i}") for i in range(4)]
        s_tf = sem("tile_rows_converted")
        s_tt = sem("tile_rows_transposed")
        s_tc = sem("step_columns_stored")
        s_steps = sem("step_tables_written")
        s_gtab = sem("step_registers_landed")
        s_chain = sem("dve_chain")
        s_pool = sem("pool_chain")
        s_slot = sem("gather_slot_free")
        s_linr = sem("linear_input_ready")
        s_linw = sem("linear_staged")
        s_linT = sem("linear_transposed")
        s_linX = sem("linear_xT_ready")
        s_linY = sem("linear_product_ready")
        s_linO = sem("linear_stored")
        s_areq = sem("act_request")
        s_arep = sem("act_reply")
        s_tabr = sem("table_ready")
        s_tabw = sem("table_written")
        s_vrow = sem("boundary_rows")
        s_atix = sem("adjacency_indices_ready")
        s_ahot = sem("adjacency_onehots_ready")
        s_amm = sem("adjacency_counts_added")
        s_acp = sem("adjacency_columns_copied")
        s_adma = [sem(f"adjacency_columns_written{i}") for i in range(8)]
        s_aload = [sem(f"adjacency_landed{i}") for i in range(3)]
        s_parts = sem("parts_ready")
        s_dmm = sem("dense_sums_ready")
        s_dev = sem("dense_sums_stored")
        s_flag = sem("path_flag_ready")
        s_flagf = sem("most_edges_turned")
        s_zero = sem("banks_zeroed")
        s_cols = sem("columns_seen")

        class Pass:
            def __init__(self, name):
                self.idx = [sem(f"{name}_indices_landed{i}") for i in range(UNROLL // QUARTER)]
                self.got = [sem(f"{name}_gathered{i}") for i in range(RING)]
                self.d = sem(f"{name}_onehot_ready")
                self.seg = sem(f"{name}_segment_sums_ready")
                self.done = sem(f"{name}_step_done")

        main, fall = Pass("edge"), Pass("fallback")
        s_d, s_seg, s_done = main.d, main.seg, main.done
        s_d2 = sem("not_onehot_ready")
        s_diag = sem("diag_ready")
        s_max = sem("masked_scores_ready")
        s_red = sem("tile_max_ready")
        s_dT = sem("onehot_transposed")
        s_dTc = sem("onehotT_stored")
        s_ex = sem("expanded")
        s_z = sem("logit_step")
        s_p = sem("weights_ready")
        s_msg = sem("messages_ready")
        s_ef = [sem(f"edge_features_landed{i}") for i in range(8)]
        s_fT = sem("edge_features_transposed")
        s_fTc = sem("edge_featuresT_stored")
        s_pre = sem("preactivation_ready")
        s_silu = sem("silu_ready")
        s_out = sem("output_written")
        block = ctx.enter_context(nc.Block())

        NW = 14 + 12
        x_in = A["x"]
        srow = setup[:, 4 * VCH * P + T:5 * VCH * P + T]
        junk = region16[:, 0:2048]
        ag16 = sb("ag16", [P, ACH], mybir.dt.int16)
        MAIN, FALL = 3, 3

        def free(ap, w):
            return ap.unsqueeze(2).to_broadcast([P, ap.shape[1], w])

        def across(ap, n):
            return ap.unsqueeze(1).to_broadcast([P, n, ap.shape[1]])

        def part_table(w):
            return parts[:, 0:G * 3 * w].rearrange("p (g k c) -> p g k c", g=G, k=3)

        def at_start(i, k, n):
            return isinstance(i, int) and i == 0 and k < n

        def dense_groups(eng, group):
            for j in range(3):
                group(0, j)
            with eng.Fori(1, (G - 1) // 3) as i:
                for j in range(3):
                    group(i, j)
            group((G - 1) // 3, 0)

        def choose(eng, d, dense, general):
            reg = eng.alloc_register(f"most_edges{d}")
            eng.load([reg], flag_i[0:1, 0:1])
            most = eng.snap(reg, min_val=0, max_val=1 << 24)
            with eng.If(most > FINE):
                general()
            with eng.Else():
                dense()
            eng.free_register(reg)

        @block.sync
        def _(sp):
            sp.wait_ge(s_xpad, 1)
            with nc.allow_non_contiguous_dma(reason="the first edge of each tile"):
                sp.dma_start(first_i[:, 0:T - 1].unsqueeze(2), A["dst"][0:(T - 1) * P].rearrange("(a t p) -> a t p", a=1, p=P)[:, :, 0:1]).then_inc(s_dst, 16)
                sp.dma_start(first_i[:, T - 1:T], A["dst"][(T - 1) * P:(T - 1) * P + 1].unsqueeze(0)).then_inc(s_dst, 16)
            sp.wait_ge(s_fill, 2)
            for pad, lst, f in ((dst_pad, A["dst"], 0), (src_pad, A["src"], 1)):
                pf = pad.rearrange("t p -> (t p)")
                body = (T - 1) * P
                sp.dma_start(pf[0:body].rearrange("(a b) -> a b", b=P), lst[0:body].rearrange("(a b) -> a b", b=P)).then_inc(s_pad, 16)
                sp.dma_start(pad[T - 1:TP, :], fill[0:TP - T + 1, f, :]).then_inc(s_pad1, 16)
            sp.wait_ge(s_pad1, 32)
            for pad, lst in ((dst_pad, A["dst"]), (src_pad, A["src"])):
                sp.dma_start(pad[T - 1:T, OVER:P], lst[(T - 1) * P:E].unsqueeze(0)).then_inc(s_pad, 16)
            sp.dma_start(X[:, 0:FULL, :], x_in[0:FULL * P].rearrange("(g p) f -> p g f", p=P)).then_inc(s_x, 16)
            sp.dma_start(X[0:TAIL, FULL:G, :], x_in[FULL * P:N].unsqueeze(1)).then_inc(s_x, 16)
            for n, w in enumerate(("gatT", "skipT", "WlT", "WrT")):
                sp.dma_start(wts[:, n, :], A[w]).then_inc(s_in, 16)
            sp.dma_start(wts[:, 4, 0:HID], A["L2_W1"]).then_inc(s_in, 16)
            sp.dma_start(wts[0:HID, 5, :], A["L2_W2"]).then_inc(s_in, 16)
            sp.dma_start(wts[:, 6, :], A["L3_W1"][0:P]).then_inc(s_in, 16)
            sp.dma_start(wts[:, 7, :], A["L3_W1"][P:2 * P]).then_inc(s_in, 16)
            sp.dma_start(wts[:, 8, :], A["L3_W2"]).then_inc(s_in, 16)
            sp.dma_start(wts[:, 9, :], A["L3_Wg"][0:P]).then_inc(s_in, 16)
            sp.dma_start(wts[:, 10, :], A["L3_Wt"][0:P]).then_inc(s_in, 16)
            sp.dma_start(wts[:, 11, :], A["L3_Wg"][P:2 * P]).then_inc(s_in, 16)
            sp.dma_start(wts[:, 12, :], A["L3_Wt"][P:2 * P]).then_inc(s_in, 16)
            sp.dma_start(wts[0:DE, 13, :], A["L3_W1"][2 * P:2 * P + DE]).then_inc(s_in, 16)
            for n, b in enumerate(("L0_bias", "att_src", "att_dst", "L1_b", "L2_b1", "L2_b2", "L3_b1", "L3_b2",
                                   "L3_bg", "L3_bt", "gamma", "beta")):
                row = A[b].rearrange("h c -> (h c)") if len(A[b].shape) == 2 else A[b]
                sp.dma_start(rows[:, n, 0:row.shape[0]], row.partition_broadcast(P)).then_inc(s_in, 16)

            sp.wait_ge(s_tix, 3)
            with nc.allow_non_contiguous_dma(reason="small tables"):
                sp.dma_start(group_steps.rearrange("a (c p) -> p (a c)", p=P), tile_i[:, 0, :]).then_inc(s_steps, 16)
                sp.dma_start(base_steps.rearrange("a (c p) -> p (a c)", p=P), tile_i[:, 2, :]).then_inc(s_steps, 16)
                sp.wait_ge(s_atix, 2)
                sp.dma_start(asteps.rearrange("a (c p) -> p (a c)", p=P), ag16[:, :]).then_inc(s_steps, 16)
            sp.wait_ge(s_steps, 48)
            sp.dma_start(gtab[:, QUARTER:QUARTER + STEPS], group_steps).then_inc(s_gtab, 16)
            sp.dma_start(atab[:, 16:16 + ACH * P], asteps).then_inc(s_gtab, 16)
            sp.wait_ge(s_tc, 2 * CH)
            sp.dma_start(src_steps, srcs[:, :]).then_inc(s_steps, 16)
            sp.wait_ge(s_steps, 64)
            sp.wait_ge(s_gtab, 32)

            def write_table(n, tab, view):
                sp.wait_ge(s_tabr, n)
                sp.dma_start(tab.rearrange("(g p) f -> p g f", p=P), view).then_inc(s_tabw, 16)

            def first_indices(S, p):
                if p:
                    sp.wait_ge(S.done, p * STEPS)
                for r in range(UNROLL // QUARTER):
                    sp.dma_start(idx[:, r * QUARTER:(r + 1) * QUARTER], src_steps[:, r * QUARTER:(r + 1) * QUARTER]).then_inc(S.idx[r], 16)

            def refresh(S, p, i, r):
                sp.wait_ge(S.done, i * UNROLL + (r + 1) * QUARTER)
                at = (i - p * BODIES + 1) * UNROLL + r * QUARTER
                sp.dma_start(idx[:, r * QUARTER:(r + 1) * QUARTER], src_steps[:, bass.ds(at, QUARTER)]).then_inc(S.idx[r], 16)

            def refresh_all(S, p):
                first_indices(S, p)
                with sp.Fori(p * BODIES, (p + 1) * BODIES - 1) as i:
                    for r in range(UNROLL // QUARTER):
                        refresh(S, p, i, r)

            write_table(1, tab_proj, TA)
            refresh_all(main, 0)

            first_indices(main, 1)
            small = [sp.alloc_register(f"small{k}") for k in range(17)]

            def columns(i, kb):
                b = (i - BODIES) * AUNROLL + kb
                if kb % 16 == 0:
                    sp.load(small, atab[0:1, bass.ds(16 + b, 17)])
                g = sp.snap(small[kb % 16], min_val=0, max_val=SG)
                after = sp.snap(small[kb % 16 + 1], min_val=0, max_val=SG)
                sp.wait_ge(s_acp, b + 1)
                sp.sem_inc(s_cols, 1)
                sp.dma_start(adj[:, bass.ds(g, 1), :].rearrange("p a c -> p (a c)"),
                             astage[:, bass.ds((g + 7) & 7, 1), :].rearrange("p a c -> p (a c)"),
                             cond=(after != g)).then_inc(s_adma[kb % 8], 16)

            def column_body(i, peeled, last):
                for kb in range(AUNROLL):
                    columns(i, kb)
                    if kb % 12 == 10 and not (peeled and kb == 10):
                        r = kb // 12 - 1
                        if r < 0:
                            refresh(main, 1, i - 1, UNROLL // QUARTER - 1)
                        elif not last:
                            refresh(main, 1, i, r)
            column_body(BODIES, True, False)
            with sp.Fori(BODIES + 1, 2 * BODIES - 1) as i:
                column_body(i, False, False)
            column_body(2 * BODIES - 1, False, True)
            for r in range(8):
                sp.wait_ge(s_adma[r], 16 * ASTEPS // 8)
            sp.dma_start(adj[:, SG, :], astage[:, (SG - 1) % 8, :]).then_inc(s_adma[0], 16)
            sp.wait_ge(s_adma[0], 16 * (ASTEPS // 8 + 1))
            for r in small:
                sp.free_register(r)

            def dense(d):
                def load(i, j):
                    n = d * G + 3 * i + j
                    if not (isinstance(i, int) and i == 0):
                        sp.wait_ge(s_dmm, n - 2)
                    at = (3 * i + j) * (P // SUB) + 1
                    sp.dma_start(acols[:, j, :].rearrange("p (g c) -> p g c", g=P // SUB), adj[:, bass.ds(at, P // SUB), :]).then_inc(s_aload[j], 16)
                sp.wait_ge(s_parts, d + 1)
                dense_groups(sp, load)

            for d, (tab, view) in enumerate(((tab_x, X[:, :, :]), (tab_y1, Y), (tab_y2, Y))):
                write_table(2 + d, tab, view)
                sp.wait_ge(s_tabw, 16 * (2 + d))
                if d == 0:
                    sp.wait_ge(s_flag, 1)
                choose(sp, d, lambda: dense(d), lambda: refresh_all(fall, d))

            write_table(5, tab_ps, TA[:, :, 0:P])
            first_indices(main, 2)
            base_regs = [sp.alloc_register(f"base{k}") for k in range(16)]

            def features(i, half, first):
                sp.load(base_regs, base_steps[0:1, bass.ds((i - 2 * BODIES) * UNROLL + 16 * half, 16)])
                for k in range(16 * half, 16 * half + 16):
                    base = sp.snap(base_regs[k % 16], min_val=0, max_val=LAST)
                    if not (first and k < 8):
                        sp.wait_ge(s_done, i * UNROLL + k - 7)
                    sp.dma_start(ef[:, k % 8, :], A["edge_attr_64"][bass.ds(base, P), :]).then_inc(s_ef[k % 8], 16)
                    if k % 8 == 7 and not (first and k == 7):
                        r = k // 8 - 1
                        if r < 0:
                            refresh(main, 2, i - 1, UNROLL // QUARTER - 1)
                        elif not (isinstance(i, int) and i == 3 * BODIES - 1):
                            refresh(main, 2, i, r)
            for half in range(2):
                features(2 * BODIES, half, True)
            with sp.Fori(2 * BODIES + 1, 3 * BODIES - 1) as i:
                for half in range(2):
                    features(i, half, False)
            for half in range(2):
                features(3 * BODIES - 1, half, False)
            sp.wait_ge(s_tabr, 6)
            sp.dma_start(out[0:FULL * P].rearrange("(g p) f -> p g f", p=P), X[:, 0:FULL, :]).then_inc(s_out, 16)
            sp.dma_start(out[FULL * P:N].unsqueeze(1), X[0:TAIL, FULL:G, :]).then_inc(s_out, 16)
            sp.wait_ge(s_out, 32)

        @block.gpsimd
        def _(pool):
            nc.gpsimd.memset(fill[:, 0, :], NO_NODE).then_inc(s_fill, 1)
            nc.gpsimd.memset(fill[:, 1, :], 0).then_inc(s_fill, 1)
            nc.gpsimd.memset(ident[:], 0.0).then_inc(s_pool, 1)
            exact = dict(allow_small_or_imprecise_dtypes=True)
            nc.gpsimd.iota(iota[:], [[1, P]], base=0, channel_multiplier=0, **exact).then_inc(s_iota, 1)
            nc.gpsimd.iota(iota16[:], [[1, AC]], base=0, channel_multiplier=0, **exact).then_inc(s_iota, 1)
            nc.gpsimd.iota(sidx[:, 0, 0:CH], [[P, CH]], base=0, channel_multiplier=1, **exact).then_inc(s_iota, 1)
            nc.gpsimd.iota(atile[:, 0, :], [[P, ACH]], base=0, channel_multiplier=1, **exact).then_inc(s_iota, 1)
            nc.gpsimd.iota(vcol[:, 0, :], [[SUB * P, VCH]], base=SUB, channel_multiplier=SUB, **exact).then_inc(s_iota, 1)
            nc.gpsimd.iota(srow, [[1, VCH * P]], base=1, channel_multiplier=0, **exact).then_inc(s_iota, 1)
            pool.wait_ge(s_pool, 1)
            nc.gpsimd.affine_select(out=ident[:], in_=ident[:], compare_op=ALU.not_equal, fill=1.0, base=0,
                                    pattern=[[-1, P]], channel_multiplier=1).then_inc(s_iota, 1)
            pool.wait_ge(s_pad, 64)
            pool.wait_ge(s_tix, 3)

            def tile_gather(cc, index):
                for f, pad in enumerate((dst_pad, src_pad)):
                    if cc >= 2:
                        pool.wait_ge(s_tf, 2 * (cc - 2) + f + 1)
                    nc.gpsimd.indirect_dma_start(
                        out=tile_rows[:, cc % 2, f, :], out_offset=None, in_=pad,
                        in_offset=bass.IndirectOffsetOnAxis(ap=index, axis=0)).then_inc(s_trow[2 * (cc % 2) + f], 16)
            for c in range(CH):
                tile_gather(c, tile_i[:, 1, c:c + 1])

            def gathers(S, p, tab, w, written):
                pool.wait_ge(s_tabw, 16 * written)

                def body(i, first):
                    for k in range(UNROLL):
                        r = k // QUARTER
                        if k % QUARTER == 0:
                            pool.wait_ge(S.idx[r], i * 16 + 16)
                        if not (first and p == 0 and k < RING):
                            pool.wait_ge(S.done, i * UNROLL + k - RING + 1)
                        pool.sem_inc(s_slot, 1)
                        nc.gpsimd.indirect_dma_start(
                            out=got[:, k % RING, 0:w], out_offset=None, in_=tab,
                            in_offset=bass.IndirectOffsetOnAxis(ap=idx[:, k:k + 1], axis=0)).then_inc(S.got[k % RING], 16)

                body(p * BODIES, True)
                with pool.Fori(p * BODIES + 1, (p + 1) * BODIES) as i:
                    body(i, False)

            gathers(main, 0, tab_proj, XW, 1)
            pool.wait_ge(s_atix, 2)
            for c in range(ACH):
                tile_gather(CH + c, atile_i[:, c:c + 1])
            gathers(main, 1, tab_proj, XW, 1)
            pool.wait_ge(s_flag, 1)
            for d, (tab, w) in enumerate(((tab_x, P), (tab_y1, HID), (tab_y2, HID))):
                pool.wait_ge(s_tabw, 16 * (2 + d))
                choose(pool, d, lambda: pool.sem_inc(s_slot, 1), lambda: gathers(fall, d, tab, w, 2 + d))
            gathers(main, 2, tab_ps, P, 5)

        def landed(eng, S, i, k):
            eng.wait_ge(S.got[k % RING], i * (16 * UNROLL // RING) + 16 * (k // RING + 1))

        def run_pass(eng, p, stages, loads=None, sub=(), subloads=None):
            first = p * BODIES

            def one(i, k, peeled, which, unroll):
                for lag, fn in which:
                    if k >= lag:
                        fn(i, k - lag)
                    elif not peeled:
                        fn(i - 1, k - lag + unroll)

            def body(i, peeled):
                for k in range(UNROLL):
                    if k % 16 == 0 and loads:
                        loads(i, k // 16)
                    one(i, k, peeled, stages, UNROLL)
                    if sub:
                        for kb in range(AUNROLL * k // UNROLL, AUNROLL * (k + 1) // UNROLL):
                            if kb % 16 == 0 and subloads:
                                subloads(i, kb // 16)
                            one(i, kb, peeled, sub, AUNROLL)

            body(first, True)
            with eng.Fori(first + 1, first + BODIES) as i:
                body(i, False)
            last = first + BODIES - 1
            for which, load, unroll in ((stages, loads, UNROLL), (sub, subloads, AUNROLL)):
                most = max([lag for lag, _ in which], default=0)
                if most and load:
                    load(last + 1, 0)
                for k in range(most):
                    for lag, fn in which:
                        if k < lag:
                            fn(last, k - lag + unroll)

        def group_loader(eng, p, lag, name):
            regs = [eng.alloc_register(f"{name}{k}") for k in range(16)]

            def loads(i, n):
                eng.load(regs, gtab[0:1, bass.ds((i - p * BODIES) * UNROLL + 16 * n + QUARTER - lag, 16)])

            def group(k):
                return eng.snap(regs[(k + lag) % 16], min_val=0, max_val=G - 1)

            return loads, group, regs

        def small_loader(eng, lag, name):
            regs = [eng.alloc_register(f"{name}{k}") for k in range(16)]

            def loads(i, n):
                eng.load(regs, atab[0:1, bass.ds((i - BODIES) * AUNROLL + 16 * n + 16 - lag, 16)])

            def group(k):
                return eng.snap(regs[(k + lag) % 16], min_val=0, max_val=SG)

            return loads, group, regs

        def release(eng, regs):
            for r in regs:
                eng.free_register(r)

        def sums_bank(k, w):
            return PS[:, 6 + k % 2, 0:w]

        LINEARS = (
            (X, 0, 2 * P, ((TA, "copy"), (TB, "copy"))),
            (TC, 2, P, ((TA, "copy"),)),
            (X, 3, P, ((TA, "add"),)),
            (X, 4, HID, ((TA, "copy"),)),
            (TC, 5, P, ((TA, "copy"),)),
            (X, 6, 2 * P, ((TA, "copy"), (TB, "copy"))),
            (TC, 8, P, ((TA, "copy"),)),
            (X, 9, 2 * P, ((TB, "copy"), (TC, "copy"))),
            (TA, 11, 2 * P, ((TB, "add"), (TC, "add"))),
        )
        NL = G // LIN

        @block.tensor
        def _(pe):
            pe.sem_inc(s_linT, 1)
            pe.sem_inc(s_linY, 1)
            pe.wait_ge(s_vrow, 1)
            for c in range(0, T, 512):
                w = min(512, T - c)
                mm = nc.tensor.matmul(PS[:, c // 512, 0:w], ones[0:1, :], first[:, c:c + w], start=True, stop=True)
            mm.then_inc(s_bnd, 1)
            pe.wait_ge(s_vrow, 2)
            nc.tensor.matmul(PS[:, 4, :], ones[:], dg[:, 0:4, :].rearrange("p c v -> p (c v)"), start=True, stop=True)
            nc.tensor.matmul(PS[:, 5, 0:(VCH - 4) * P], ones[:], dg[:, 4:VCH, :].rearrange("p c v -> p (c v)"), start=True, stop=True).then_inc(s_bnd, 1)
            pe.wait_ge(s_iota, 7)

            def tile_transposes(first_n, last_n):
                for n in range(first_n, last_n):
                    pe.wait_ge(s_tf, n + 1)
                    if n >= 2:
                        pe.wait_ge(s_tc, n - 1)
                    nc.tensor.transpose(PS[:, 2 + n % 2, 0:P], tile_f[:, (n // 2) % 2, n % 2, :], ident[:]).then_inc(s_tt, 1)
            tile_transposes(0, 2 * CH)
            pe.wait_ge(s_in, 16 * NW)

            def linear(L):
                _, w, cols, _ = LINEARS[L]
                with pe.Fori(L * NL, (L + 1) * NL) as i:
                    pe.wait_ge(s_linw, i + 1)
                    pe.wait_ge(s_linX, i + 1)
                    for j in range(LIN):
                        mm = nc.tensor.transpose(lin_in[:, j, :], stage[:, j, :], ident[:])
                    mm.then_inc(s_linT, 1)
                    pe.wait_ge(s_linX, i + 2)
                    pe.wait_ge(s_linO, 2 * i + 2)
                    rhs = wts[:, w:w + 2, :].rearrange("p a b -> p (a b)")[:, 0:cols]
                    for j in range(LIN):
                        mm = nc.tensor.matmul(lin_o[:, j, 0:cols], xT[:, j, :], rhs, start=True, stop=True)
                    mm.then_inc(s_linY, 1)

            def segment_sum(S, w, rhs, ready):
                base = BODIES if S is main else 0

                def fn(i, k):
                    ready(i, k)
                    if not at_start(i - base if isinstance(i, int) else i, k, 2):
                        pe.wait_ge(S.done, i * UNROLL + k - 1)
                    nc.tensor.matmul(sums_bank(k, w), D[:, k % 8, :], rhs(k), start=True, stop=True).then_inc(S.seg, 1)
                return fn

            def transpose_onehot(p):
                banks = 1 if p == 1 else 2

                def fn(i, k):
                    pe.wait_ge(s_d, i * UNROLL + k + 1)
                    if not at_start(i - BODIES if isinstance(i, int) else i, k, banks):
                        pe.wait_ge(s_dTc, (i - BODIES) * UNROLL + k + 1 - banks)
                    nc.tensor.transpose(PS[:, k % banks, 0:P], D[:, k % 8, :], ident[:]).then_inc(s_dT, 1)
                return fn

            linear(0)

            def masked_scores(i, k):
                g = i * UNROLL + k
                pe.wait_ge(s_d, g + 1)
                pe.wait_ge(s_d2, g + 1)
                pe.wait_ge(s_diag, g + 1)
                if not at_start(i, k, 2):
                    pe.wait_ge(s_red, g - 1)
                o = PS[:, 4 + k % 2, :]
                nc.tensor.matmul(o, D[:, k % 8, :], diag[:, k % 2].rearrange("p h e -> p (h e)"), start=True, stop=False)
                nc.tensor.matmul(o, ND[:, k % 4, :], nident[:].rearrange("p h e -> p (h e)"), start=False, stop=True).then_inc(s_max, 1)
            run_pass(pe, 0, ((0, masked_scores),))
            tile_transposes(2 * CH, 2 * (CH + ACH))

            pe.wait_ge(s_gtab, 32)
            loads, group, regs = group_loader(pe, 1, 1, "peg")
            subloads, small, sregs = small_loader(pe, 0, "pea")

            def expand_scores(i, k):
                g = (i - BODIES) * UNROLL + k
                pe.wait_ge(s_dTc, g + 1)
                if not (isinstance(i, int) and i == BODIES and k < 1):
                    pe.wait_ge(s_z, 3 * g)
                nc.tensor.matmul(PS[:, 1, 0:2 * H], DT[:, k % 2, :], node_ad[:, bass.ds(group(k), 1), :].rearrange("p a c -> p (a c)"),
                                 start=True, stop=True).then_inc(s_ex, 1)

            def attention_ready(i, k):
                pe.wait_ge(s_msg, 2 * ((i - BODIES) * UNROLL + k) + 2)

            pe.wait_ge(s_zero, 1)
            for b in range(4):
                mm = nc.tensor.matmul(PS[:, 2 + b, 0:AC], zero16, KEY[:, 0, :], start=True, stop=False, skip_group_check=True)
            mm.then_inc(s_zero, 1)

            def count_edges(i, kb):
                b = (i - BODIES) * AUNROLL + kb
                g = small(kb)
                pe.wait_ge(s_ahot, 2 * b + 2)
                if not (isinstance(i, int) and i == BODIES and kb < 2):
                    pe.wait_ge(s_acp, b - 1)
                nc.tensor.matmul(PS[:, bass.ds(((g + 1) & 3) + 2, 1), 0:AC].rearrange("p a c -> p (a c)"), zero16, KEY[:, kb % 4, :],
                                 start=True, stop=False, skip_group_check=True)
                nc.tensor.matmul(PS[:, bass.ds((g & 3) + 2, 1), 0:AC].rearrange("p a c -> p (a c)"), LO[:, kb % 4, :], KEY[:, kb % 4, :],
                                 start=False, stop=False, skip_group_check=True).then_inc(s_amm, 1)
            run_pass(pe, 1, ((0, transpose_onehot(1)), (1, expand_scores),
                             (5, segment_sum(main, AW, lambda k: msg[:, k % 2, :], attention_ready))), loads,
                     ((0, count_edges),), subloads)
            release(pe, regs)
            release(pe, sregs)

            def dense(d, w):
                table = part_table(w)
                pe.wait_ge(s_parts, d + 1)

                def multiply(i, j):
                    pe.wait_ge(s_aload[j], 16 * (d * ((G - 1) // 3 + (j == 0)) + 1) + 16 * i)
                    if not (isinstance(i, int) and i == 0):
                        pe.wait_ge(s_dev, d * G + 3 * i + j - 2)
                    cols = acols[:, j, :].rearrange("p (n h) -> p n h", h=HI)
                    for h in range(HI):
                        mm = nc.tensor.matmul(PS[:, j, 0:3 * w], cols[:, :, h], table[:, h, :, :].rearrange("p k c -> p (k c)"),
                                              start=(h == 0), stop=(h == HI - 1))
                    mm.then_inc(s_dmm, 1)
                dense_groups(pe, multiply)

            def gathered_ready(i, k):
                pe.wait_ge(fall.d, i * UNROLL + k + 1)
                landed(pe, fall, i, k)

            pe.wait_ge(s_flagf, 1)
            nc.tensor.transpose(PS[0:1, 0, 0:P], flag[:, 0:1], ident[:]).then_inc(s_flagf, 1)
            pe.wait_ge(s_flag, 1)
            linear_after = {0: (1, 2, 3), 1: (), 2: (4, 5)}
            for d, w in enumerate((P, HID, HID)):
                choose(pe, d, lambda: dense(d, w),
                       lambda: run_pass(pe, d, ((0, segment_sum(fall, w, lambda k: got[:, k % RING, 0:w], gathered_ready)),)))
                for L in linear_after[d]:
                    linear(L)

            loads, group, regs = group_loader(pe, 2, 1, "pem")

            def transpose_both(i, k):
                g = (i - 2 * BODIES) * UNROLL + k
                pe.wait_ge(s_ef[k % 8], (i - 2 * BODIES) * (16 * UNROLL // 8) + 16 * (k // 8 + 1))
                if not (isinstance(i, int) and i == 2 * BODIES and k < 2):
                    pe.wait_ge(s_fTc, g - 1)
                transpose_onehot(2)(i, k)
                nc.tensor.transpose(PS[0:DE, 2 + k % 2, 0:P], ef[:, k % 8, :], ident[:]).then_inc(s_fT, 1)

            def edge_linear(i, k):
                g = (i - 2 * BODIES) * UNROLL + k
                pe.wait_ge(s_dTc, g + STEPS + 1)
                pe.wait_ge(s_fTc, g + 1)
                if not (isinstance(i, int) and i == 2 * BODIES and k < 2):
                    pe.wait_ge(s_pre, g - 1)
                o = PS[:, 4 + k % 2, 0:P]
                nc.tensor.matmul(o, DT[:, k % 2, :], TB[:, bass.ds(group(k), 1), :].rearrange("p a c -> p (a c)"), start=True, stop=False)
                nc.tensor.matmul(o, efT[:, k % 2, :], wts[0:DE, 13, :], start=False, stop=True).then_inc(s_ex, 1)

            def silu_ready(i, k):
                pe.wait_ge(s_silu, (i - 2 * BODIES) * UNROLL + k + 1)
            run_pass(pe, 2, ((0, transpose_both), (1, edge_linear),
                             (3, segment_sum(main, P, lambda k: silu_out[:, k % 2, :], silu_ready))), loads)
            for L in (6, 7, 8):
                linear(L)

        @block.scalar
        def _(act):
            act.sem_inc(s_linX, 1)
            requests = [0]

            def serve(out_, in_, func, scale=1.0):
                requests[0] += 1
                act.wait_ge(s_areq, requests[0])
                nc.scalar.activation(out_, in_, func, scale=scale).then_inc(s_arep, 1)

            def linear(L):
                tab = LINEARS[L][0]
                act.wait_ge(s_linr, L + 1)
                with act.Fori(L * NL, (L + 1) * NL) as i:
                    act.wait_ge(s_linT, i + 1)
                    nc.scalar.copy(stage, tab[:, bass.ds((i - L * NL) * LIN, LIN), 0:P]).then_inc(s_linw, 1)
                    act.wait_ge(s_linT, i + 2)
                    act.wait_ge(s_linY, i + 1)
                    nc.scalar.copy(xT, lin_in).then_inc(s_linX, 1)

            def norm():
                serve(stat[:, 2, :], stat[:, 1, :], ACT.Sqrt)

            def store_onehotT(banks):
                def fn(i, k):
                    g = (i - BODIES) * UNROLL + k
                    act.wait_ge(s_dT, g + 1)
                    if not (isinstance(i, int) and i == BODIES and k < 2):
                        act.wait_ge(s_ex, g - 1)
                    nc.scalar.copy(DT[:, k % 2, :], PS[:, k % banks, 0:P]).then_inc(s_dTc, 1)
                return fn

            linear(0)

            def diagonals(i, k):
                g = i * UNROLL + k
                landed(act, main, i, k)
                if not at_start(i, k, 2):
                    act.wait_ge(s_max, g - 1)
                for h in range(H):
                    ins = nc.scalar.activation(diag[:, k % 2, h, :], ident[:], ACT.Copy, scale=got[:, k % RING, P + h:P + h + 1])
                ins.then_inc(s_diag, 1)
            act.wait_ge(s_iota, 7)
            run_pass(act, 0, ((0, diagonals),))
            serve(p_self, p_self, ACT.Exp)

            def weights(i, k):
                g = (i - BODIES) * UNROLL + k
                act.wait_ge(s_z, 3 * g + 3)
                if not (isinstance(i, int) and i == BODIES and k < 4):
                    act.wait_ge(s_msg, 2 * (g - 3))
                nc.scalar.activation(p4[:, k % 4, :], z4[:, k % 4, 2, :], ACT.Exp).then_inc(s_p, 1)

            subloads, small, sregs = small_loader(act, 0, "aca")

            def copy_columns(i, kb):
                b = (i - BODIES) * AUNROLL + kb
                g = small(kb)
                if not (isinstance(i, int) and i == BODIES and kb < 1):
                    act.wait_ge(s_acp, b)
                act.wait_ge(s_amm, b + 1)
                if not (isinstance(i, int) and i == BODIES and kb < 6):
                    kd = (kb - 6) % AUNROLL
                    body = i - BODIES - (kb < 6)
                    act.wait_ge(s_adma[kd % 8], body * (16 * AUNROLL // 8) + 16 * (kd // 8 + 1))
                nc.scalar.copy(astage[:, bass.ds((g + 7) & 7, 1), :].rearrange("p a c -> p (a c)"),
                               PS[:, bass.ds(((g + 3) & 3) + 2, 1), 0:AC].rearrange("p a c -> p (a c)")).then_inc(s_acp, 1)
            act.wait_ge(s_gtab, 32)
            act.wait_ge(s_zero, 2)
            run_pass(act, 1, ((0, store_onehotT(1)), (3, weights)), None, ((0, copy_columns),), subloads)
            release(act, sregs)
            serve(TC, TC, ACT.Exp)
            norm()
            serve(dinv[:], dinv[:], ACT.Sqrt)
            linear(1)
            linear(2)
            serve(TA[:, :, 0:P], TA[:, :, 0:P], ACT.Tanh)
            norm()
            linear(3)
            linear(4)
            norm()
            linear(5)

            def store_featuresT(i, k):
                g = (i - 2 * BODIES) * UNROLL + k
                act.wait_ge(s_fT, g + 1)
                act.wait_ge(s_ex, STEPS + g - 1)
                nc.scalar.copy(efT[:, k % 2, :], PS[0:DE, 2 + k % 2, 0:P]).then_inc(s_fTc, 1)

            def silu(i, k):
                g = (i - 2 * BODIES) * UNROLL + k
                act.wait_ge(s_pre, g + 1)
                act.wait_ge(s_seg, STEPS + g - 1)
                nc.scalar.activation(silu_out[:, k % 2, :], pre[:, k % 2, :], ACT.Silu).then_inc(s_silu, 1)
            run_pass(act, 2, ((0, store_onehotT(2)), (0, store_featuresT), (2, silu)))
            for L in (6, 7, 8):
                linear(L)
            serve(TB, TB, ACT.Sigmoid)
            serve(TC, TC, ACT.Tanh)
            norm()
            norm()

        @block.vector
        def _(dve):
            v = nc.vector
            dve.sem_inc(s_linO, 2)
            chain = [0]
            asked = [0]
            linears = [0]

            def link(ins):
                chain[0] += 1
                ins.then_inc(s_chain, 1)
                dve.wait_ge(s_chain, chain[0])

            def ask():
                asked[0] += 1
                dve.sem_inc(s_areq, 1)
                dve.wait_ge(s_arep, asked[0])

            def linear():
                L = linears[0]
                linears[0] += 1
                outs = LINEARS[L][3]
                cols = min(LINEARS[L][2], P)
                dve.sem_inc(s_linr, 1)
                with dve.Fori(L * NL, (L + 1) * NL) as i:
                    dve.wait_ge(s_linY, i + 2)
                    for n, (tab, mode) in enumerate(outs):
                        o = tab[:, bass.ds((i - L * NL) * LIN, LIN), 0:cols]
                        y = lin_o[:, :, n * P:n * P + cols]
                        ins = v.tensor_tensor(o, o, y, ALU.add) if mode == "add" else v.tensor_copy(o, y)
                        ins.then_inc(s_linO, 2 // len(outs))
                dve.wait_ge(s_linO, 2 * (L + 1) * NL + 2)

            def layernorm(Z, scratch):
                link(v.tensor_reduce(stat[:, 0, :], Z, AX.X, ALU.add))
                link(v.tensor_scalar(stat[:, 0, :], stat[:, 0, :], 1.0 / P, None, ALU.mult))
                link(v.tensor_tensor(Z, Z, free(stat[:, 0, :], P), ALU.subtract))
                link(v.tensor_tensor(scratch, Z, Z, ALU.mult))
                link(v.tensor_reduce(stat[:, 1, :], scratch, AX.X, ALU.add))
                link(v.tensor_scalar(stat[:, 1, :], stat[:, 1, :], 1.0 / P, EPS, ALU.mult, ALU.add))
                ask()
                link(v.reciprocal(stat[:, 3, :], stat[:, 2, :]))
                link(v.tensor_tensor(Z, Z, free(stat[:, 3, :], P), ALU.mult))

            def row(n, w=P):
                return across(rows[:, n, 0:w], G)

            def heads(tab):
                return tab.rearrange("p g (h c) -> p g h c", h=H)

            v.memset(X[96:P, FULL:G, :], 0.0).then_inc(s_xpad, 1)
            link(v.memset(ones[:], 1.0))
            link(v.memset(gtab[:], 0))
            link(v.memset(atab[:], 0))
            dve.wait_ge(s_iota, 7)
            for h in range(H):
                link(v.tensor_scalar(nident[:, h, :], ident[:], -BIG, None, ALU.mult))

            dve.wait_ge(s_dst, 32)
            link(v.tensor_copy(first, first_i))
            dve.sem_inc(s_vrow, 1)
            dve.wait_ge(s_bnd, 1)
            for c in range(VCH):
                link(v.tensor_scalar(junk[:, 0:T], PS[:, 0:4, :].rearrange("p b c -> p (b c)")[:, 0:T], vcol[:, 0, c:c + 1], None,
                                     ALU.is_lt, ALU.add, accum_out=vcol[:, 1, c:c + 1]))
                link(v.tensor_scalar(dg[:, c, :], ident[:], vcol[:, 1, c:c + 1], None, ALU.mult))
            dve.sem_inc(s_vrow, 1)
            dve.wait_ge(s_bnd, 2)
            link(v.tensor_scalar(trow, PS[:, 4:6, :].rearrange("p b c -> p (b c)")[:, 0:VCH * P], -1.0, 0.0, ALU.add, ALU.max))
            SP_ = P // SUB
            link(v.tensor_tensor(pos[:, 0:NB].unsqueeze(2), trow[:, 0:NB * SP_].rearrange("p (g s) -> p g s", s=SP_)[:, :, SP_ - 1:SP_],
                                 srow[:, 0:NB].unsqueeze(2), ALU.add))
            cmp3 = cmp[:, 0:CH * NB].rearrange("p (c b) -> p c b", c=CH)
            link(v.tensor_tensor(cmp3, free(sidx[:, 0, 0:CH], NB), across(pos[:, 0:NB], CH), ALU.is_ge))
            link(v.tensor_reduce(sidx[:, 1, 0:CH], cmp3, AX.X, ALU.add))
            link(v.tensor_tensor(sidx[:, 2, 0:CH], sidx[:, 0, 0:CH], sidx[:, 1, 0:CH], ALU.subtract))
            link(v.tensor_scalar(sidx[:, 3, 0:CH], sidx[:, 2, 0:CH], float(P), float(LAST), ALU.mult, ALU.min))
            link(v.tensor_scalar(sidx[:, 4, 0:CH], sidx[:, 1, 0:CH], float(P), None, ALU.mult))
            v.tensor_copy(tile_i[:, 0, :], sidx[:, 1, 0:CH]).then_inc(s_tix, 1)
            v.tensor_copy(tile_i[:, 1, :], sidx[:, 2, 0:CH]).then_inc(s_tix, 1)
            v.tensor_copy(tile_i[:, 2, :], sidx[:, 3, 0:CH]).then_inc(s_tix, 1)
            link(v.tensor_tensor(pos[:, 0:SG], trow[:, 0:SG], srow[:, 0:SG], ALU.add))
            for c in range(ACH):
                link(v.tensor_scalar(junk[:, 0:SG], pos[:, 0:SG], atile[:, 0, c:c + 1], None, ALU.is_le, ALU.add, accum_out=atile[:, 1, c:c + 1]))
            link(v.tensor_tensor(atile[:, 2, :], atile[:, 0, :], atile[:, 1, :], ALU.subtract))
            link(v.tensor_scalar(atile[:, 2, :], atile[:, 2, :], float(TP - 1), None, ALU.min))
            link(v.tensor_scalar(atile[:, 3, :], atile[:, 1, :], float(SUB), None, ALU.mult))
            v.tensor_copy(atile_i[:], atile[:, 2, :]).then_inc(s_atix, 1)
            v.tensor_copy(ag16[:], atile[:, 1, :]).then_inc(s_atix, 1)

            def tile_columns(first_c, chunks, convert, outs):
                lo, hi = 2 * first_c, 2 * (first_c + chunks)
                for n in range(lo, hi + 2):
                    if n < hi:
                        cc, f = n // 2, n % 2
                        dve.wait_ge(s_trow[2 * (cc % 2) + f], 16 * (cc // 2 + 1))
                        if n >= 4:
                            dve.wait_ge(s_tt, n - 3)
                        convert(cc - first_c, cc % 2, f).then_inc(s_tf, 1)
                    if n >= lo + 2:
                        m = n - 2
                        dve.wait_ge(s_tt, m + 1)
                        at = (m - lo) // 2 * P
                        v.tensor_copy(outs[m % 2][:, at:at + P], PS[:, 2 + m % 2, 0:P]).then_inc(s_tc, 1)
                dve.wait_ge(s_tc, hi)

            def local_or_source(c, b, f):
                if f == 0:
                    return v.tensor_scalar(tile_f[:, b, 0, :], tile_rows[:, b, 0, :], sidx[:, 4, c:c + 1], None, ALU.subtract)
                return v.tensor_copy(tile_f[:, b, 1, :], tile_rows[:, b, 1, :])
            tile_columns(0, CH, local_or_source, (dloc, srcs))

            def onehot(S, p):
                def fn(i, k):
                    g = i * UNROLL + k
                    if S is main and p == 0:
                        if not at_start(i, k, 8):
                            dve.wait_ge(s_max, g - 7)
                    elif S is main:
                        if not (isinstance(i, int) and i == BODIES and k < 8):
                            dve.wait_ge(S.seg, g - STEPS - 7)
                    elif not at_start(i, k, 8):
                        dve.wait_ge(S.seg, g - 7)
                    v.tensor_scalar(D[:, k % 8, :], iota[:], dloc[:, bass.ds((i - p * BODIES) * UNROLL + k, 1)], None, ALU.is_equal).then_inc(S.d, 1)
                return fn

            dve.wait_ge(s_x, 32)
            dve.wait_ge(s_in, 16 * NW)
            linear()
            for n, o in ((1, node_as[:]), (2, node_ad[:, :, 0:H])):
                link(v.tensor_tensor(TC, TA[:, :, 0:P], row(n), ALU.mult))
                link(v.tensor_reduce(o, heads(TC), AX.X, ALU.add))
            link(v.tensor_copy(TA[:, :, P:XW], node_as[:]))
            link(v.tensor_copy(node_max[:], node_as[:]))
            dve.sem_inc(s_tabr, 1)

            dve.wait_ge(s_gtab, 32)
            loads, group, regs = group_loader(dve, 0, 2, "dvg")

            def not_onehot(i, k):
                if not at_start(i, k, 4):
                    dve.wait_ge(s_max, i * UNROLL + k - 3)
                v.tensor_scalar(ND[:, k % 4, :], iota[:], dloc[:, bass.ds(i * UNROLL + k, 1)], None, ALU.not_equal).then_inc(s_d2, 1)

            def tile_max(i, k):
                g = i * UNROLL + k
                dve.wait_ge(s_max, g + 1)
                if not at_start(i, k, 2):
                    dve.wait_ge(s_done, g - 1)
                v.tensor_reduce(m4[:, k % 2, :], PS[:, 4 + k % 2, :].rearrange("p (h e) -> p h e", h=H), AX.X, ALU.max).then_inc(s_red, 1)
                dve.wait_ge(s_red, g + 1)
                if not at_start(i, k, 1):
                    dve.wait_ge(s_done, g)
                m = node_max[:, bass.ds(group(k), 1), :].rearrange("p a c -> p (a c)")
                v.tensor_tensor(m, m, m4[:, k % 2, :], ALU.max).then_inc(s_done, 1)
            run_pass(dve, 0, ((0, not_onehot), (0, onehot(main, 0)), (2, tile_max)), loads)
            release(dve, regs)
            dve.wait_ge(s_done, STEPS)

            link(v.tensor_tensor(s0, node_ad[:, :, 0:H], node_max[:], ALU.add))
            link(v.scalar_tensor_tensor(out=node_ad[:, :, H:2 * H], in0=s0, scalar=SLOPE, in1=s0, op0=ALU.mult, op1=ALU.max))
            link(v.tensor_tensor(s0, node_as[:], node_ad[:, :, 0:H], ALU.add))
            link(v.scalar_tensor_tensor(out=p_self, in0=s0, scalar=SLOPE, in1=s0, op0=ALU.mult, op1=ALU.max))
            link(v.tensor_tensor(p_self, p_self, node_ad[:, :, H:2 * H], ALU.subtract))
            ask()
            link(v.memset(ACC[:], 0.0))
            link(v.tensor_copy(ACC[:, :, P:P + H], p_self))
            for h in range(H):
                link(v.tensor_tensor(ACC[:, :, h * C:(h + 1) * C], TA[:, :, h * C:(h + 1) * C], p_self[:, :, h:h + 1].to_broadcast([P, G, C]), ALU.mult))
            link(v.memset(msg[:], 1.0))

            def column_or_place(c, b, f):
                if f == 0:
                    return v.tensor_scalar(tile_f[:, b, 0, :], tile_rows[:, b, 0, :], atile[:, 3, c:c + 1], None, ALU.subtract)
                return v.tensor_copy(tile_f[:, b, 1, :], tile_rows[:, b, 1, :])
            tile_columns(CH, ACH, column_or_place, (akey, alo))
            src_i = region[:, 0:ACH * P].bitcast(I32)
            blk_i = region[:, ACH * P:2 * ACH * P].bitcast(I32)
            link(v.tensor_copy(src_i, alo))
            link(v.tensor_scalar(blk_i, src_i, 7, None, ALU.arith_shift_right))
            link(v.tensor_scalar(src_i, src_i, P - 1, None, ALU.bitwise_and))
            link(v.tensor_copy(alo, src_i))
            link(v.scalar_tensor_tensor(out=akey, in0=akey, scalar=float(HI), in1=blk_i, op0=ALU.mult, op1=ALU.add))
            link(v.memset(KEY, 0.0))
            link(v.memset(zero16, 0.0))
            dve.sem_inc(s_zero, 1)
            dve.wait_ge(s_zero, 2)

            def add_sums(S, w, group):
                def fn(i, k):
                    g = i * UNROLL + k
                    dve.wait_ge(S.seg, g + 1 - (STEPS if S is main else 0))
                    if not at_start(i, k, 1):
                        dve.wait_ge(S.done, g)
                    a = ACC[:, bass.ds(group(k), 1), 0:w].rearrange("p a c -> p (a c)")
                    v.tensor_tensor(a, a, sums_bank(k, w), ALU.add).then_inc(S.done, 1)
                return fn
            loads, group, regs = group_loader(dve, 1, 6, "dva")

            def logits(i, k):
                g = (i - BODIES) * UNROLL + k
                dve.wait_ge(s_ex, g + 1)
                landed(dve, main, i, k)
                if not (isinstance(i, int) and i == BODIES and k < 4):
                    dve.wait_ge(s_p, g - 3)
                z, a = z4[:, k % 4], PS[:, 1, 0:2 * H]
                v.tensor_tensor(z[:, 0, :], got[:, k % RING, P:P + H], a[:, 0:H], ALU.add).then_inc(s_z, 1)
                dve.wait_ge(s_z, 3 * g + 1)
                v.scalar_tensor_tensor(out=z[:, 1, :], in0=z[:, 0, :], scalar=SLOPE, in1=z[:, 0, :], op0=ALU.mult, op1=ALU.max).then_inc(s_z, 1)
                dve.wait_ge(s_z, 3 * g + 2)
                v.tensor_tensor(z[:, 2, :], z[:, 1, :], a[:, H:2 * H], ALU.subtract).then_inc(s_z, 1)

            def messages(i, k):
                g = (i - BODIES) * UNROLL + k
                dve.wait_ge(s_p, g + 1)
                if not (isinstance(i, int) and i == BODIES and k < 2):
                    dve.wait_ge(s_seg, g - 1)
                o = msg[:, k % 2, :]
                p = p4[:, k % 4, :]
                v.scalar_tensor_tensor(out=o[:, 0:P].rearrange("p (h c) -> p h c", h=H), in0=free(p, C), scalar=1.0,
                                       in1=got[:, k % RING, 0:P].rearrange("p (h c) -> p h c", h=H), op0=ALU.min, op1=ALU.mult).then_inc(s_msg, 1)
                v.tensor_scalar(o[:, P:P + H], p, 1.0, None, ALU.min).then_inc(s_msg, 1)

            def adjacency_onehots(i, kb):
                b = (i - BODIES) * AUNROLL + kb
                if not (isinstance(i, int) and i == BODIES and kb < 4):
                    dve.wait_ge(s_amm, b - 3)
                v.tensor_scalar(LO[:, kb % 4, :], iota16[:, 0:P], alo[:, bass.ds(b, 1)], None, ALU.is_equal).then_inc(s_ahot, 1)
                v.tensor_scalar(KEY[:, kb % 4, :], iota16[:], akey[:, bass.ds(b, 1)], None, ALU.is_equal).then_inc(s_ahot, 1)
            run_pass(dve, 1, ((0, onehot(main, 1)), (2, logits), (4, messages), (6, add_sums(main, AW, group))), loads,
                     ((0, adjacency_onehots),))
            release(dve, regs)
            dve.wait_ge(s_done, 2 * STEPS)
            dve.wait_ge(s_acp, ASTEPS)
            dve.wait_ge(s_amm, ASTEPS)

            sums = ACC[:, :, 0:P]
            link(v.tensor_scalar(ACC[:, :, P:P + H], ACC[:, :, P:P + H], 1e-16, None, ALU.add))
            link(v.reciprocal(ACC[:, :, P:P + H], ACC[:, :, P:P + H]))
            for h in range(H):
                link(v.tensor_tensor(TC[:, :, h * C:(h + 1) * C], ACC[:, :, h * C:(h + 1) * C], ACC[:, :, P + h:P + h + 1].to_broadcast([P, G, C]), ALU.mult))
            link(v.tensor_tensor(TC, TC, row(0), ALU.add))
            link(v.tensor_tensor(TB, TB, TC, ALU.add))
            link(v.tensor_scalar(TC, TB, 0.0, None, ALU.min))
            ask()
            link(v.tensor_scalar(TC, TC, -1.0, None, ALU.add))
            link(v.scalar_tensor_tensor(out=TC, in0=TB, scalar=0.0, in1=TC, op0=ALU.max, op1=ALU.add))
            link(v.tensor_tensor(X[:], X[:], TC, ALU.add))
            layernorm(X[:], TC)
            dve.sem_inc(s_tabr, 1)
            link(v.tensor_copy(count[:], ACC[:, :, P + H:AW].rearrange("p g a -> p (g a)")))
            link(v.tensor_scalar(rcount[:], count[:], 1.0, None, ALU.max))
            link(v.reciprocal(rcount[:], rcount[:]))
            link(v.tensor_scalar(dinv[:], count[:], 1.0, None, ALU.add))
            ask()
            link(v.reciprocal(dinv[:], dinv[:]))
            link(v.tensor_reduce(flag[:, 0:1], count[:], AX.X, ALU.max))
            dve.sem_inc(s_flagf, 1)
            dve.wait_ge(s_flagf, 2)
            link(v.tensor_reduce(flag[0:1, 1:2], PS[0:1, 0, 0:P], AX.X, ALU.max))
            link(v.tensor_copy(flag_i[:], flag[0:1, 1:2]))
            dve.sem_inc(s_flag, 1)

            def neighbour_sums(d, V, w):
                def general():
                    link(v.memset(ACC[:, :, 0:w], 0.0))
                    loads, group, regs = group_loader(dve, d, 2, f"dv{d}_")
                    run_pass(dve, d, ((0, onehot(fall, d)), (2, add_sums(fall, w, group))), loads)
                    release(dve, regs)
                    dve.wait_ge(fall.done, (d + 1) * STEPS)

                def dense():
                    t, rest = part_table(w), ACC[:, :, 0:w]
                    link(v.tensor_copy(t[:, :, 0, :], V))
                    link(v.tensor_tensor(rest, V, t[:, :, 0, :], ALU.subtract))
                    link(v.tensor_copy(t[:, :, 1, :], rest))
                    link(v.tensor_tensor(rest, rest, t[:, :, 1, :], ALU.subtract))
                    link(v.tensor_copy(t[:, :, 2, :], rest))
                    dve.sem_inc(s_parts, 1)

                    def store(i, j):
                        dve.wait_ge(s_dmm, d * G + 3 * i + j + 1)
                        v.tensor_reduce(ACC[:, bass.ds(3 * i + j, 1), 0:w].rearrange("p a c -> p (a c)"),
                                        PS[:, j, 0:3 * w].rearrange("p (k c) -> p c k", k=3), AX.X, ALU.add).then_inc(s_dev, 1)
                    dense_groups(dve, store)
                    dve.wait_ge(s_dev, (d + 1) * G)

                start = chain[0]
                most = dve.alloc_register(f"most_edges{d}")
                dve.load([most], flag_i[0:1, 0:1])
                with dve.If(dve.snap(most, min_val=0, max_val=1 << 24) > FINE):
                    general()
                    dve.sem_inc(s_chain, 5 - (chain[0] - start))
                chain[0] = start
                with dve.Else():
                    dense()
                dve.free_register(most)

            neighbour_sums(0, X[:], P)
            link(v.tensor_tensor(TC, sums, free(rcount[:], P), ALU.mult))
            linear()
            linear()
            ta = TA[:, :, 0:P]
            link(v.tensor_tensor(ta, ta, row(3), ALU.add))
            ask()
            link(v.tensor_tensor(X[:], X[:], ta, ALU.add))
            layernorm(X[:], TC)

            linear()
            hid = ACC[:, :, 0:HID]
            link(v.tensor_tensor(Y, TA[:, :, 0:HID], free(dinv[:], HID), ALU.mult))
            dve.sem_inc(s_tabr, 1)
            neighbour_sums(1, Y, HID)
            dve.wait_ge(s_tabw, 16 * 3)
            link(v.tensor_tensor(Y, hid, Y, ALU.add))
            link(v.tensor_tensor(Y, Y, free(dinv[:], HID), ALU.mult))
            link(v.tensor_tensor(Y, Y, row(4, HID), ALU.add))
            link(v.tensor_tensor(Y, Y, free(dinv[:], HID), ALU.mult))
            dve.sem_inc(s_tabr, 1)
            neighbour_sums(2, Y, HID)
            dve.wait_ge(s_tabw, 16 * 4)
            link(v.tensor_tensor(hid, hid, Y, ALU.add))
            link(v.memset(TC, 0.0))
            link(v.memset(wts[HID:2 * HID, 5, :], 0.0))
            link(v.memset(wts[2 * HID:P, 5, :], 0.0))
            link(v.tensor_tensor(TC[:, :, 0:HID], hid, free(dinv[:], HID), ALU.mult))
            linear()
            link(v.tensor_tensor(ta, ta, row(5), ALU.add))
            link(v.scalar_tensor_tensor(out=X[:], in0=ta, scalar=0.0, in1=X[:], op0=ALU.max, op1=ALU.add))
            layernorm(X[:], TC)

            linear()
            dve.sem_inc(s_tabr, 1)
            link(v.tensor_tensor(TB, TB, row(6), ALU.add))
            link(v.memset(ACC[:], 0.0))
            loads, group, regs = group_loader(dve, 2, 4, "dvm")

            def preactivation(i, k):
                g = (i - 2 * BODIES) * UNROLL + k
                dve.wait_ge(s_ex, STEPS + g + 1)
                landed(dve, main, i, k)
                if not (isinstance(i, int) and i == 2 * BODIES and k < 2):
                    dve.wait_ge(s_silu, g - 1)
                v.tensor_tensor(pre[:, k % 2, :], got[:, k % RING, 0:P], PS[:, 4 + k % 2, 0:P], ALU.add).then_inc(s_pre, 1)
            run_pass(dve, 2, ((0, onehot(main, 2)), (2, preactivation), (4, add_sums(main, P, group))), loads)
            dve.wait_ge(s_done, 3 * STEPS)
            link(v.tensor_copy(TC, sums))
            dve.wait_ge(s_tabw, 16 * 5)
            linear()
            link(v.tensor_tensor(TC, free(count[:], P), row(7), ALU.mult))
            link(v.tensor_tensor(ta, ta, TC, ALU.add))
            link(v.tensor_tensor(ta, ta, free(rcount[:], P), ALU.mult))
            linear()
            linear()
            link(v.tensor_tensor(TB, TB, row(8), ALU.add))
            ask()
            link(v.tensor_tensor(TC, TC, row(9), ALU.add))
            ask()
            link(v.tensor_tensor(ta, X[:], TC, ALU.subtract))
            link(v.tensor_tensor(ta, ta, TB, ALU.mult))
            link(v.tensor_tensor(TC, TC, ta, ALU.add))
            layernorm(TC, TB)
            link(v.tensor_tensor(TC, TC, row(10), ALU.mult))
            link(v.tensor_tensor(TC, TC, row(11), ALU.add))
            link(v.tensor_tensor(X[:], X[:], TC, ALU.add))
            layernorm(X[:], TC)
            dve.sem_inc(s_tabr, 1)


_NAMES = {"x": "x", "src": "src", "dst": "dst", "edge_attr_64": "edge_attr_64",
          "att_src": "L0_gnn_att_src", "att_dst": "L0_gnn_att_dst", "L0_bias": "L0_gnn_bias",
          "L1_b": "L1_gnn_b_l", "L2_W1": "L2_gnn_W1", "L2_b1": "L2_gnn_b1", "L2_W2": "L2_gnn_W2", "L2_b2": "L2_gnn_b2",
          "L3_W1": "L3_gnn_W1", "L3_b1": "L3_gnn_b1", "L3_W2": "L3_gnn_W2", "L3_b2": "L3_gnn_b2",
          "L3_Wg": "L3_gnn_Wg", "L3_bg": "L3_gnn_bg", "L3_Wt": "L3_gnn_Wt", "L3_bt": "L3_gnn_bt",
          "gamma": "L3_gnn_gamma", "beta": "L3_gnn_beta"}
_TRANSPOSED = {"gatT": "L0_gnn_W_gat", "skipT": "L0_gnn_W_skip", "WlT": "L1_gnn_W_l", "WrT": "L1_gnn_W_r"}


def kernel(**inputs):
    import numpy as np
    import concourse.bacc as bacc
    from concourse.bass_utils import run_bass_kernel_spmd

    nc = bacc.Bacc("TRN2", target_bir_lowering=False, num_devices=1)
    arrays, A = {}, {}
    for short, name in _NAMES.items():
        arrays[f"in_{short}"] = np.ascontiguousarray(inputs[name])
    for short, name in _TRANSPOSED.items():
        arrays[f"in_{short}"] = np.ascontiguousarray(np.asarray(inputs[name]).T)
    for key, a in arrays.items():
        A[key[3:]] = nc.dram_tensor(key, a.shape, mybir.dt.from_np(a.dtype), kind="ExternalInput").ap()
    out = nc.dram_tensor("out_x", A["x"].shape, F32, kind="ExternalOutput").ap()
    gnn(nc, A, out)
    r = run_bass_kernel_spmd(nc, [arrays], core_ids=[0])
    return r.results[0]["out_x"]
```

```python
from contextlib import ExitStack

import concourse.bass as bass
from concourse import mybir

ALU = mybir.AluOpType
ACT = mybir.ActivationFunctionType
AX = mybir.AxisListType
F32 = mybir.dt.float32
BF16 = mybir.dt.bfloat16
I32 = mybir.dt.int32

P = 128
EPS = 1e-5
BIG = float(2.0 ** 100)
SLOPE = 0.2
NO_NODE = 20000
UNROLL = 32
RING = 16
DRING = 16
BATCH = 4
QUARTER = 8
SUB = 8
ABODY = (16, 32)
FINE = 256
LIN = 7
XW = 132
AW = 133


def gnn(nc, A, out):
    N, DF = A["x"].shape
    E = A["src"].shape[0]
    DE = A["edge_attr_64"].shape[1]
    H, C = A["att_src"].shape
    HID = A["L2_W1"].shape[1]
    G = -(-N // P)
    T = -(-E // P)
    FULL = N // P
    TAIL = N - FULL * P
    STEPS = -(-(T + G - 1) // UNROLL) * UNROLL
    BODIES = STEPS // UNROLL
    CH = STEPS // P
    HI = G
    AC = SUB * HI
    SG = G * P // SUB
    ASTEPS = BODIES * sum(ABODY)
    ACH = -(-ASTEPS // P)
    VCH = -(-SG // P)
    TP = STEPS - (G - 1)
    LAST = E - P
    OVER = T * P - E
    NB = G - 1
    assert DF == P and G % LIN == 0 and STEPS % P == 0 and TP >= T and OVER > 0
    assert AC <= 512 and ASTEPS >= T + SG + 1 and (G - 1) % 3 == 0 and T <= 2048

    def dram(name, shape, dt):
        return nc.dram_tensor(name, shape, dt).ap()

    dst_pad = dram("dst_pad", [TP, P], I32)
    src_pad = dram("src_pad", [TP, P], I32)
    src_steps = dram("src_steps", [P, STEPS], I32)
    group_steps = dram("group_steps", [1, STEPS], I32)
    asteps = dram("asteps", [1, ACH * P], mybir.dt.int16)
    base_steps = dram("base_steps", [1, STEPS], I32)
    adj = dram("adj", [P, SG + 1, AC], BF16)
    tab_proj = dram("tab_proj", [G * P, XW], F32)
    tab_x = dram("tab_x", [G * P, P], F32)
    tab_y1 = dram("tab_y1", [G * P, HID], F32)
    tab_y2 = dram("tab_y2", [G * P, HID], F32)
    tab_ps = dram("tab_ps", [G * P, P], F32)

    with ExitStack() as ctx:
        def sb(name, shape, dt=F32):
            return ctx.enter_context(nc.sbuf_tensor(name, shape, dt))

        def sem(name):
            return ctx.enter_context(nc.semaphore(name))

        X = sb("X", [P, G, P])
        ACC = sb("ACC", [P, G, AW])
        region = sb("region", [P, G * (XW + 2 * P)])
        TA = region[:, 0:G * XW].rearrange("p (g c) -> p g c", g=G)
        TB = region[:, G * XW:G * (XW + P)].rearrange("p (g c) -> p g c", g=G)
        TC = region[:, G * (XW + P):].rearrange("p (g c) -> p g c", g=G)
        region16 = region[:].bitcast(BF16)
        parts = region16[:, 0:G * 3 * P]
        acols = region16[:, G * 3 * P:G * 3 * P + 3 * P // SUB * AC].rearrange("p (b c) -> p b c", b=3)
        node_ad = sb("node_ad", [P, G, 2 * H])
        node_as = sb("node_as", [P, G, H])
        node_max = sb("node_max", [P, G, H])
        stat = sb("stat", [P, 4, G])
        count = sb("count", [P, G])
        rcount = sb("rcount", [P, G])
        dinv = sb("dinv", [P, G])
        dloc = sb("dloc", [P, STEPS])
        srcs = sb("srcs", [P, STEPS], I32)
        gtab = sb("gtab", [1, 16 + STEPS + UNROLL], I32)
        atab = sb("atab", [1, 16 + ACH * P + 32], mybir.dt.int16)
        iota = sb("iota", [P, P])
        ident = sb("ident", [P, P])
        nident = sb("nident", [P, H, P], BF16)
        iota16 = sb("iota16", [P, AC], mybir.dt.float16)
        flag = sb("flag", [P, 2])
        flag_i = sb("flag_i", [1, 1], I32)
        ones = sb("ones", [P, P])
        wts = sb("wts", [P, 14, P])
        rows = sb("rows", [P, 12, P])
        fill = sb("fill", [8, 2, P], I32)
        astage = sb("astage", [P, 8, AC], BF16)
        setup = ACC[:].rearrange("p g a -> p (g a)")
        trow = setup[:, 0:VCH * P]
        pos = setup[:, VCH * P:2 * VCH * P]
        cmp = setup[:, 2 * VCH * P:3 * VCH * P]
        dg = setup[:, 3 * VCH * P:4 * VCH * P].rearrange("p (c v) -> p c v", c=VCH)
        first_i = setup[0:1, 4 * VCH * P:4 * VCH * P + T].bitcast(I32)
        first = setup[0:1, 0:T]
        vcol = sb("vcol", [P, 2, VCH])
        sidx = sb("sidx", [P, 5, CH])
        tile_i = sb("tile_i", [P, 3, CH], I32)
        atile = sb("atile", [P, 4, ACH])
        atile_i = sb("atile_i", [P, ACH], I32)
        tile_rows = sb("tile_rows", [P, 2, 2, P], I32)
        tile_f = sb("tile_f", [P, 2, 2, P])
        alo = TC.rearrange("p g c -> p (g c)")[:, 0:ACH * P]
        akey = TC.rearrange("p g c -> p (g c)")[:, ACH * P:2 * ACH * P]
        LO, KEY = [], []
        for room in (ACC[:].rearrange("p g a -> p (g a)").bitcast(BF16), region16):
            LO.append(room[:, 0:4 * P].rearrange("p (k c) -> p k c", k=4))
            KEY.append(room[:, 4 * P:4 * P + 4 * AC].rearrange("p (k c) -> p k c", k=4))
        zero16 = sb("zero16", [P, P], BF16)
        idx = sb("idx", [P, UNROLL], I32)
        got = sb("got", [P, RING, XW])
        D = sb("D", [P, DRING, P])
        DT = tile_f[:].rearrange("p a b c -> p (a b) c")
        diag = setup[:, 2048:2048 + 4 * H * P].rearrange("p (k h e) -> p k h e", k=4, h=H)
        ND = setup[:, 4096:4096 + 8 * P // 2].bitcast(BF16).rearrange("p (k c) -> p k c", k=8)
        m4 = sb("m4", [P, 4, H])
        z4 = sb("z4", [P, 2, 3, BATCH, H])
        p4 = sb("p4", [P, 2, BATCH, H])
        msg = sb("msg", [P, 4, AW])
        ef = sb("ef", [P, 8, DE])
        efT = sb("efT", [DE, 2, P])
        pre = sb("pre", [P, 2, P])
        silu_out = sb("silu_out", [P, 2, P])
        tc = TC.rearrange("p g c -> p (g c)")
        Y = TB.rearrange("p g c -> p (g c)")[:, 0:G * HID].rearrange("p (g c) -> p g c", g=G)
        s0 = tc[:, 2 * ACH * P:2 * ACH * P + G * H].rearrange("p (g h) -> p g h", g=G)
        p_self = tc[:, 2 * ACH * P + G * H:2 * ACH * P + 2 * G * H].rearrange("p (g h) -> p g h", g=G)
        flat = got[:].rearrange("p r w -> p (r w)")
        stage = flat[:, 0:LIN * P].rearrange("p (j c) -> p j c", j=LIN)
        xT = flat[:, LIN * P:2 * LIN * P].rearrange("p (j c) -> p j c", j=LIN)

        PS = ctx.enter_context(nc.psum_tensor("PS", [P, 8, 512], F32))
        ps_flat = PS[:].rearrange("p b c -> p (b c)")
        lin_in = ps_flat[:, 0:LIN * P].rearrange("p (j c) -> p j c", j=LIN)
        lin_o = ps_flat[:, 1024:1024 + LIN * 2 * P].rearrange("p (j c) -> p j c", j=LIN)

        s_in = sem("inputs_landed")
        s_x = sem("x_landed")
        s_xpad = sem("x_pad_zeroed")
        s_fill = sem("fill_ready")
        s_pad1 = sem("pad_rows_written")
        s_pad = sem("pad_lists_written")
        s_dst = sem("dst_landed")
        s_iota = sem("iotas_ready")
        s_bnd = sem("bounds_summed")
        s_tix = sem("tile_indices_ready")
        s_trow = [sem(f"tile_rows_landed{i}") for i in range(4)]
        s_tf = sem("tile_rows_converted")
        s_tt = sem("tile_rows_transposed")
        s_tc = sem("step_columns_stored")
        s_steps = sem("step_tables_written")
        s_gtab = sem("step_registers_landed")
        s_chain = sem("dve_chain")
        s_pool = sem("pool_chain")
        s_slot = sem("gather_slot_free")
        s_linr = sem("linear_input_ready")
        s_linw = sem("linear_staged")
        s_linT = sem("linear_transposed")
        s_linX = sem("linear_xT_ready")
        s_linY = sem("linear_product_ready")
        s_linO = sem("linear_stored")
        s_areq = sem("act_request")
        s_arep = sem("act_reply")
        s_tabr = sem("table_ready")
        s_tabw = sem("table_written")
        s_vrow = sem("boundary_rows")
        s_atix = sem("adjacency_indices_ready")
        s_ahot = sem("adjacency_onehots_ready")
        s_amm = sem("adjacency_counts_added")
        s_acp = sem("adjacency_columns_copied")
        s_adma = [sem(f"adjacency_columns_written{i}") for i in range(8)]
        s_aload = [sem(f"adjacency_landed{i}") for i in range(3)]
        s_parts = sem("parts_ready")
        s_dmm = sem("dense_sums_ready")
        s_dev = sem("dense_sums_stored")
        s_flag = sem("path_flag_ready")
        s_flagf = sem("most_edges_turned")
        s_zero = sem("banks_zeroed")
        s_cols = sem("columns_seen")

        class Pass:
            def __init__(self, name):
                self.idx = [sem(f"{name}_indices_landed{i}") for i in range(UNROLL // QUARTER)]
                self.got = [sem(f"{name}_gathered{i}") for i in range(RING)]
                self.d = sem(f"{name}_onehot_ready")
                self.seg = sem(f"{name}_segment_sums_ready")
                self.done = sem(f"{name}_step_done")

        main, fall = Pass("edge"), Pass("fallback")
        s_d, s_seg, s_done = main.d, main.seg, main.done
        s_d2 = sem("not_onehot_ready")
        s_diag = sem("diag_ready")
        s_max = sem("masked_scores_ready")
        s_red = sem("tile_max_ready")
        s_dT = sem("onehot_transposed")
        s_dTc = sem("onehotT_stored")
        s_ex = sem("expanded")
        s_z = sem("logit_step")
        s_p = sem("weights_ready")
        s_msg = sem("messages_ready")
        s_ef = [sem(f"edge_features_landed{i}") for i in range(8)]
        s_fT = sem("edge_features_transposed")
        s_fTc = sem("edge_featuresT_stored")
        s_pre = sem("preactivation_ready")
        s_silu = sem("silu_ready")
        s_out = sem("output_written")
        block = ctx.enter_context(nc.Block())

        NW = 14 + 12
        x_in = A["x"]
        srow = setup[:, 4 * VCH * P + T:5 * VCH * P + T]
        junk = region16[:, 0:2048]
        ag16 = sb("ag16", [P, ACH], mybir.dt.int16)
        BATCHES = STEPS // BATCH
        IN_BODY = UNROLL // BATCH

        def free(ap, w):
            return ap.unsqueeze(2).to_broadcast([P, ap.shape[1], w])

        def across(ap, n):
            return ap.unsqueeze(1).to_broadcast([P, n, ap.shape[1]])

        def part_table(w):
            return parts[:, 0:G * 3 * w].rearrange("p (g k c) -> p g k c", g=G, k=3)

        def at_start(i, k, n):
            return isinstance(i, int) and i == 0 and k < n

        def opens(p, i, k, n):
            return isinstance(i, int) and i == p * BODIES and k < n

        def adjacency_step(p, i, kb):
            return p * BODIES * ABODY[0] + (i - p * BODIES) * ABODY[p] + kb

        def dense_groups(eng, group):
            for j in range(3):
                group(0, j)
            with eng.Fori(1, (G - 1) // 3) as i:
                for j in range(3):
                    group(i, j)
            group((G - 1) // 3, 0)

        def choose(eng, d, dense, general):
            reg = eng.alloc_register(f"most_edges{d}")
            eng.load([reg], flag_i[0:1, 0:1])
            most = eng.snap(reg, min_val=0, max_val=1 << 24)
            with eng.If(most > FINE):
                general()
            with eng.Else():
                dense()
            eng.free_register(reg)

        @block.sync
        def _(sp):
            sp.wait_ge(s_xpad, 1)
            with nc.allow_non_contiguous_dma(reason="the first edge of each tile"):
                sp.dma_start(first_i[:, 0:T - 1].unsqueeze(2), A["dst"][0:(T - 1) * P].rearrange("(a t p) -> a t p", a=1, p=P)[:, :, 0:1]).then_inc(s_dst, 16)
                sp.dma_start(first_i[:, T - 1:T], A["dst"][(T - 1) * P:(T - 1) * P + 1].unsqueeze(0)).then_inc(s_dst, 16)
            sp.wait_ge(s_fill, 2)
            for pad, lst, f in ((dst_pad, A["dst"], 0), (src_pad, A["src"], 1)):
                pf = pad.rearrange("t p -> (t p)")
                body = (T - 1) * P
                sp.dma_start(pf[0:body].rearrange("(a b) -> a b", b=P), lst[0:body].rearrange("(a b) -> a b", b=P)).then_inc(s_pad, 16)
                sp.dma_start(pad[T - 1:TP, :], fill[0:TP - T + 1, f, :]).then_inc(s_pad1, 16)
            sp.wait_ge(s_pad1, 32)
            for pad, lst in ((dst_pad, A["dst"]), (src_pad, A["src"])):
                sp.dma_start(pad[T - 1:T, OVER:P], lst[(T - 1) * P:E].unsqueeze(0)).then_inc(s_pad, 16)
            sp.dma_start(X[:, 0:FULL, :], x_in[0:FULL * P].rearrange("(g p) f -> p g f", p=P)).then_inc(s_x, 16)
            sp.dma_start(X[0:TAIL, FULL:G, :], x_in[FULL * P:N].unsqueeze(1)).then_inc(s_x, 16)
            for n, w in enumerate(("gatT", "skipT", "WlT", "WrT")):
                sp.dma_start(wts[:, n, :], A[w]).then_inc(s_in, 16)
            sp.dma_start(wts[:, 4, 0:HID], A["L2_W1"]).then_inc(s_in, 16)
            sp.dma_start(wts[0:HID, 5, :], A["L2_W2"]).then_inc(s_in, 16)
            sp.dma_start(wts[:, 6, :], A["L3_W1"][0:P]).then_inc(s_in, 16)
            sp.dma_start(wts[:, 7, :], A["L3_W1"][P:2 * P]).then_inc(s_in, 16)
            sp.dma_start(wts[:, 8, :], A["L3_W2"]).then_inc(s_in, 16)
            sp.dma_start(wts[:, 9, :], A["L3_Wg"][0:P]).then_inc(s_in, 16)
            sp.dma_start(wts[:, 10, :], A["L3_Wt"][0:P]).then_inc(s_in, 16)
            sp.dma_start(wts[:, 11, :], A["L3_Wg"][P:2 * P]).then_inc(s_in, 16)
            sp.dma_start(wts[:, 12, :], A["L3_Wt"][P:2 * P]).then_inc(s_in, 16)
            sp.dma_start(wts[0:DE, 13, :], A["L3_W1"][2 * P:2 * P + DE]).then_inc(s_in, 16)
            for n, b in enumerate(("L0_bias", "att_src", "att_dst", "L1_b", "L2_b1", "L2_b2", "L3_b1", "L3_b2",
                                   "L3_bg", "L3_bt", "gamma", "beta")):
                row = A[b].rearrange("h c -> (h c)") if len(A[b].shape) == 2 else A[b]
                sp.dma_start(rows[:, n, 0:row.shape[0]], row.partition_broadcast(P)).then_inc(s_in, 16)

            sp.wait_ge(s_tix, 3)
            with nc.allow_non_contiguous_dma(reason="small tables"):
                sp.dma_start(group_steps.rearrange("a (c p) -> p (a c)", p=P), tile_i[:, 0, :]).then_inc(s_steps, 16)
                sp.dma_start(base_steps.rearrange("a (c p) -> p (a c)", p=P), tile_i[:, 2, :]).then_inc(s_steps, 16)
                sp.wait_ge(s_atix, 2)
                sp.dma_start(asteps.rearrange("a (c p) -> p (a c)", p=P), ag16[:, :]).then_inc(s_steps, 16)
            sp.wait_ge(s_steps, 48)
            sp.dma_start(gtab[:, 16:16 + STEPS], group_steps).then_inc(s_gtab, 16)
            sp.dma_start(atab[:, 16:16 + ACH * P], asteps).then_inc(s_gtab, 16)
            sp.wait_ge(s_tc, 2 * CH)
            sp.dma_start(src_steps, srcs[:, :]).then_inc(s_steps, 16)
            sp.wait_ge(s_steps, 64)
            sp.wait_ge(s_gtab, 32)

            def write_table(n, tab, view):
                sp.wait_ge(s_tabr, n)
                sp.dma_start(tab.rearrange("(g p) f -> p g f", p=P), view).then_inc(s_tabw, 16)

            def first_indices(S, p):
                if p:
                    sp.wait_ge(S.done, p * STEPS)
                for r in range(UNROLL // QUARTER):
                    sp.dma_start(idx[:, r * QUARTER:(r + 1) * QUARTER], src_steps[:, r * QUARTER:(r + 1) * QUARTER]).then_inc(S.idx[r], 16)

            def refresh(S, p, i, r):
                sp.wait_ge(S.done, i * UNROLL + (r + 1) * QUARTER)
                at = (i - p * BODIES + 1) * UNROLL + r * QUARTER
                sp.dma_start(idx[:, r * QUARTER:(r + 1) * QUARTER], src_steps[:, bass.ds(at, QUARTER)]).then_inc(S.idx[r], 16)

            def refresh_all(S, p):
                first_indices(S, p)
                with sp.Fori(p * BODIES, (p + 1) * BODIES - 1) as i:
                    for r in range(UNROLL // QUARTER):
                        refresh(S, p, i, r)

            write_table(1, tab_proj, TA)
            small = [sp.alloc_register(f"small{k}") for k in range(17)]

            def columns(p, i, kb):
                b = adjacency_step(p, i, kb)
                if kb % 16 == 0:
                    sp.load(small, atab[0:1, bass.ds(16 + b, 17)])
                g = sp.snap(small[kb % 16], min_val=0, max_val=SG)
                after = sp.snap(small[kb % 16 + 1], min_val=0, max_val=SG)
                sp.wait_ge(s_acp, b + 1)
                sp.sem_inc(s_cols, 1)
                sp.dma_start(adj[:, bass.ds(g, 1), :].rearrange("p a c -> p (a c)"),
                             astage[:, bass.ds((g + 7) & 7, 1), :].rearrange("p a c -> p (a c)"),
                             cond=(after != g)).then_inc(s_adma[kb % 8], 16)

            def column_body(p, i, peeled, last):
                part = ABODY[p] // (UNROLL // QUARTER)
                at, behind = (part - 1, 1) if p == 0 else (part // 2, 2)
                for kb in range(ABODY[p]):
                    columns(p, i, kb)
                    if kb % part == at:
                        r = kb // part - behind
                        if r < 0 and not peeled:
                            refresh(main, p, i - 1, r + UNROLL // QUARTER)
                        elif r >= 0 and not last:
                            refresh(main, p, i, r)
            for p in range(2):
                first_indices(main, p)
                column_body(p, p * BODIES, True, False)
                with sp.Fori(p * BODIES + 1, (p + 1) * BODIES - 1) as i:
                    column_body(p, i, False, False)
                column_body(p, (p + 1) * BODIES - 1, False, True)
            for r in range(8):
                sp.wait_ge(s_adma[r], 16 * ASTEPS // 8)
            sp.dma_start(adj[:, SG, :], astage[:, (SG - 1) % 8, :]).then_inc(s_adma[0], 16)
            sp.wait_ge(s_adma[0], 16 * (ASTEPS // 8 + 1))
            for r in small:
                sp.free_register(r)

            def dense(d):
                def load(i, j):
                    n = d * G + 3 * i + j
                    if not (isinstance(i, int) and i == 0):
                        sp.wait_ge(s_dmm, n - 2)
                    at = (3 * i + j) * (P // SUB) + 1
                    sp.dma_start(acols[:, j, :].rearrange("p (g c) -> p g c", g=P // SUB), adj[:, bass.ds(at, P // SUB), :]).then_inc(s_aload[j], 16)
                sp.wait_ge(s_parts, d + 1)
                dense_groups(sp, load)

            for d, (tab, view) in enumerate(((tab_x, X[:, :, :]), (tab_y1, Y), (tab_y2, Y))):
                write_table(2 + d, tab, view)
                sp.wait_ge(s_tabw, 16 * (2 + d))
                if d == 0:
                    sp.wait_ge(s_flag, 1)
                choose(sp, d, lambda: dense(d), lambda: refresh_all(fall, d))

            write_table(5, tab_ps, TA[:, :, 0:P])
            first_indices(main, 2)
            base_regs = [sp.alloc_register(f"base{k}") for k in range(16)]

            def features(i, half, first):
                sp.load(base_regs, base_steps[0:1, bass.ds((i - 2 * BODIES) * UNROLL + 16 * half, 16)])
                for k in range(16 * half, 16 * half + 16):
                    base = sp.snap(base_regs[k % 16], min_val=0, max_val=LAST)
                    if not (first and k < 8):
                        sp.wait_ge(s_done, i * UNROLL + k - 7)
                    sp.dma_start(ef[:, k % 8, :], A["edge_attr_64"][bass.ds(base, P), :]).then_inc(s_ef[k % 8], 16)
                    if k % 8 == 7 and not (first and k == 7):
                        r = k // 8 - 1
                        if r < 0:
                            refresh(main, 2, i - 1, UNROLL // QUARTER - 1)
                        elif not (isinstance(i, int) and i == 3 * BODIES - 1):
                            refresh(main, 2, i, r)
            for half in range(2):
                features(2 * BODIES, half, True)
            with sp.Fori(2 * BODIES + 1, 3 * BODIES - 1) as i:
                for half in range(2):
                    features(i, half, False)
            for half in range(2):
                features(3 * BODIES - 1, half, False)
            sp.wait_ge(s_tabr, 6)
            sp.dma_start(out[0:FULL * P].rearrange("(g p) f -> p g f", p=P), X[:, 0:FULL, :]).then_inc(s_out, 16)
            sp.dma_start(out[FULL * P:N].unsqueeze(1), X[0:TAIL, FULL:G, :]).then_inc(s_out, 16)
            sp.wait_ge(s_out, 32)

        @block.gpsimd
        def _(pool):
            nc.gpsimd.memset(fill[:, 0, :], NO_NODE).then_inc(s_fill, 1)
            nc.gpsimd.memset(fill[:, 1, :], 0).then_inc(s_fill, 1)
            nc.gpsimd.memset(ident[:], 0.0).then_inc(s_pool, 1)
            exact = dict(allow_small_or_imprecise_dtypes=True)
            nc.gpsimd.iota(iota[:], [[1, P]], base=0, channel_multiplier=0, **exact).then_inc(s_iota, 1)
            nc.gpsimd.iota(iota16[:], [[1, AC]], base=0, channel_multiplier=0, **exact).then_inc(s_iota, 1)
            nc.gpsimd.iota(sidx[:, 0, 0:CH], [[P, CH]], base=0, channel_multiplier=1, **exact).then_inc(s_iota, 1)
            nc.gpsimd.iota(atile[:, 0, :], [[P, ACH]], base=0, channel_multiplier=1, **exact).then_inc(s_iota, 1)
            nc.gpsimd.iota(vcol[:, 0, :], [[SUB * P, VCH]], base=SUB, channel_multiplier=SUB, **exact).then_inc(s_iota, 1)
            nc.gpsimd.iota(srow, [[1, VCH * P]], base=1, channel_multiplier=0, **exact).then_inc(s_iota, 1)
            pool.wait_ge(s_pool, 1)
            nc.gpsimd.affine_select(out=ident[:], in_=ident[:], compare_op=ALU.not_equal, fill=1.0, base=0,
                                    pattern=[[-1, P]], channel_multiplier=1).then_inc(s_iota, 1)
            pool.wait_ge(s_pad, 64)
            pool.wait_ge(s_tix, 3)

            def tile_gather(cc, index):
                for f, pad in enumerate((dst_pad, src_pad)):
                    if cc >= 2:
                        pool.wait_ge(s_tf, 2 * (cc - 2) + f + 1)
                    nc.gpsimd.indirect_dma_start(
                        out=tile_rows[:, cc % 2, f, :], out_offset=None, in_=pad,
                        in_offset=bass.IndirectOffsetOnAxis(ap=index, axis=0)).then_inc(s_trow[2 * (cc % 2) + f], 16)
            for c in range(CH):
                tile_gather(c, tile_i[:, 1, c:c + 1])
            pool.wait_ge(s_atix, 2)
            for c in range(ACH):
                tile_gather(CH + c, atile_i[:, c:c + 1])

            def gathers(S, p, tab, w, written):
                pool.wait_ge(s_tabw, 16 * written)

                def body(i, first):
                    for k in range(UNROLL):
                        r = k // QUARTER
                        if k % QUARTER == 0:
                            pool.wait_ge(S.idx[r], i * 16 + 16)
                        if not (first and p == 0 and k < RING):
                            pool.wait_ge(S.done, i * UNROLL + k - RING + 1)
                        pool.sem_inc(s_slot, 1)
                        nc.gpsimd.indirect_dma_start(
                            out=got[:, k % RING, 0:w], out_offset=None, in_=tab,
                            in_offset=bass.IndirectOffsetOnAxis(ap=idx[:, k:k + 1], axis=0)).then_inc(S.got[k % RING], 16)

                body(p * BODIES, True)
                with pool.Fori(p * BODIES + 1, (p + 1) * BODIES) as i:
                    body(i, False)

            gathers(main, 0, tab_proj, XW, 1)
            gathers(main, 1, tab_proj, XW, 1)
            pool.wait_ge(s_flag, 1)
            for d, (tab, w) in enumerate(((tab_x, P), (tab_y1, HID), (tab_y2, HID))):
                pool.wait_ge(s_tabw, 16 * (2 + d))
                choose(pool, d, lambda: pool.sem_inc(s_slot, 1), lambda: gathers(fall, d, tab, w, 2 + d))
            gathers(main, 2, tab_ps, P, 5)

        def landed(eng, S, i, k):
            eng.wait_ge(S.got[k % RING], i * (16 * UNROLL // RING) + 16 * (k // RING + 1))

        def run_pass(eng, p, stages, loads=None, sub=(), subloads=None):
            first = p * BODIES
            beside = ABODY[p] if sub else 0
            behind = eng is nc.scalar or (eng is nc.tensor and p == 1)

            def adjacency(i, k):
                for kb in range(beside * k // UNROLL, beside * (k + 1) // UNROLL):
                    if kb % 16 == 0 and subloads:
                        subloads(i, kb // 16)
                    for fn in sub:
                        fn(i, kb)

            def body(i, peeled):
                for k in range(UNROLL):
                    if k % 16 == 0 and loads:
                        loads(i, k // 16)
                    if not behind:
                        adjacency(i, k)
                    for lag, fn in stages:
                        if k >= lag:
                            fn(i, k - lag)
                        elif not peeled:
                            fn(i - 1, k - lag + UNROLL)
                    if behind:
                        adjacency(i, k)

            body(first, True)
            with eng.Fori(first + 1, first + BODIES) as i:
                body(i, False)
            last = first + BODIES - 1
            most = max(lag for lag, _ in stages)
            if most and loads:
                loads(last + 1, 0)
            for k in range(most):
                for lag, fn in stages:
                    if k < lag:
                        fn(last, k - lag + UNROLL)

        def group_loader(eng, p, lag, name):
            regs = [eng.alloc_register(f"{name}{k}") for k in range(16)]

            def loads(i, n):
                eng.load(regs, gtab[0:1, bass.ds((i - p * BODIES) * UNROLL + 16 * n + 16 - lag, 16)])

            def group(k):
                return eng.snap(regs[(k + lag) % 16], min_val=0, max_val=G - 1)

            return loads, group, regs

        def small_loader(eng, p, name):
            regs = [eng.alloc_register(f"{name}{k}") for k in range(16)]

            def loads(i, n):
                eng.load(regs, atab[0:1, bass.ds(adjacency_step(p, i, 16 * n) + 16, 16)])

            def group(k):
                return eng.snap(regs[k % 16], min_val=0, max_val=SG)

            return loads, group, regs

        def release(eng, regs):
            for r in regs:
                eng.free_register(r)

        def sums_bank(k, w, paired):
            return PS[:, 6 + k // 2 % 2, (k % 2) * AW:(k % 2) * AW + w] if paired else PS[:, 6 + k % 2, 0:w]

        LINEARS = (
            (X, 0, 2 * P, ((TA, "copy"), (TB, "copy"))),
            (TC, 2, P, ((TA, "copy"),)),
            (X, 3, P, ((TA, "add"),)),
            (X, 4, HID, ((TA, "copy"),)),
            (TC, 5, P, ((TA, "copy"),)),
            (X, 6, 2 * P, ((TA, "copy"), (TB, "copy"))),
            (TC, 8, P, ((TA, "copy"),)),
            (X, 9, 2 * P, ((TB, "copy"), (TC, "copy"))),
            (TA, 11, 2 * P, ((TB, "add"), (TC, "add"))),
        )
        NL = G // LIN

        @block.tensor
        def _(pe):
            pe.sem_inc(s_linT, 1)
            pe.sem_inc(s_linY, 1)
            pe.wait_ge(s_vrow, 1)
            for c in range(0, T, 512):
                w = min(512, T - c)
                mm = nc.tensor.matmul(PS[:, c // 512, 0:w], ones[0:1, :], first[:, c:c + w], start=True, stop=True)
            mm.then_inc(s_bnd, 1)
            pe.wait_ge(s_vrow, 2)
            nc.tensor.matmul(PS[:, 4, :], ones[:], dg[:, 0:4, :].rearrange("p c v -> p (c v)"), start=True, stop=True)
            nc.tensor.matmul(PS[:, 5, 0:(VCH - 4) * P], ones[:], dg[:, 4:VCH, :].rearrange("p c v -> p (c v)"), start=True, stop=True).then_inc(s_bnd, 1)
            pe.wait_ge(s_iota, 7)

            def tile_transposes(first_n, last_n):
                for n in range(first_n, last_n):
                    pe.wait_ge(s_tf, n + 1)
                    if n >= 2:
                        pe.wait_ge(s_tc, n - 1)
                    nc.tensor.transpose(PS[:, 2 + n % 2, 0:P], tile_f[:, (n // 2) % 2, n % 2, :], ident[:]).then_inc(s_tt, 1)
            tile_transposes(0, 2 * (CH + ACH))
            pe.wait_ge(s_in, 16 * NW)

            def linear(L):
                _, w, cols, _ = LINEARS[L]
                with pe.Fori(L * NL, (L + 1) * NL) as i:
                    pe.wait_ge(s_linw, i + 1)
                    pe.wait_ge(s_linX, i + 1)
                    for j in range(LIN):
                        mm = nc.tensor.transpose(lin_in[:, j, :], stage[:, j, :], ident[:])
                    mm.then_inc(s_linT, 1)
                    pe.wait_ge(s_linX, i + 2)
                    pe.wait_ge(s_linO, 2 * i + 2)
                    rhs = wts[:, w:w + 2, :].rearrange("p a b -> p (a b)")[:, 0:cols]
                    for j in range(LIN):
                        mm = nc.tensor.matmul(lin_o[:, j, 0:cols], xT[:, j, :], rhs, start=True, stop=True)
                    mm.then_inc(s_linY, 1)

            def segment_sum(S, w, rhs, ready, paired=False):
                base = BODIES if S is main else 0

                def fn(i, k):
                    ready(i, k)
                    if paired:
                        if k % 2 == 0 and not opens(1, i, k, 4):
                            pe.wait_ge(S.done, i * UNROLL + k - 2)
                    elif not opens(base // BODIES, i, k, 2):
                        pe.wait_ge(S.done, i * UNROLL + k - 1)
                    nc.tensor.matmul(sums_bank(k, w, paired), D[:, k % DRING, :], rhs(k), start=True, stop=True).then_inc(S.seg, 1)
                return fn

            def transpose_batch(i, k):
                if k % BATCH == 0:
                    batch = (i - BODIES) * IN_BODY + k // BATCH
                    pe.wait_ge(s_d, i * UNROLL + k + BATCH)
                    if not opens(1, i, k, BATCH):
                        pe.wait_ge(s_dTc, batch)
                    for j in range(BATCH):
                        mm = nc.tensor.transpose(PS[:, 0, j * P:(j + 1) * P], D[:, k % DRING + j, :], ident[:])
                    mm.then_inc(s_dT, 1)

            linear(0)

            def masked_scores(i, k):
                g = i * UNROLL + k
                pe.wait_ge(s_d, g + 1)
                pe.wait_ge(s_d2, g + 1)
                pe.wait_ge(s_diag, g + 1)
                if not at_start(i, k, 4):
                    pe.wait_ge(s_red, g - 3)
                o = PS[:, (6 + k % 4) % 8, :]
                nc.tensor.matmul(o, D[:, k % DRING, :], diag[:, k % 4].rearrange("p h e -> p (h e)"), start=True, stop=False)
                nc.tensor.matmul(o, ND[:, k % 8, :], nident[:].rearrange("p h e -> p (h e)"), start=False, stop=True).then_inc(s_max, 1)

            pe.wait_ge(s_zero, 1)
            for b in range(4):
                mm = nc.tensor.matmul(PS[:, 2 + b, 0:AC], zero16[:], KEY[0][:, 0, :], start=True, stop=False, skip_group_check=True)
            mm.then_inc(s_zero, 1)
            pe.wait_ge(s_gtab, 32)

            def edge_counter(p):
                loads, small, regs = small_loader(pe, p, f"pea{p}_")

                def fn(i, kb):
                    b = adjacency_step(p, i, kb)
                    g = small(kb)
                    pe.wait_ge(s_ahot, 2 * b + 2)
                    if not at_start(i, kb, 2):
                        pe.wait_ge(s_acp, b - 1)
                    nc.tensor.matmul(PS[:, bass.ds(((g + 1) & 3) + 2, 1), 0:AC].rearrange("p a c -> p (a c)"), zero16[:], KEY[p][:, kb % 4, :],
                                     start=True, stop=False, skip_group_check=True)
                    nc.tensor.matmul(PS[:, bass.ds((g & 3) + 2, 1), 0:AC].rearrange("p a c -> p (a c)"), LO[p][:, kb % 4, :], KEY[p][:, kb % 4, :],
                                     start=False, stop=False, skip_group_check=True).then_inc(s_amm, 1)
                return loads, fn, regs

            subloads, count_edges, sregs = edge_counter(0)
            run_pass(pe, 0, ((3, masked_scores),), None, (count_edges,), subloads)
            release(pe, sregs)

            loads, group, regs = group_loader(pe, 1, 4, "peg")

            def expand_scores(i, k):
                if k % BATCH == 0:
                    batch = (i - BODIES) * IN_BODY + k // BATCH
                    pe.wait_ge(s_dTc, batch + 1)
                    if not opens(1, i, k, BATCH):
                        pe.wait_ge(s_z, 3 * batch)
                    for j in range(BATCH):
                        mm = nc.tensor.matmul(PS[:, 1, j * 2 * H:(j + 1) * 2 * H], DT[:, j, :],
                                              node_ad[:, bass.ds(group(k + j), 1), :].rearrange("p a c -> p (a c)"),
                                              start=True, stop=True)
                    mm.then_inc(s_ex, 1)

            def attention_ready(i, k):
                pe.wait_ge(s_msg, 2 * ((i - BODIES) * UNROLL + k) + 2)
            subloads, count_edges, sregs = edge_counter(1)
            run_pass(pe, 1, ((4, expand_scores), (1, transpose_batch),
                             (11, segment_sum(main, AW, lambda k: msg[:, k % 4, :], attention_ready, True))), loads,
                     (count_edges,), subloads)
            release(pe, regs)
            release(pe, sregs)

            def dense(d, w):
                table = part_table(w)
                pe.wait_ge(s_parts, d + 1)

                def multiply(i, j):
                    pe.wait_ge(s_aload[j], 16 * (d * ((G - 1) // 3 + (j == 0)) + 1) + 16 * i)
                    if not (isinstance(i, int) and i == 0):
                        pe.wait_ge(s_dev, d * G + 3 * i + j - 2)
                    cols = acols[:, j, :].rearrange("p (n h) -> p n h", h=HI)
                    for h in range(HI):
                        mm = nc.tensor.matmul(PS[:, j, 0:3 * w], cols[:, :, h], table[:, h, :, :].rearrange("p k c -> p (k c)"),
                                              start=(h == 0), stop=(h == HI - 1))
                    mm.then_inc(s_dmm, 1)
                dense_groups(pe, multiply)

            def gathered_ready(i, k):
                pe.wait_ge(fall.d, i * UNROLL + k + 1)
                landed(pe, fall, i, k)

            pe.wait_ge(s_flagf, 1)
            nc.tensor.transpose(PS[0:1, 0, 0:P], flag[:, 0:1], ident[:]).then_inc(s_flagf, 1)
            pe.wait_ge(s_flag, 1)
            linear_after = {0: (1, 2, 3), 1: (), 2: (4, 5)}
            for d, w in enumerate((P, HID, HID)):
                choose(pe, d, lambda: dense(d, w),
                       lambda: run_pass(pe, d, ((0, segment_sum(fall, w, lambda k: got[:, k % RING, 0:w], gathered_ready)),)))
                for L in linear_after[d]:
                    linear(L)

            loads, group, regs = group_loader(pe, 2, 1, "pem")

            def transpose_both(i, k):
                g = (i - 2 * BODIES) * UNROLL + k
                pe.wait_ge(s_ef[k % 8], (i - 2 * BODIES) * (16 * UNROLL // 8) + 16 * (k // 8 + 1))
                if not (isinstance(i, int) and i == 2 * BODIES and k < 2):
                    pe.wait_ge(s_fTc, g - 1)
                pe.wait_ge(s_d, i * UNROLL + k + 1)
                pe.wait_ge(s_dTc, BATCHES + g - 1)
                nc.tensor.transpose(PS[:, k % 2, 0:P], D[:, k % DRING, :], ident[:]).then_inc(s_dT, 1)
                nc.tensor.transpose(PS[0:DE, 2 + k % 2, 0:P], ef[:, k % 8, :], ident[:]).then_inc(s_fT, 1)

            def edge_linear(i, k):
                g = (i - 2 * BODIES) * UNROLL + k
                pe.wait_ge(s_dTc, BATCHES + g + 1)
                pe.wait_ge(s_fTc, g + 1)
                if not (isinstance(i, int) and i == 2 * BODIES and k < 2):
                    pe.wait_ge(s_pre, g - 1)
                o = PS[:, 4 + k % 2, 0:P]
                nc.tensor.matmul(o, DT[:, k % 2, :], TB[:, bass.ds(group(k), 1), :].rearrange("p a c -> p (a c)"), start=True, stop=False)
                nc.tensor.matmul(o, efT[:, k % 2, :], wts[0:DE, 13, :], start=False, stop=True).then_inc(s_ex, 1)

            def silu_ready(i, k):
                pe.wait_ge(s_silu, (i - 2 * BODIES) * UNROLL + k + 1)
            run_pass(pe, 2, ((0, transpose_both), (1, edge_linear),
                             (3, segment_sum(main, P, lambda k: silu_out[:, k % 2, :], silu_ready))), loads)
            for L in (6, 7, 8):
                linear(L)

        @block.scalar
        def _(act):
            act.sem_inc(s_linX, 1)
            requests = [0]

            def serve(out_, in_, func, scale=1.0):
                requests[0] += 1
                act.wait_ge(s_areq, requests[0])
                nc.scalar.activation(out_, in_, func, scale=scale).then_inc(s_arep, 1)

            def linear(L):
                tab = LINEARS[L][0]
                act.wait_ge(s_linr, L + 1)
                with act.Fori(L * NL, (L + 1) * NL) as i:
                    act.wait_ge(s_linT, i + 1)
                    nc.scalar.copy(stage, tab[:, bass.ds((i - L * NL) * LIN, LIN), 0:P]).then_inc(s_linw, 1)
                    act.wait_ge(s_linT, i + 2)
                    act.wait_ge(s_linY, i + 1)
                    nc.scalar.copy(xT, lin_in).then_inc(s_linX, 1)

            def norm():
                serve(stat[:, 2, :], stat[:, 1, :], ACT.Sqrt)

            def store_batch(i, k):
                if k % BATCH == 0:
                    batch = (i - BODIES) * IN_BODY + k // BATCH
                    act.wait_ge(s_dT, batch + 1)
                    if not opens(1, i, k, BATCH):
                        act.wait_ge(s_ex, batch)
                    nc.scalar.copy(DT, PS[:, 0, :].rearrange("p (j c) -> p j c", j=BATCH)).then_inc(s_dTc, 1)

            def store_onehotT(i, k):
                g = (i - 2 * BODIES) * UNROLL + k + BATCHES
                act.wait_ge(s_dT, g + 1)
                act.wait_ge(s_ex, g - 1)
                nc.scalar.copy(DT[:, k % 2, :], PS[:, k % 2, 0:P]).then_inc(s_dTc, 1)

            linear(0)

            def diagonals(i, k):
                g = i * UNROLL + k
                landed(act, main, i, k)
                if not at_start(i, k, 4):
                    act.wait_ge(s_max, g - 3)
                for h in range(H):
                    ins = nc.scalar.activation(diag[:, k % 4, h, :], ident[:], ACT.Copy, scale=got[:, k % RING, P + h:P + h + 1])
                ins.then_inc(s_diag, 1)

            def column_copier(p):
                loads, small, regs = small_loader(act, p, f"aca{p}_")

                def fn(i, kb):
                    b = adjacency_step(p, i, kb)
                    g = small(kb)
                    if not at_start(i, kb, 1):
                        act.wait_ge(s_acp, b)
                    act.wait_ge(s_amm, b + 1)
                    if not at_start(i, kb, 6):
                        act.wait_ge(s_adma[(kb - 6) % 8], adjacency_step(p, i, 0) * 2 + 16 * ((kb - 6) // 8 + 1))
                    nc.scalar.copy(astage[:, bass.ds((g + 7) & 7, 1), :].rearrange("p a c -> p (a c)"),
                                   PS[:, bass.ds(((g + 3) & 3) + 2, 1), 0:AC].rearrange("p a c -> p (a c)")).then_inc(s_acp, 1)
                return loads, fn, regs
            act.wait_ge(s_iota, 7)
            act.wait_ge(s_gtab, 32)
            act.wait_ge(s_zero, 2)
            subloads, copy_columns, sregs = column_copier(0)
            run_pass(act, 0, ((0, diagonals),), None, (copy_columns,), subloads)
            release(act, sregs)
            serve(p_self, p_self, ACT.Exp)

            def weights(i, k):
                if k % BATCH == 0:
                    batch = (i - BODIES) * IN_BODY + k // BATCH
                    act.wait_ge(s_z, 3 * batch + 3)
                    if not opens(1, i, k, 2 * BATCH):
                        act.wait_ge(s_msg, 2 * BATCH * (batch - 1))
                    slot = k // BATCH % 2
                    nc.scalar.activation(p4[:, slot], z4[:, slot, 2], ACT.Exp).then_inc(s_p, 1)

            subloads, copy_columns, sregs = column_copier(1)
            run_pass(act, 1, ((1, store_batch), (8, weights)), None, (copy_columns,), subloads)
            release(act, sregs)
            serve(TC, TC, ACT.Exp)
            norm()
            serve(dinv[:], dinv[:], ACT.Sqrt)
            linear(1)
            linear(2)
            serve(TA[:, :, 0:P], TA[:, :, 0:P], ACT.Tanh)
            norm()
            linear(3)
            linear(4)
            norm()
            linear(5)

            def store_featuresT(i, k):
                g = (i - 2 * BODIES) * UNROLL + k
                act.wait_ge(s_fT, g + 1)
                act.wait_ge(s_ex, BATCHES + g - 1)
                nc.scalar.copy(efT[:, k % 2, :], PS[0:DE, 2 + k % 2, 0:P]).then_inc(s_fTc, 1)

            def silu(i, k):
                g = (i - 2 * BODIES) * UNROLL + k
                act.wait_ge(s_pre, g + 1)
                act.wait_ge(s_seg, STEPS + g - 1)
                nc.scalar.activation(silu_out[:, k % 2, :], pre[:, k % 2, :], ACT.Silu).then_inc(s_silu, 1)
            run_pass(act, 2, ((0, store_onehotT), (0, store_featuresT), (2, silu)))
            for L in (6, 7, 8):
                linear(L)
            serve(TB, TB, ACT.Sigmoid)
            serve(TC, TC, ACT.Tanh)
            norm()
            norm()

        @block.vector
        def _(dve):
            v = nc.vector
            dve.sem_inc(s_linO, 2)
            chain = [0]
            asked = [0]
            linears = [0]

            def link(ins):
                chain[0] += 1
                ins.then_inc(s_chain, 1)
                dve.wait_ge(s_chain, chain[0])

            def ask():
                asked[0] += 1
                dve.sem_inc(s_areq, 1)
                dve.wait_ge(s_arep, asked[0])

            def linear():
                L = linears[0]
                linears[0] += 1
                outs = LINEARS[L][3]
                cols = min(LINEARS[L][2], P)
                dve.sem_inc(s_linr, 1)
                with dve.Fori(L * NL, (L + 1) * NL) as i:
                    dve.wait_ge(s_linY, i + 2)
                    for n, (tab, mode) in enumerate(outs):
                        o = tab[:, bass.ds((i - L * NL) * LIN, LIN), 0:cols]
                        y = lin_o[:, :, n * P:n * P + cols]
                        ins = v.tensor_tensor(o, o, y, ALU.add) if mode == "add" else v.tensor_copy(o, y)
                        ins.then_inc(s_linO, 2 // len(outs))
                dve.wait_ge(s_linO, 2 * (L + 1) * NL + 2)

            def layernorm(Z, scratch):
                link(v.tensor_reduce(stat[:, 0, :], Z, AX.X, ALU.add))
                link(v.tensor_scalar(stat[:, 0, :], stat[:, 0, :], 1.0 / P, None, ALU.mult))
                link(v.tensor_tensor(Z, Z, free(stat[:, 0, :], P), ALU.subtract))
                link(v.tensor_tensor(scratch, Z, Z, ALU.mult))
                link(v.tensor_reduce(stat[:, 1, :], scratch, AX.X, ALU.add))
                link(v.tensor_scalar(stat[:, 1, :], stat[:, 1, :], 1.0 / P, EPS, ALU.mult, ALU.add))
                ask()
                link(v.reciprocal(stat[:, 3, :], stat[:, 2, :]))
                link(v.tensor_tensor(Z, Z, free(stat[:, 3, :], P), ALU.mult))

            def row(n, w=P):
                return across(rows[:, n, 0:w], G)

            v.memset(X[96:P, FULL:G, :], 0.0).then_inc(s_xpad, 1)
            link(v.memset(ones[:], 1.0))
            link(v.memset(gtab[:], 0))
            link(v.memset(atab[:], 0))
            dve.wait_ge(s_iota, 7)
            for h in range(H):
                link(v.tensor_scalar(nident[:, h, :], ident[:], -BIG, None, ALU.mult))

            dve.wait_ge(s_dst, 32)
            link(v.tensor_copy(first, first_i))
            dve.sem_inc(s_vrow, 1)
            dve.wait_ge(s_bnd, 1)
            for c in range(VCH):
                link(v.tensor_scalar(junk[:, 0:T], PS[:, 0:4, :].rearrange("p b c -> p (b c)")[:, 0:T], vcol[:, 0, c:c + 1], None,
                                     ALU.is_lt, ALU.add, accum_out=vcol[:, 1, c:c + 1]))
                link(v.tensor_scalar(dg[:, c, :], ident[:], vcol[:, 1, c:c + 1], None, ALU.mult))
            dve.sem_inc(s_vrow, 1)
            dve.wait_ge(s_bnd, 2)
            link(v.tensor_scalar(trow, PS[:, 4:6, :].rearrange("p b c -> p (b c)")[:, 0:VCH * P], -1.0, 0.0, ALU.add, ALU.max))
            IN_GROUP = P // SUB
            link(v.tensor_tensor(pos[:, 0:NB].unsqueeze(2), trow[:, 0:NB * IN_GROUP].rearrange("p (g s) -> p g s", s=IN_GROUP)[:, :, IN_GROUP - 1:IN_GROUP],
                                 srow[:, 0:NB].unsqueeze(2), ALU.add))
            cmp3 = cmp[:, 0:CH * NB].rearrange("p (c b) -> p c b", c=CH)
            link(v.tensor_tensor(cmp3, free(sidx[:, 0, 0:CH], NB), across(pos[:, 0:NB], CH), ALU.is_ge))
            link(v.tensor_reduce(sidx[:, 1, 0:CH], cmp3, AX.X, ALU.add))
            link(v.tensor_tensor(sidx[:, 2, 0:CH], sidx[:, 0, 0:CH], sidx[:, 1, 0:CH], ALU.subtract))
            link(v.tensor_scalar(sidx[:, 3, 0:CH], sidx[:, 2, 0:CH], float(P), float(LAST), ALU.mult, ALU.min))
            link(v.tensor_scalar(sidx[:, 4, 0:CH], sidx[:, 1, 0:CH], float(P), None, ALU.mult))
            v.tensor_copy(tile_i[:, 0, :], sidx[:, 1, 0:CH]).then_inc(s_tix, 1)
            v.tensor_copy(tile_i[:, 1, :], sidx[:, 2, 0:CH]).then_inc(s_tix, 1)
            v.tensor_copy(tile_i[:, 2, :], sidx[:, 3, 0:CH]).then_inc(s_tix, 1)
            link(v.tensor_tensor(pos[:, 0:SG], trow[:, 0:SG], srow[:, 0:SG], ALU.add))
            for c in range(ACH):
                link(v.tensor_scalar(junk[:, 0:SG], pos[:, 0:SG], atile[:, 0, c:c + 1], None, ALU.is_le, ALU.add, accum_out=atile[:, 1, c:c + 1]))
            link(v.tensor_tensor(atile[:, 2, :], atile[:, 0, :], atile[:, 1, :], ALU.subtract))
            link(v.tensor_scalar(atile[:, 2, :], atile[:, 2, :], float(TP - 1), None, ALU.min))
            link(v.tensor_scalar(atile[:, 3, :], atile[:, 1, :], float(SUB), None, ALU.mult))
            v.tensor_copy(atile_i[:], atile[:, 2, :]).then_inc(s_atix, 1)
            v.tensor_copy(ag16[:], atile[:, 1, :]).then_inc(s_atix, 1)

            def tile_columns(first_c, chunks, convert, outs):
                lo, hi = 2 * first_c, 2 * (first_c + chunks)
                for n in range(lo, hi + 2):
                    if n < hi:
                        cc, f = n // 2, n % 2
                        dve.wait_ge(s_trow[2 * (cc % 2) + f], 16 * (cc // 2 + 1))
                        if n >= 4:
                            dve.wait_ge(s_tt, n - 3)
                        convert(cc - first_c, cc % 2, f).then_inc(s_tf, 1)
                    if n >= lo + 2:
                        m = n - 2
                        dve.wait_ge(s_tt, m + 1)
                        at = (m - lo) // 2 * P
                        v.tensor_copy(outs[m % 2][:, at:at + P], PS[:, 2 + m % 2, 0:P]).then_inc(s_tc, 1)
                dve.wait_ge(s_tc, hi)

            def local_or_source(c, b, f):
                if f == 0:
                    return v.tensor_scalar(tile_f[:, b, 0, :], tile_rows[:, b, 0, :], sidx[:, 4, c:c + 1], None, ALU.subtract)
                return v.tensor_copy(tile_f[:, b, 1, :], tile_rows[:, b, 1, :])
            tile_columns(0, CH, local_or_source, (dloc, srcs))

            def column_or_place(c, b, f):
                if f == 0:
                    return v.tensor_scalar(tile_f[:, b, 0, :], tile_rows[:, b, 0, :], atile[:, 3, c:c + 1], None, ALU.subtract)
                return v.tensor_copy(tile_f[:, b, 1, :], tile_rows[:, b, 1, :])
            tile_columns(CH, ACH, column_or_place, (akey, alo))
            src_i = setup[:, 0:ACH * P].bitcast(I32)
            blk_i = setup[:, ACH * P:2 * ACH * P].bitcast(I32)
            link(v.tensor_copy(src_i, alo))
            link(v.tensor_scalar(blk_i, src_i, 7, None, ALU.arith_shift_right))
            link(v.tensor_scalar(src_i, src_i, P - 1, None, ALU.bitwise_and))
            link(v.tensor_copy(alo, src_i))
            link(v.scalar_tensor_tensor(out=akey, in0=akey, scalar=float(HI), in1=blk_i, op0=ALU.mult, op1=ALU.add))

            def onehot(S, p):
                def fn(i, k):
                    if k % BATCH == 0:
                        g = i * UNROLL + k
                        if S is main and p == 0:
                            if not at_start(i, k, DRING):
                                dve.wait_ge(s_max, g + BATCH - DRING)
                        elif S is main:
                            if not opens(1, i, k, DRING):
                                dve.wait_ge(S.seg, g - STEPS + BATCH - DRING)
                        elif not at_start(i, k, DRING):
                            dve.wait_ge(S.seg, g + BATCH - DRING)
                        at, slot = (i - p * BODIES) * UNROLL + k, k % DRING
                        v.tensor_tensor(D[:, slot:slot + BATCH, :], across(iota[:], BATCH), free(dloc[:, bass.ds(at, BATCH)], P),
                                        ALU.is_equal).then_inc(S.d, BATCH)
                return fn

            dve.wait_ge(s_x, 32)
            dve.wait_ge(s_in, 16 * NW)
            linear()
            for n, o in ((1, node_as[:]), (2, node_ad[:, :, 0:H])):
                link(v.tensor_tensor(ACC[:, :, 0:P], TA[:, :, 0:P], row(n), ALU.mult))
                link(v.tensor_reduce(o, ACC[:, :, 0:P].rearrange("p g (h c) -> p g h c", h=H), AX.X, ALU.add))
            link(v.tensor_copy(TA[:, :, P:XW], node_as[:]))
            link(v.tensor_copy(node_max[:], node_as[:]))
            dve.sem_inc(s_tabr, 1)

            link(v.memset(KEY[0], 0.0))
            link(v.memset(zero16[:], 0.0))
            dve.sem_inc(s_zero, 1)
            dve.wait_ge(s_zero, 2)
            dve.wait_ge(s_gtab, 32)
            loads, group, regs = group_loader(dve, 0, 6, "dvg")

            def not_onehot(i, k):
                if k % BATCH == 0:
                    g = i * UNROLL + k
                    dve.wait_ge(s_d, g + BATCH)
                    if not at_start(i, k, 8):
                        dve.wait_ge(s_max, g + BATCH - 8)
                    v.tensor_scalar(ND[:, k % 8:k % 8 + BATCH, :], D[:, k % DRING:k % DRING + BATCH, :], -1.0, 1.0,
                                    ALU.mult, ALU.add).then_inc(s_d2, BATCH)

            def tile_max(i, k):
                g = i * UNROLL + k
                dve.wait_ge(s_max, g + 1)
                if not at_start(i, k, 4):
                    dve.wait_ge(s_done, g - 3)
                v.tensor_reduce(m4[:, k % 4, :], PS[:, (6 + k % 4) % 8, :].rearrange("p (h e) -> p h e", h=H), AX.X, ALU.max).then_inc(s_red, 1)

            def node_maximum(i, k):
                g = i * UNROLL + k
                dve.wait_ge(s_red, g + 1)
                if not at_start(i, k, 1):
                    dve.wait_ge(s_done, g)
                m = node_max[:, bass.ds(group(k), 1), :].rearrange("p a c -> p (a c)")
                v.tensor_tensor(m, m, m4[:, k % 4, :], ALU.max).then_inc(s_done, 1)

            def adjacency_onehots(p):
                def fn(i, kb):
                    b = adjacency_step(p, i, kb)
                    if kb % 2 == 0 and not at_start(i, kb, 4):
                        dve.wait_ge(s_amm, b - 2)
                    v.tensor_scalar(LO[p][:, kb % 4, :], iota16[:, 0:P], alo[:, bass.ds(b, 1)], None, ALU.is_equal).then_inc(s_ahot, 1)
                    v.tensor_scalar(KEY[p][:, kb % 4, :], iota16[:], akey[:, bass.ds(b, 1)], None, ALU.is_equal).then_inc(s_ahot, 1)
                return fn
            run_pass(dve, 0, ((6, node_maximum), (0, onehot(main, 0)), (1, not_onehot), (5, tile_max)), loads, (adjacency_onehots(0),))
            release(dve, regs)
            dve.wait_ge(s_done, STEPS)
            dve.wait_ge(s_amm, BODIES * ABODY[0])

            link(v.tensor_tensor(s0, node_ad[:, :, 0:H], node_max[:], ALU.add))
            link(v.scalar_tensor_tensor(out=node_ad[:, :, H:2 * H], in0=s0, scalar=SLOPE, in1=s0, op0=ALU.mult, op1=ALU.max))
            link(v.tensor_tensor(s0, node_as[:], node_ad[:, :, 0:H], ALU.add))
            link(v.scalar_tensor_tensor(out=p_self, in0=s0, scalar=SLOPE, in1=s0, op0=ALU.mult, op1=ALU.max))
            link(v.tensor_tensor(p_self, p_self, node_ad[:, :, H:2 * H], ALU.subtract))
            ask()
            link(v.memset(ACC[:], 0.0))
            link(v.tensor_copy(ACC[:, :, P:P + H], p_self))
            for h in range(H):
                link(v.tensor_tensor(ACC[:, :, h * C:(h + 1) * C], TA[:, :, h * C:(h + 1) * C], p_self[:, :, h:h + 1].to_broadcast([P, G, C]), ALU.mult))
            link(v.memset(msg[:], 1.0))

            def add_sums(S, w, group, paired=False):
                def fn(i, k):
                    g = i * UNROLL + k
                    if not paired:
                        dve.wait_ge(S.seg, g + 1 - (STEPS if S is main else 0))
                    elif k % 2 == 0:
                        dve.wait_ge(S.seg, g + 2 - STEPS)
                    if not at_start(i, k, 1):
                        dve.wait_ge(S.done, g)
                    a = ACC[:, bass.ds(group(k), 1), 0:w].rearrange("p a c -> p (a c)")
                    v.tensor_tensor(a, a, sums_bank(k, w, paired), ALU.add).then_inc(S.done, 1)
                return fn
            loads, group, regs = group_loader(dve, 1, 13, "dva")

            def logits(i, k):
                if k % BATCH == 0:
                    batch = (i - BODIES) * IN_BODY + k // BATCH
                    dve.wait_ge(s_ex, batch + 1)
                    for kk in range(k, k + BATCH):
                        landed(dve, main, i, kk)
                    if not opens(1, i, k, 2 * BATCH):
                        dve.wait_ge(s_p, batch - 1)
                    slot, r = k // BATCH % 2, k % RING
                    z, a = z4[:, slot], PS[:, 1, 0:BATCH * 2 * H].rearrange("p (j c) -> p j c", j=BATCH)
                    v.tensor_tensor(z[:, 0], got[:, r:r + BATCH, P:P + H], a[:, :, 0:H], ALU.add).then_inc(s_z, 1)
                    dve.wait_ge(s_z, 3 * batch + 1)
                    v.scalar_tensor_tensor(out=z[:, 1], in0=z[:, 0], scalar=SLOPE, in1=z[:, 0], op0=ALU.mult, op1=ALU.max).then_inc(s_z, 1)
                    dve.wait_ge(s_z, 3 * batch + 2)
                    v.tensor_tensor(z[:, 2], z[:, 1], a[:, :, H:2 * H], ALU.subtract).then_inc(s_z, 1)

            def messages(i, k):
                g = (i - BODIES) * UNROLL + k
                if k % BATCH == 0:
                    dve.wait_ge(s_p, (i - BODIES) * IN_BODY + k // BATCH + 1)
                if not opens(1, i, k, 4):
                    dve.wait_ge(s_seg, g - 3)
                o = msg[:, k % 4, :]
                p = p4[:, k // BATCH % 2, k % BATCH, :]
                v.scalar_tensor_tensor(out=o[:, 0:P].rearrange("p (h c) -> p h c", h=H), in0=free(p, C), scalar=1.0,
                                       in1=got[:, k % RING, 0:P].rearrange("p (h c) -> p h c", h=H), op0=ALU.min, op1=ALU.mult).then_inc(s_msg, 1)
                v.tensor_scalar(o[:, P:P + H], p, 1.0, None, ALU.min).then_inc(s_msg, 1)
            run_pass(dve, 1, ((0, onehot(main, 1)), (13, add_sums(main, AW, group, True)), (7, logits), (10, messages)), loads,
                     (adjacency_onehots(1),))
            release(dve, regs)
            dve.wait_ge(s_done, 2 * STEPS)
            dve.wait_ge(s_acp, ASTEPS)
            dve.wait_ge(s_amm, ASTEPS)

            sums = ACC[:, :, 0:P]
            link(v.tensor_scalar(ACC[:, :, P:P + H], ACC[:, :, P:P + H], 1e-16, None, ALU.add))
            link(v.reciprocal(ACC[:, :, P:P + H], ACC[:, :, P:P + H]))
            for h in range(H):
                link(v.tensor_tensor(TC[:, :, h * C:(h + 1) * C], ACC[:, :, h * C:(h + 1) * C], ACC[:, :, P + h:P + h + 1].to_broadcast([P, G, C]), ALU.mult))
            link(v.tensor_tensor(TC, TC, row(0), ALU.add))
            link(v.tensor_tensor(TB, TB, TC, ALU.add))
            link(v.tensor_scalar(TC, TB, 0.0, None, ALU.min))
            ask()
            link(v.tensor_scalar(TC, TC, -1.0, None, ALU.add))
            link(v.scalar_tensor_tensor(out=TC, in0=TB, scalar=0.0, in1=TC, op0=ALU.max, op1=ALU.add))
            link(v.tensor_tensor(X[:], X[:], TC, ALU.add))
            layernorm(X[:], TC)
            dve.sem_inc(s_tabr, 1)
            link(v.tensor_copy(count[:], ACC[:, :, P + H:AW].rearrange("p g a -> p (g a)")))
            link(v.tensor_scalar(rcount[:], count[:], 1.0, None, ALU.max))
            link(v.reciprocal(rcount[:], rcount[:]))
            link(v.tensor_scalar(dinv[:], count[:], 1.0, None, ALU.add))
            ask()
            link(v.reciprocal(dinv[:], dinv[:]))
            link(v.tensor_reduce(flag[:, 0:1], count[:], AX.X, ALU.max))
            dve.sem_inc(s_flagf, 1)
            dve.wait_ge(s_flagf, 2)
            link(v.tensor_reduce(flag[0:1, 1:2], PS[0:1, 0, 0:P], AX.X, ALU.max))
            link(v.tensor_copy(flag_i[:], flag[0:1, 1:2]))
            dve.sem_inc(s_flag, 1)

            def neighbour_sums(d, V, w):
                def general():
                    link(v.memset(ACC[:, :, 0:w], 0.0))
                    loads, group, regs = group_loader(dve, d, 2, f"dv{d}_")
                    run_pass(dve, d, ((0, onehot(fall, d)), (2, add_sums(fall, w, group))), loads)
                    release(dve, regs)
                    dve.wait_ge(fall.done, (d + 1) * STEPS)

                def dense():
                    t, rest = part_table(w), ACC[:, :, 0:w]
                    link(v.tensor_copy(t[:, :, 0, :], V))
                    link(v.tensor_tensor(rest, V, t[:, :, 0, :], ALU.subtract))
                    link(v.tensor_copy(t[:, :, 1, :], rest))
                    link(v.tensor_tensor(rest, rest, t[:, :, 1, :], ALU.subtract))
                    link(v.tensor_copy(t[:, :, 2, :], rest))
                    dve.sem_inc(s_parts, 1)

                    def store(i, j):
                        dve.wait_ge(s_dmm, d * G + 3 * i + j + 1)
                        v.tensor_reduce(ACC[:, bass.ds(3 * i + j, 1), 0:w].rearrange("p a c -> p (a c)"),
                                        PS[:, j, 0:3 * w].rearrange("p (k c) -> p c k", k=3), AX.X, ALU.add).then_inc(s_dev, 1)
                    dense_groups(dve, store)
                    dve.wait_ge(s_dev, (d + 1) * G)

                start = chain[0]
                most = dve.alloc_register(f"most_edges{d}")
                dve.load([most], flag_i[0:1, 0:1])
                with dve.If(dve.snap(most, min_val=0, max_val=1 << 24) > FINE):
                    general()
                    dve.sem_inc(s_chain, 5 - (chain[0] - start))
                chain[0] = start
                with dve.Else():
                    dense()
                dve.free_register(most)

            neighbour_sums(0, X[:], P)
            link(v.tensor_tensor(TC, sums, free(rcount[:], P), ALU.mult))
            linear()
            linear()
            ta = TA[:, :, 0:P]
            link(v.tensor_tensor(ta, ta, row(3), ALU.add))
            ask()
            link(v.tensor_tensor(X[:], X[:], ta, ALU.add))
            layernorm(X[:], TC)

            linear()
            hid = ACC[:, :, 0:HID]
            link(v.tensor_tensor(Y, TA[:, :, 0:HID], free(dinv[:], HID), ALU.mult))
            dve.sem_inc(s_tabr, 1)
            neighbour_sums(1, Y, HID)
            dve.wait_ge(s_tabw, 16 * 3)
            link(v.tensor_tensor(Y, hid, Y, ALU.add))
            link(v.tensor_tensor(Y, Y, free(dinv[:], HID), ALU.mult))
            link(v.tensor_tensor(Y, Y, row(4, HID), ALU.add))
            link(v.tensor_tensor(Y, Y, free(dinv[:], HID), ALU.mult))
            dve.sem_inc(s_tabr, 1)
            neighbour_sums(2, Y, HID)
            dve.wait_ge(s_tabw, 16 * 4)
            link(v.tensor_tensor(hid, hid, Y, ALU.add))
            link(v.memset(TC, 0.0))
            link(v.memset(wts[HID:2 * HID, 5, :], 0.0))
            link(v.memset(wts[2 * HID:P, 5, :], 0.0))
            link(v.tensor_tensor(TC[:, :, 0:HID], hid, free(dinv[:], HID), ALU.mult))
            linear()
            link(v.tensor_tensor(ta, ta, row(5), ALU.add))
            link(v.scalar_tensor_tensor(out=X[:], in0=ta, scalar=0.0, in1=X[:], op0=ALU.max, op1=ALU.add))
            layernorm(X[:], TC)

            linear()
            dve.sem_inc(s_tabr, 1)
            link(v.tensor_tensor(TB, TB, row(6), ALU.add))
            link(v.memset(ACC[:], 0.0))
            loads, group, regs = group_loader(dve, 2, 4, "dvm")

            def preactivation(i, k):
                g = (i - 2 * BODIES) * UNROLL + k
                dve.wait_ge(s_ex, BATCHES + g + 1)
                landed(dve, main, i, k)
                if not (isinstance(i, int) and i == 2 * BODIES and k < 2):
                    dve.wait_ge(s_silu, g - 1)
                v.tensor_tensor(pre[:, k % 2, :], got[:, k % RING, 0:P], PS[:, 4 + k % 2, 0:P], ALU.add).then_inc(s_pre, 1)
            run_pass(dve, 2, ((0, onehot(main, 2)), (2, preactivation), (4, add_sums(main, P, group))), loads)
            dve.wait_ge(s_done, 3 * STEPS)
            link(v.tensor_copy(TC, sums))
            dve.wait_ge(s_tabw, 16 * 5)
            linear()
            link(v.tensor_tensor(TC, free(count[:], P), row(7), ALU.mult))
            link(v.tensor_tensor(ta, ta, TC, ALU.add))
            link(v.tensor_tensor(ta, ta, free(rcount[:], P), ALU.mult))
            linear()
            linear()
            link(v.tensor_tensor(TB, TB, row(8), ALU.add))
            ask()
            link(v.tensor_tensor(TC, TC, row(9), ALU.add))
            ask()
            link(v.tensor_tensor(ta, X[:], TC, ALU.subtract))
            link(v.tensor_tensor(ta, ta, TB, ALU.mult))
            link(v.tensor_tensor(TC, TC, ta, ALU.add))
            layernorm(TC, TB)
            link(v.tensor_tensor(TC, TC, row(10), ALU.mult))
            link(v.tensor_tensor(TC, TC, row(11), ALU.add))
            link(v.tensor_tensor(X[:], X[:], TC, ALU.add))
            layernorm(X[:], TC)
            dve.sem_inc(s_tabr, 1)


_NAMES = {"x": "x", "src": "src", "dst": "dst", "edge_attr_64": "edge_attr_64",
          "att_src": "L0_gnn_att_src", "att_dst": "L0_gnn_att_dst", "L0_bias": "L0_gnn_bias",
          "L1_b": "L1_gnn_b_l", "L2_W1": "L2_gnn_W1", "L2_b1": "L2_gnn_b1", "L2_W2": "L2_gnn_W2", "L2_b2": "L2_gnn_b2",
          "L3_W1": "L3_gnn_W1", "L3_b1": "L3_gnn_b1", "L3_W2": "L3_gnn_W2", "L3_b2": "L3_gnn_b2",
          "L3_Wg": "L3_gnn_Wg", "L3_bg": "L3_gnn_bg", "L3_Wt": "L3_gnn_Wt", "L3_bt": "L3_gnn_bt",
          "gamma": "L3_gnn_gamma", "beta": "L3_gnn_beta"}
_TRANSPOSED = {"gatT": "L0_gnn_W_gat", "skipT": "L0_gnn_W_skip", "WlT": "L1_gnn_W_l", "WrT": "L1_gnn_W_r"}


def kernel(**inputs):
    import numpy as np
    import concourse.bacc as bacc
    from concourse.bass_utils import run_bass_kernel_spmd

    nc = bacc.Bacc("TRN2", target_bir_lowering=False, num_devices=1)
    arrays, A = {}, {}
    for short, name in _NAMES.items():
        arrays[f"in_{short}"] = np.ascontiguousarray(inputs[name])
    for short, name in _TRANSPOSED.items():
        arrays[f"in_{short}"] = np.ascontiguousarray(np.asarray(inputs[name]).T)
    for key, a in arrays.items():
        A[key[3:]] = nc.dram_tensor(key, a.shape, mybir.dt.from_np(a.dtype), kind="ExternalInput").ap()
    out = nc.dram_tensor("out_x", A["x"].shape, F32, kind="ExternalOutput").ap()
    gnn(nc, A, out)
    r = run_bass_kernel_spmd(nc, [arrays], core_ids=[0])
    return r.results[0]["out_x"]
```
